# Optimizing a Trainium2 kernel written in Bass

```python
import numpy as np
import jax
import jax.numpy as jnp

def _softmax(x, axis=-1):
    return jax.nn.softmax(x, axis=axis)

def _gelu(x):
    return jax.nn.gelu(x, approximate=True)

def _silu(x):
    return jax.nn.silu(x)

def _sigmoid(x):
    return jax.nn.sigmoid(x)

def _layernorm(x, axis=-1, eps=1e-05):
    m = jnp.mean(x, axis=axis, keepdims=True)
    v = jnp.var(x, axis=axis, keepdims=True)
    return (x - m) / jnp.sqrt(v + eps)

def _scatter_add(tgt, idx, src, axis=0):
    return tgt.at[idx].add(src)

def _segment_sum(src, seg, n):
    return jax.ops.segment_sum(src, seg, n)
kernel_name = 'mk_seq_preln_d2_jaxref_r8_9f4d85'

def setup_inputs(seed: int=0):
    np.random.seed(seed)
    _w = jnp.asarray

    def _L0_attn_setup():
        import jax, jax.numpy as jnp
        import numpy as np
        B, T, HID = (1, 256, 256)
        H = 16
        D = HID // H
        EPS = 1e-05

        def _layer_norm(x, eps=1e-05):
            mu = jnp.mean(x, axis=-1, keepdims=True)
            var = jnp.mean((x - mu) ** 2, axis=-1, keepdims=True)
            return (x - mu) * jax.lax.rsqrt(var + eps)

        def _feature_map(x, gamma, beta):
            return _layer_norm(x * gamma + beta)
        key = jax.random.key(seed)
        ks = jax.random.split(key, 8)
        s = HID ** (-0.5)
        return {'hidden_states': jax.random.normal(ks[0], (B, T, HID), jnp.float32), 'Wq': jax.random.normal(ks[1], (HID, HID), jnp.float32) * s, 'Wk': jax.random.normal(ks[2], (HID, HID), jnp.float32) * s, 'Wv': jax.random.normal(ks[3], (HID, HID), jnp.float32) * s, 'Wo': jax.random.normal(ks[4], (HID, HID), jnp.float32) * s, 'gamma': 1.0 + 0.1 * jax.random.normal(ks[5], (D,), jnp.float32), 'beta': 0.1 * jax.random.normal(ks[6], (D,), jnp.float32)}
    _L0_attn_in = _L0_attn_setup()

    def _L0_ffn_setup():
        import jax, jax.numpy as jnp
        import numpy as np
        HIDDEN = 256
        MOE_INTER = 128
        SHARED_INTER = 512
        N_EXPERTS = 16
        TOP_K = 2
        N_GROUP = 4
        TOPK_GROUP = 2
        NORM_TOPK_PROB = True
        ROUTED_SCALING = 1.0

        def relu2(x):
            r = jax.nn.relu(x)
            return r * r

        def _get_topk_indices(scores, e_bias):
            T, E = scores.shape
            s = scores + e_bias[None, :]
            gsz = E // N_GROUP
            group_scores = jax.lax.top_k(s.reshape(T, N_GROUP, gsz), 2)[0].sum(-1)
            group_idx = jax.lax.top_k(group_scores, TOPK_GROUP)[1]
            group_mask = jnp.zeros((T, N_GROUP), dtype=bool).at[jnp.arange(T)[:, None], group_idx].set(True)
            score_mask = jnp.repeat(group_mask, gsz, axis=1)
            masked = jnp.where(score_mask, s, 0.0)
            topk_indices = jax.lax.top_k(masked, TOP_K)[1]
            return jax.lax.stop_gradient(topk_indices)

        def _router(x_flat, router_weight, e_bias):
            logits = jnp.einsum('th,eh->te', x_flat.astype(jnp.float32), router_weight.astype(jnp.float32))
            scores = jax.nn.sigmoid(logits)
            topk_indices = _get_topk_indices(scores, e_bias)
            topk_weights = jnp.take_along_axis(scores, topk_indices, axis=1)
            if NORM_TOPK_PROB:
                topk_weights = topk_weights / (topk_weights.sum(-1, keepdims=True) + 1e-20)
            return (topk_indices, topk_weights * ROUTED_SCALING)
        key = jax.random.key(seed)
        ks = jax.random.split(key, 6)
        s = 0.02
        hidden_states = jax.random.normal(ks[0], (1, 256, HIDDEN), dtype=jnp.float32)
        router_weight = jax.random.normal(ks[1], (N_EXPERTS, HIDDEN), dtype=jnp.float32) * s
        e_bias = jnp.zeros((N_EXPERTS,), dtype=jnp.float32)
        w_up = jax.random.normal(ks[2], (N_EXPERTS, HIDDEN, MOE_INTER), dtype=jnp.float32) * s
        w_down = jax.random.normal(ks[3], (N_EXPERTS, MOE_INTER, HIDDEN), dtype=jnp.float32) * s
        shared_up = jax.random.normal(ks[4], (HIDDEN, SHARED_INTER), dtype=jnp.float32) * s
        shared_down = jax.random.normal(ks[5], (SHARED_INTER, HIDDEN), dtype=jnp.float32) * s
        return {'hidden_states': hidden_states, 'router_weight': router_weight, 'e_bias': e_bias, 'w_up': w_up, 'w_down': w_down, 'shared_up': shared_up, 'shared_down': shared_down}
    _L0_ffn_in = _L0_ffn_setup()

    def _L1_attn_setup():
        import jax, jax.numpy as jnp
        import numpy as np
        B, T, C = (4, 128, 256)
        H, DN, DR = (16, 128, 64)
        D = DN + DR
        Q_RANK, KV_RANK = (192, 64)
        ROPE_BASE = 10000.0

        def rope_cos_sin(seq_len, dim, dtype=jnp.float32):
            inv_freq = 1.0 / ROPE_BASE ** (jnp.arange(0, dim, 2, dtype=jnp.float32) / dim)
            t = jnp.arange(seq_len, dtype=jnp.float32)
            freqs = jnp.outer(t, inv_freq)
            return (jnp.cos(freqs).astype(dtype), jnp.sin(freqs).astype(dtype))

        def apply_rope(x, cos, sin):
            x1 = x[..., 0::2]
            x2 = x[..., 1::2]
            c = cos[None, :, None, :]
            s = sin[None, :, None, :]
            o1 = x1 * c - x2 * s
            o2 = x1 * s + x2 * c
            return jnp.stack([o1, o2], axis=-1).reshape(x.shape)
        key = jax.random.key(seed)
        ks = jax.random.split(key, 9)

        def g(k, shape, scale):
            return jax.random.normal(k, shape, dtype=jnp.float32) * scale
        return {'x': g(ks[0], (B, T, C), 1.0), 'wq_down': g(ks[1], (C, Q_RANK), C ** (-0.5)), 'wq_nope': g(ks[2], (Q_RANK, H * DN), Q_RANK ** (-0.5)), 'wq_rope': g(ks[3], (Q_RANK, H * DR), Q_RANK ** (-0.5)), 'wkv_down': g(ks[4], (C, KV_RANK), C ** (-0.5)), 'wv_up': g(ks[5], (KV_RANK, H * D), KV_RANK ** (-0.5)), 'wk_nope': g(ks[6], (KV_RANK, H * DN), KV_RANK ** (-0.5)), 'wk_rope': g(ks[7], (KV_RANK, H * DR), KV_RANK ** (-0.5)), 'wo': g(ks[8], (H * D, C), (H * D) ** (-0.5))}
    _L1_attn_in = _L1_attn_setup()

    def _L1_ffn_setup():
        import jax, jax.numpy as jnp
        import numpy as np
        HIDDEN = 256
        INTER = 704
        B, S = (2, 256)

        def _ternary(key, shape):
            return jax.random.randint(key, shape, -1, 2).astype(jnp.float32)
        key = jax.random.key(seed)
        ks = jax.random.split(key, 7)
        x = jax.random.normal(ks[0], (B, S, HIDDEN), dtype=jnp.float32)
        gate_w = _ternary(ks[1], (INTER, HIDDEN))
        up_w = _ternary(ks[2], (INTER, HIDDEN))
        down_w = _ternary(ks[3], (HIDDEN, INTER))
        gate_s = jax.random.uniform(ks[4], (INTER,), minval=0.01, maxval=0.1, dtype=jnp.float32)
        up_s = jax.random.uniform(ks[5], (INTER,), minval=0.01, maxval=0.1, dtype=jnp.float32)
        down_s = jax.random.uniform(ks[6], (HIDDEN,), minval=0.01, maxval=0.1, dtype=jnp.float32)
        return {'x': x, 'gate_w': gate_w, 'up_w': up_w, 'down_w': down_w, 'gate_s': gate_s, 'up_s': up_s, 'down_s': down_s}
    _L1_ffn_in = _L1_ffn_setup()
    _d = {'L0_attn_hidden_states': _L0_attn_in['hidden_states'], 'L0_attn_Wq': _L0_attn_in['Wq'], 'L0_attn_Wk': _L0_attn_in['Wk'], 'L0_attn_Wv': _L0_attn_in['Wv'], 'L0_attn_Wo': _L0_attn_in['Wo'], 'L0_attn_gamma': _L0_attn_in['gamma'], 'L0_attn_beta': _L0_attn_in['beta'], 'L0_ffn_router_weight': _L0_ffn_in['router_weight'], 'L0_ffn_e_bias': _L0_ffn_in['e_bias'], 'L0_ffn_w_up': _L0_ffn_in['w_up'], 'L0_ffn_w_down': _L0_ffn_in['w_down'], 'L0_ffn_shared_up': _L0_ffn_in['shared_up'], 'L0_ffn_shared_down': _L0_ffn_in['shared_down'], 'L1_attn_wq_down': _L1_attn_in['wq_down'], 'L1_attn_wq_nope': _L1_attn_in['wq_nope'], 'L1_attn_wq_rope': _L1_attn_in['wq_rope'], 'L1_attn_wkv_down': _L1_attn_in['wkv_down'], 'L1_attn_wv_up': _L1_attn_in['wv_up'], 'L1_attn_wk_nope': _L1_attn_in['wk_nope'], 'L1_attn_wk_rope': _L1_attn_in['wk_rope'], 'L1_attn_wo': _L1_attn_in['wo'], 'L1_ffn_gate_w': _L1_ffn_in['gate_w'], 'L1_ffn_up_w': _L1_ffn_in['up_w'], 'L1_ffn_down_w': _L1_ffn_in['down_w'], 'L1_ffn_gate_s': _L1_ffn_in['gate_s'], 'L1_ffn_up_s': _L1_ffn_in['up_s'], 'L1_ffn_down_s': _L1_ffn_in['down_s']}
    _x0 = _d['L0_attn_hidden_states']
    _d['L0_attn_hidden_states'] = jax.random.normal(jax.random.fold_in(jax.random.key(seed), 1), (1, 1024, 256), dtype=_x0.dtype)
    del _x0
    return _d

def reference(L0_attn_hidden_states, L0_attn_Wq, L0_attn_Wk, L0_attn_Wv, L0_attn_Wo, L0_attn_gamma, L0_attn_beta, L0_ffn_router_weight, L0_ffn_e_bias, L0_ffn_w_up, L0_ffn_w_down, L0_ffn_shared_up, L0_ffn_shared_down, L1_attn_wq_down, L1_attn_wq_nope, L1_attn_wq_rope, L1_attn_wkv_down, L1_attn_wv_up, L1_attn_wk_nope, L1_attn_wk_rope, L1_attn_wo, L1_ffn_gate_w, L1_ffn_up_w, L1_ffn_down_w, L1_ffn_gate_s, L1_ffn_up_s, L1_ffn_down_s):

    def _L0_attn_ref(hidden_states, Wq, Wk, Wv, Wo, gamma, beta):
        import jax, jax.numpy as jnp
        import numpy as np
        B, T, HID = (1, 256, 256)
        H = 16
        D = HID // H
        EPS = 1e-05

        def _layer_norm(x, eps=1e-05):
            mu = jnp.mean(x, axis=-1, keepdims=True)
            var = jnp.mean((x - mu) ** 2, axis=-1, keepdims=True)
            return (x - mu) * jax.lax.rsqrt(var + eps)

        def _feature_map(x, gamma, beta):
            return _layer_norm(x * gamma + beta)
        b, t, _ = hidden_states.shape
        q = (hidden_states @ Wq.T).reshape(b, t, H, D)
        k = (hidden_states @ Wk.T).reshape(b, t, H, D)
        v = (hidden_states @ Wv.T).reshape(b, t, H, D)
        q = _feature_map(q, gamma, beta)
        k = _feature_map(k, gamma, beta)
        q = q * D ** (-0.5)
        attn = jnp.einsum('bqhd,bkhd->bhqk', q, k) ** 2
        mask = jnp.tril(jnp.ones((t, t), dtype=bool))
        attn = jnp.where(mask, attn, 0.0)
        o = jnp.einsum('bhqk,bkhd->bqhd', attn, v)
        z = jnp.sum(attn, axis=-1)
        o = o / (jnp.swapaxes(z, 1, 2)[..., None] + EPS)
        o = o.reshape(b, t, H * D)
        return o @ Wo.T

    def _L0_ffn_ref(hidden_states, router_weight, e_bias, w_up, w_down, shared_up, shared_down):
        import jax, jax.numpy as jnp
        import numpy as np
        HIDDEN = 256
        MOE_INTER = 128
        SHARED_INTER = 512
        N_EXPERTS = 16
        TOP_K = 2
        N_GROUP = 4
        TOPK_GROUP = 2
        NORM_TOPK_PROB = True
        ROUTED_SCALING = 1.0

        def relu2(x):
            r = jax.nn.relu(x)
            return r * r

        def _get_topk_indices(scores, e_bias):
            T, E = scores.shape
            s = scores + e_bias[None, :]
            gsz = E // N_GROUP
            group_scores = jax.lax.top_k(s.reshape(T, N_GROUP, gsz), 2)[0].sum(-1)
            group_idx = jax.lax.top_k(group_scores, TOPK_GROUP)[1]
            group_mask = jnp.zeros((T, N_GROUP), dtype=bool).at[jnp.arange(T)[:, None], group_idx].set(True)
            score_mask = jnp.repeat(group_mask, gsz, axis=1)
            masked = jnp.where(score_mask, s, 0.0)
            topk_indices = jax.lax.top_k(masked, TOP_K)[1]
            return jax.lax.stop_gradient(topk_indices)

        def _router(x_flat, router_weight, e_bias):
            logits = jnp.einsum('th,eh->te', x_flat.astype(jnp.float32), router_weight.astype(jnp.float32))
            scores = jax.nn.sigmoid(logits)
            topk_indices = _get_topk_indices(scores, e_bias)
            topk_weights = jnp.take_along_axis(scores, topk_indices, axis=1)
            if NORM_TOPK_PROB:
                topk_weights = topk_weights / (topk_weights.sum(-1, keepdims=True) + 1e-20)
            return (topk_indices, topk_weights * ROUTED_SCALING)
        orig_shape = hidden_states.shape
        x = hidden_states.reshape(-1, HIDDEN)
        T = x.shape[0]
        topk_indices, topk_weights = _router(x, router_weight, e_bias)
        combine = jnp.zeros((T, N_EXPERTS), dtype=topk_weights.dtype).at[jnp.arange(T)[:, None], topk_indices].add(topk_weights)
        h1 = jnp.einsum('th,ehi->tei', x, w_up)
        a = relu2(h1) * combine[:, :, None]
        routed = jnp.einsum('tei,eih->th', a, w_down)
        shared = relu2(hidden_states @ shared_up) @ shared_down
        return routed.reshape(orig_shape) + shared

    def _L1_attn_ref(x, wq_down, wq_nope, wq_rope, wkv_down, wv_up, wk_nope, wk_rope, wo):
        import jax, jax.numpy as jnp
        import numpy as np
        B, T, C = (4, 128, 256)
        H, DN, DR = (16, 128, 64)
        D = DN + DR
        Q_RANK, KV_RANK = (192, 64)
        ROPE_BASE = 10000.0

        def rope_cos_sin(seq_len, dim, dtype=jnp.float32):
            inv_freq = 1.0 / ROPE_BASE ** (jnp.arange(0, dim, 2, dtype=jnp.float32) / dim)
            t = jnp.arange(seq_len, dtype=jnp.float32)
            freqs = jnp.outer(t, inv_freq)
            return (jnp.cos(freqs).astype(dtype), jnp.sin(freqs).astype(dtype))

        def apply_rope(x, cos, sin):
            x1 = x[..., 0::2]
            x2 = x[..., 1::2]
            c = cos[None, :, None, :]
            s = sin[None, :, None, :]
            o1 = x1 * c - x2 * s
            o2 = x1 * s + x2 * c
            return jnp.stack([o1, o2], axis=-1).reshape(x.shape)
        b, t, c = x.shape
        q_latent = x @ wq_down
        kv_latent = x @ wkv_down
        q_c = (q_latent @ wq_nope).reshape(b, t, H, DN)
        q_r = (q_latent @ wq_rope).reshape(b, t, H, DR)
        v = (kv_latent @ wv_up).reshape(b, t, H, D)
        k_c = (kv_latent @ wk_nope).reshape(b, t, H, DN)
        k_r = (kv_latent @ wk_rope).reshape(b, t, H, DR)
        cos, sin = rope_cos_sin(t, DR, x.dtype)
        q_r = apply_rope(q_r, cos, sin)
        k_r = apply_rope(k_r, cos, sin)
        q = jnp.concatenate([q_c, q_r], axis=-1)
        k = jnp.concatenate([k_c, k_r], axis=-1)
        scale = 1.0 / D ** 0.5
        scores = jnp.einsum('bthd,bshd->bhts', q, k) * scale
        causal = jnp.tril(jnp.ones((t, t), dtype=bool))
        scores = jnp.where(causal[None, None], scores, jnp.finfo(scores.dtype).min)
        probs = jax.nn.softmax(scores, axis=-1)
        out = jnp.einsum('bhts,bshd->bthd', probs, v).reshape(b, t, H * D)
        return out @ wo

    def _L1_ffn_ref(x, gate_w, up_w, down_w, gate_s, up_s, down_s):
        import jax, jax.numpy as jnp
        import numpy as np
        HIDDEN = 256
        INTER = 704
        B, S = (2, 256)

        def _ternary(key, shape):
            return jax.random.randint(key, shape, -1, 2).astype(jnp.float32)
        b, s, h = x.shape
        xf = x.reshape(b * s, h)
        g = jnp.einsum('th,ih->ti', xf, gate_w) * gate_s
        u = jnp.einsum('th,ih->ti', xf, up_w) * up_s
        hdn = jax.nn.silu(g) * u
        out = jnp.einsum('ti,hi->th', hdn, down_w) * down_s
        return out.reshape(b, s, -1)
    x = L0_attn_hidden_states
    x = x + _L0_attn_ref(_layernorm(x, axis=-1), L0_attn_Wq, L0_attn_Wk, L0_attn_Wv, L0_attn_Wo, L0_attn_gamma, L0_attn_beta)
    x = x + _L0_ffn_ref(_layernorm(x, axis=-1), L0_ffn_router_weight, L0_ffn_e_bias, L0_ffn_w_up, L0_ffn_w_down, L0_ffn_shared_up, L0_ffn_shared_down)
    x = x + _L1_attn_ref(_layernorm(x, axis=-1), L1_attn_wq_down, L1_attn_wq_nope, L1_attn_wq_rope, L1_attn_wkv_down, L1_attn_wv_up, L1_attn_wk_nope, L1_attn_wk_rope, L1_attn_wo)
    x = x + _L1_ffn_ref(_layernorm(x, axis=-1), L1_ffn_gate_w, L1_ffn_up_w, L1_ffn_down_w, L1_ffn_gate_s, L1_ffn_up_s, L1_ffn_down_s)
    return x

_drawn_inputs = setup_inputs


def setup_inputs(seed=0):
    import zlib

    import numpy as np

    out = dict(_drawn_inputs(seed))
    spreads = {'L0_ffn_e_bias': (0.0, 0.296)}
    factors = {'L0_ffn_router_weight': 3.927, 'L0_ffn_w_up': 2.804}
    for name, (base, spread) in spreads.items():
        noise = np.random.default_rng([zlib.crc32(name.encode()), seed]).standard_normal(out[name].shape)
        drawn = base * np.exp(spread * noise) if base else spread * noise
        out[name] = jnp.asarray(drawn.astype(out[name].dtype))
    for name, factor in factors.items():
        out[name] = (out[name] * factor).astype(out[name].dtype)
    return out
```

```python
import numpy as np
import concourse.bass as bass
from concourse import mybir
from contextlib import ExitStack

F32 = mybir.dt.float32
F32R = mybir.dt.float32r
BF16 = mybir.dt.bfloat16
ALU = mybir.AluOpType
ACT = mybir.ActivationFunctionType
AX = mybir.AxisListType

P = 128
T = 1024
NT = T // P
D = 256
NC = D // P
EPS = 1e-5

H0, D0 = 16, 16
SLOTS = 8

NSH = 4
NR = 16
NE = NSH + NR
MI = 128
NGRP = 4

H1 = 16
DN, DR = 128, 64
QR, KVR = 192, 64
DV = DN + DR
SCALE = 1.0 / float(DN + DR) ** 0.5
NEG = -1.0e30

FI = 704
NF = 6

KB = 1024


def build(nc, x, consts, wqkv, wo0, wr, up, down, wd, wqn, wkn, wqr, wkr, wv, wo1, rope, gu, gsus, dnw, ds, out,
          stop_after=99, dbg=None):
    ctx = ExitStack()
    with ctx:
        def place(start_kb, *tensors):
            with ExitStack() as s:
                if start_kb:
                    s.enter_context(nc.sbuf_tensor(f"pad_{tensors[0][0]}", [P, int(start_kb * KB) // 4], F32))
                return [s.enter_context(nc.sbuf_tensor(n, shape, dt)) for n, shape, dt in tensors]

        X, XN, XTH, XTL = place(0, ("X", [P, NT, D], F32), ("XN", [P, NT, D], F32),
                                ("XTH", [P, NC, T], F32R), ("XTL", [P, NC, T], F32R))
        (IDF, IDB, MASKB, CST, STAT, MV, VE, RSTD, HALF, ROPE, WRR, WRH, WRL, RT, CMB, GSUS, DS) = place(
            32, ("IDF", [P, P], F32), ("IDB", [P, P], BF16), ("MASKB", [P, P], BF16), ("CST", [P, 208], F32),
            ("STAT", [P, NT, 6], F32), ("MV", [P, NT, 2], F32), ("VE", [P, 64], F32), ("RSTD", [P, 64], F32),
            ("HALF", [P, 64], F32), ("ROPE", [P, 2, NT, DR], F32), ("WRR", [P, NC, NR], F32),
            ("WRH", [P, NC, NR], F32R), ("WRL", [P, NC, NR], F32R), ("RT", [P, 8, P], F32),
            ("CMB", [P, NT, NE], F32), ("GSUS", [P, 2, NF], F32), ("DS", [P, D], F32))
        Y, SQ, WC, WS, BETAC, BH, BL, ONE = place(
            48, ("Y", [P, NT, 2, H0, D0], F32), ("SQ", [P, 2, 2 * H0, D0], F32), ("WC", [P, NC, 2 * D], F32),
            ("WS", [P, NC * 2 * H0 + 1], F32), ("BETAC", [1, 2, D0], F32), ("BH", [1, 2 * D], F32R),
            ("BL", [1, 2 * D], F32R), ("ONE", [1, P], F32R))
        WQH, WQL, WQR = place(88, ("WQH", [P, NC, 3 * D], F32R), ("WQL", [P, NC, 3 * D], F32R),
                              ("WQR", [P, NC, 3 * D], F32))
        (WO0,) = place(106, ("WO0", [P, NC, D], F32))
        SLT, VA = place(108, ("SLT", [P, 2, NT, H0, SLOTS, D0], BF16), ("VA", [P, NT, H0, D0 + 1], F32))
        VS, SD = place(181, ("VS", [P, NT, 2, H0], F32), ("SD", [P, NT, 2, H0], F32))
        AT, VR = place(181, ("AT", [P, 2, 2304], F32), ("VR", [P, 2, NT, D0 + 1], F32))
        (OT4,) = place(16, ("OT4", [P, H0 // 4, T], F32))
        STK = place(88, ("STK", [P, 2, 2, T], BF16))[0]
        (OT0,) = place(108, ("OT0", [P, NC, T], F32))
        UP, DOWN = place(48, ("UP", [P, NE, NC, MI], F32), ("DOWN", [P, NE, D], F32))
        UPH, UPL, RELU, AH, AL, DNH, DNL = place(
            88, ("UPH", [P, 2, NC, MI], F32R), ("UPL", [P, 2, NC, MI], F32R), ("RELU", [P, 2, T // 2], F32),
            ("AH", [P, 2, T], F32R), ("AL", [P, 2, T], F32R), ("DNH", [P, 2, D], F32R), ("DNL", [P, 2, D], F32R))

        W2, WRN, WKR, WDR, WDH, WDL = place(
            109, ("W2", [P, H1 // 2, D], F32), ("WRN", [P, 2, 2 * H1 * DR], F32), ("WKR", [P, H1 * DR], F32),
            ("WDR", [P, NC, D], F32), ("WDH", [P, NC, D], F32R), ("WDL", [P, NC, D], F32R))
        WQN, WKN, WV, WO1 = place(143, ("WQN", [P, H1, QR], F32), ("WKN", [P, H1, KVR], F32),
                                  ("WV", [96, H1, 2, P], F32), ("WO1", [96, H1, 2, D], F32))
        (QT,) = place(45, ("QT", [P, H1, T], F32))
        (KT,) = place(175, ("KT", [P, H1 // 2, T], F32))
        LT, QTOK, KTOK = place(143, ("LT", [P, 2, T], F32), ("QTOK", [P, 2, H1 * P], F32),
                               ("KTOK", [P, 2, H1 * DR], F32))
        TQ, TK = place(8, ("TQ", [P, 2, H1 * DR], F32), ("TK", [P, 2, H1 * DR], F32))
        PB, PT, KV, NM, LS, RL = place(8, ("PB", [P, 2, T], F32), ("PT", [P, 4, 512], F32),
                                       ("KV", [P, NT, KVR], F32), ("NM", [P, H1 * NT], F32),
                                       ("LS", [P, H1 * NT], F32), ("RL", [P, H1 * NT], F32))
        QH, QL, KH, KL = place(143, ("QH", [P, 2, T], F32R), ("QL", [P, 2, T], F32R),
                               ("KH", [P, 2, T], F32R), ("KL", [P, 2, T], F32R))
        (OT1,) = place(143, ("OT1", [P, 2, H1 // 2, P], F32))
        GU, DNW, GUH, GUL = place(117, ("GU", [P, NF, 2 * NC, P], F32), ("DNW", [P, NF, D], F32),
                                  ("GUH", [P, 2, 2 * NC, P], F32R), ("GUL", [P, 2, 2 * NC, P], F32R))
        HT, EX = place(151, ("HT", [P, NF, T], F32), ("EX", [P, 2, T], F32))

        PS = ctx.enter_context(nc.psum_tensor("PS", [P, 8, 512], F32))

        made = {}

        def sem(name):
            if name not in made:
                made[name] = ctx.enter_context(nc.semaphore(name))
            return made[name]

        loads = {}

        def mm3(o, left, right, start=True, stop=True):
            (lh, ll), (rh, rl) = left, right
            nc.tensor.matmul(o, lh, rh, start=start, stop=False)
            nc.tensor.matmul(o, lh, rl, start=False, stop=False)
            return nc.tensor.matmul(o, ll, rh, start=False, stop=stop)

        def f(ap):
            return ap.bitcast(F32)

        GAMMA, BETA = CST[:, 0:16], CST[:, 16:32]
        EBIAS, KEY, LTRI = CST[:, 32:48], CST[:, 48:64], CST[:, 64:80]

        block = ctx.enter_context(nc.Block())

        def ln_dve_stats(dve, k, x_ready):
            for tt in range(NT):
                x_ready(tt)
                nc.vector.bn_stats(STAT[:, tt, :], X[:, tt, :]).then_inc(sem(f"ln{k}_stat"), 1)
                if tt % 2:
                    for t2 in (tt - 1, tt):
                        dve.wait_ge(sem(f"ln{k}_stat"), t2 + 1)
                        nc.vector.bn_aggr(MV[:, t2, :], STAT[:, t2, :]).then_inc(sem(f"ln{k}_var"), 1)

        def ln_pool(pool, k):
            for j in range(NT // 2):
                pool.wait_ge(sem(f"ln{k}_var"), 2 * j + 2)
                g = slice(2 * j, 2 * j + 2)
                nc.gpsimd.tensor_scalar(VE[:, g], MV[:, g, 1], 1.0, EPS, ALU.mult, ALU.add).then_inc(sem(f"ln{k}_ve"), 1)
                pool.wait_ge(sem(f"ln{k}_ve"), j + 1)
                if k == 0 and j == 0:
                    pool.wait_ge(sem("half"), 1)
                nc.gpsimd.tensor_tensor(RSTD[:, g], VE[:, g], HALF[:, g], ALU.pow).then_inc(sem(f"ln{k}_rstd"), 1)

        def ln_dve_norm(dve, k):
            for tt in range(NT):
                if tt % 2 == 0:
                    dve.wait_ge(sem(f"ln{k}_rstd"), tt // 2 + 1)
                nc.vector.tensor_scalar(XN[:, tt, :], X[:, tt, :], MV[:, tt, 0:1], RSTD[:, tt:tt + 1],
                                        ALU.subtract, ALU.mult).then_inc(sem(f"ln{k}_xn"), 1)

        def ln_pe(pe, k, banks, j):
            pe.wait_ge(sem(f"ln{k}_xn"), 2 * j + 2)
            if j >= 2:
                pe.wait_ge(sem(f"ln{k}_lo"), j - 1)
            bank = PS[:, banks[j % 2], :].rearrange("p (c t) -> p c t", c=NC)
            for i in range(2):
                for c in range(NC):
                    last = nc.tensor.transpose(bank[:, c, i * P:(i + 1) * P],
                                               XN[:, 2 * j + i, c * P:(c + 1) * P], IDF[:, :])
            last.then_inc(sem(f"ln{k}_tr"), 1)

        def ln_act(act, k, banks):
            for j in range(NT // 2):
                act.wait_ge(sem(f"ln{k}_tr"), j + 1)
                bank = PS[:, banks[j % 2], :].rearrange("p (c t) -> p c t", c=NC)
                nc.scalar.copy(XTH[:, :, 256 * j:256 * j + 256], bank).then_inc(sem(f"ln{k}_hi"), 1)

        def ln_dve_lo(dve, k, banks):
            for j in range(NT // 2):
                dve.wait_ge(sem(f"ln{k}_hi"), j + 1)
                bank = PS[:, banks[j % 2], :].rearrange("p (c t) -> p c t", c=NC)
                cols = slice(256 * j, 256 * j + 256)
                nc.vector.tensor_tensor(XTL[:, :, cols], bank, f(XTH[:, :, cols]), ALU.subtract)\
                    .then_inc(sem(f"ln{k}_lo"), 1)

        def xt(c, cols):
            return XTH[:, c, cols], XTL[:, c, cols]

        def pool_wait(pool, name, value):
            pool.wait_ge(sem(name), value)
            pool.sem_inc(sem("pool_waited"), 1)

        def tile(tt):
            return slice(tt * P, (tt + 1) * P)

        def qk_bank(tt):
            return PS[:, 2 + tt % 6, :]

        BASE = [0, 1, 3, 6]
        NB = 4
        OPS, SPB = 4, (6, 7)
        LN_BANKS = (0, 1)

        def l0_scores(pe, h, p, g):
            for j in range(g + 1):
                n = BASE[g] + j
                if not (isinstance(h, int) and 10 * h + n < NB):
                    pe.wait_ge(sem("l0_sq"), 10 * h + n - NB + 1)
                for i in range(2):
                    last = nc.tensor.matmul(PS[:, (10 * p + n) % NB, 256 * i:256 * i + 256],
                                            STK[:, p, 1, tile(2 * j + i)], STK[:, p, 0, 256 * g:256 * g + 256],
                                            start=True, stop=True)
                last.then_inc(sem("l0_score"), 1)

        def l0_stack(pe, h, qk):
            if not (isinstance(h, int) and 2 * h + qk == 0):
                pe.wait_ge(sem("l0_stke"), 2 * h + qk)
            for tt in range(NT):
                last = nc.tensor.matmul(PS[:, SPB[tt // 4], (tt % 4) * P:(tt % 4 + 1) * P],
                                        SLT[:, qk, tt, bass.ds(h, 1), :, :].rearrange("p o s d -> p (o s d)"),
                                        IDB[:, :], start=True, stop=True)
            last.then_inc(sem("l0_stk"), 1)

        def l0_av(pe, h, p, g):
            pe.wait_ge(sem("l0_sq"), 10 * h + BASE[g] + g + 1)
            pe.wait_ge(sem("l0_mask"), 4 * h + g + 1)
            pe.wait_ge(sem("l0_vr"), h + 1)
            if not (isinstance(h, int) and h == 0 and g < 2):
                pe.wait_ge(sem("l0_oev"), 4 * h + g - 1)
            at = AT[:, g % 2, 0:2048].rearrange("p (s t) -> p s t", s=8)
            o = PS[0:D0 + 1, OPS + g % 2, 0:256]
            for sb in range(2 * g + 2):
                skip = P if sb == 2 * g + 1 else 0
                last = nc.tensor.matmul(o[:, skip:], VR[:, p, sb, :], at[:, sb, skip:256],
                                        start=(sb == 0), stop=(sb == 2 * g + 1))
            last.then_inc(sem("l0_av"), 1)

        def pe_head(pe, h, p, first=False, final=False):
            pe.wait_ge(sem("l0_stke"), 2 * h + 2)
            l0_scores(pe, h, p, 0)
            if not final:
                l0_stack(pe, h + 1, 0)
            if not first:
                l0_av(pe, h - 1, 1 - p, 3)
            l0_scores(pe, h, p, 1)
            l0_av(pe, h, p, 0)
            l0_scores(pe, h, p, 2)
            if not final:
                l0_stack(pe, h + 1, 1)
            l0_av(pe, h, p, 1)
            l0_scores(pe, h, p, 3)
            l0_av(pe, h, p, 2)

        def act_head(act, h, p, first=False):
            for g in range(4):
                if not (first and g < 2):
                    act.wait_ge(sem("l0_av"), 4 * h + g - 1)
                for j in range(g + 1):
                    n = BASE[g] + j
                    act.wait_ge(sem("l0_score"), 10 * h + n + 1)
                    nc.scalar.activation(AT[:, g % 2, 512 * j:512 * j + 512], PS[:, (10 * p + n) % NB, :], ACT.Square)\
                        .then_inc(sem("l0_sq"), 1)

        def pool_head(pool, h):
            for g in range(4):
                pool_wait(pool, "l0_sq", 10 * h + BASE[g] + g + 1)
                v = AT[:, g % 2, 512 * g:512 * g + 768].rearrange("p (b t) -> p b t", b=2)[:, :, 0:P]
                nc.gpsimd.affine_select(out=v, in_=v, pattern=[[0, 2], [1, P]], compare_op=ALU.is_ge, fill=0.0,
                                        base=0, channel_multiplier=-1).then_inc(sem("l0_mask"), 1)

        def dve_stack_out(dve, h, p, qk):
            dve.wait_ge(sem("l0_stk"), 2 * h + qk + 1)
            if not (isinstance(h, int) and h < 2):
                dve.wait_ge(sem("l0_score"), 10 * (h - 1))
            nc.vector.tensor_copy(STK[:, p, qk, :].rearrange("p (b t) -> p b t", b=2), PS[:, SPB[0]:SPB[1] + 1, :])\
                .then_inc(sem("l0_stke"), 1)

        def dve_values(dve, h, p):
            if not (isinstance(h, int) and h < 2):
                dve.wait_ge(sem("l0_av"), 4 * (h - 1))
            nc.vector.tensor_copy(VR[:, p], VA[:, :, bass.ds(h, 1), :].rearrange("p t o e -> p t (o e)"))\
                .then_inc(sem("l0_vr"), 1)

        def dve_out(dve, h, r, g):
            dve.wait_ge(sem("l0_av"), 4 * h + g + 1)
            dst = OT4[32 * r:32 * r + D0 + 1, :, :].rearrange("p q t -> p (q t)")
            nc.vector.tensor_copy(dst[:, bass.ds((h - r) * (T // 4) + 256 * g, 256)], PS[0:D0 + 1, OPS + g % 2, 0:256])\
                .then_inc(sem("l0_oev"), 1)

        def dve_head(dve, h, r, first=False, final=False):
            if not final:
                dve_stack_out(dve, h + 1, 1 - r % 2, 0)
            if not first:
                dve_out(dve, h - 1, (r - 1) % 4, 3)
            if not final:
                dve_values(dve, h + 1, 1 - r % 2)
            dve_out(dve, h, r, 0)
            if not final:
                dve_stack_out(dve, h + 1, 1 - r % 2, 1)
            dve_out(dve, h, r, 1)
            dve_out(dve, h, r, 2)

        def loop_heads4(eng, one):
            one(0, 0, first=True)
            with eng.Fori(0, (H0 - 4) // 4) as i:
                for r in (1, 2, 3):
                    one(4 * i + r, r)
                one(4 * i + 4, 0)
            one(H0 - 3, 1)
            one(H0 - 2, 2)
            one(H0 - 1, 3, final=True)

        def loop_heads(eng, one):
            one(0, 0, first=True)
            with eng.Fori(0, H0 // 2 - 1) as i:
                one(2 * i + 1, 1)
                one(2 * i + 2, 0)
            one(H0 - 1, 1, final=True)

        def moe_split(pool, e, p):
            if not (isinstance(e, int) and e < 2):
                pool_wait(pool, "m_up", 2 * e - 2)
            src = UP[:, bass.ds(e, 1), :, :].rearrange("p o c i -> p (o c) i")
            nc.gpsimd.tensor_copy(UPH[:, p], src).then_inc(sem("m_hi"), 1)
            pool_wait(pool, "m_hi", 2 * e + 1)
            nc.gpsimd.tensor_tensor(UPL[:, p], src, f(UPH[:, p]), ALU.subtract).then_inc(sem("m_split"), 1)
            if not (isinstance(e, int) and e < 2):
                pool_wait(pool, "m_dn", 4 * e - 4)
            src = DOWN[:, bass.ds(e, 1), :].rearrange("p o d -> p (o d)")
            nc.gpsimd.tensor_copy(DNH[:, p], src).then_inc(sem("m_hi"), 1)
            pool_wait(pool, "m_hi", 2 * e + 2)
            nc.gpsimd.tensor_tensor(DNL[:, p], src, f(DNH[:, p]), ALU.subtract).then_inc(sem("m_dsplit"), 1)

        def moe_up(pe, e, p):
            pe.wait_ge(sem("m_split"), e + 1)
            for n in range(2):
                if not (isinstance(e, int) and e < 2):
                    pe.wait_ge(sem("m_relu"), 2 * (e - 2) + n + 1)
                for c in range(NC):
                    last = mm3(PS[:, 2 * p + n, :], (UPH[:, p, c, :], UPL[:, p, c, :]),
                               xt(c, slice(512 * n, 512 * n + 512)), start=(c == 0), stop=(c == NC - 1))
                last.then_inc(sem("m_up"), 1)

        def moe_down(pe, e, p):
            for b in range(4):
                if b == 0:
                    pe.wait_ge(sem("m_dsplit"), e + 1)
                if b % 2 == 0:
                    pe.wait_ge(sem("m_al"), 2 * e + b // 2 + 1)
                if not (isinstance(e, int) and e < 1):
                    pe.wait_ge(sem("m_acc"), 8 * (e - 1) + 2 * b + 2)
                for i in range(2):
                    last = mm3(PS[:, 4 + b, 256 * i:256 * i + 256], (AH[:, p, tile(2 * b + i)], AL[:, p, tile(2 * b + i)]),
                               (DNH[:, p, :], DNL[:, p, :]))
                last.then_inc(sem("m_dn"), 1)

        def moe_act(act, e, p):
            for n in range(2):
                act.wait_ge(sem("m_up"), 2 * e + n + 1)
                if not (isinstance(e, int) and e < 1):
                    act.wait_ge(sem("m_al"), 2 * e - 1 + n)
                nc.scalar.activation(RELU[:, n, :], PS[:, 2 * p + n, :], ACT.Relu).then_inc(sem("m_relu"), 1)
                act.wait_ge(sem("m_relu"), 2 * e + n + 1)
                if not (isinstance(e, int) and e < 2):
                    act.wait_ge(sem("m_dn"), 4 * e - 4)
                nc.scalar.activation(AH[:, p, 512 * n:512 * n + 512], RELU[:, n, :], ACT.Square).then_inc(sem("m_ah"), 1)
                act.wait_ge(sem("m_ah"), 2 * e + n + 1)
                nc.scalar.activation(RELU[:, n, :], RELU[:, n, :], ACT.Square).then_inc(sem("m_sq"), 1)

        def moe_lo(dve, e, p):
            for n in range(2):
                dve.wait_ge(sem("m_sq"), 2 * e + n + 1)
                nc.vector.tensor_tensor(AL[:, p, 512 * n:512 * n + 512], RELU[:, n, :],
                                        f(AH[:, p, 512 * n:512 * n + 512]), ALU.subtract).then_inc(sem("m_al"), 1)

        def moe_acc(dve, e):
            for b in range(4):
                dve.wait_ge(sem("m_dn"), 4 * e + b + 1)
                for i in range(2):
                    tt = 2 * b + i
                    if not (isinstance(e, int) and e < 1):
                        dve.wait_ge(sem("m_acc"), 8 * (e - 1) + tt + 1)
                    nc.vector.scalar_tensor_tensor(
                        out=X[:, tt, :], in0=PS[:, 4 + b, 256 * i:256 * i + 256],
                        scalar=CMB[:, tt, bass.ds(e, 1)], in1=X[:, tt, :], op0=ALU.mult, op1=ALU.add)\
                        .then_inc(sem("m_acc"), 1)

        def grab(bank, n, rows=slice(0, P)):
            return PS[rows, bank, 0:n]

        def l1_products(pe):
            pe.wait_ge(sem("ld_prod"), 64)
            for half in range(2):
                for m, (r0, r1) in enumerate(((0, P), (P, QR))):
                    bank = 2 * m + half
                    for i in range(8):
                        last = nc.tensor.matmul(PS[0:r1 - r0, bank, 64 * i:64 * i + 64], WQN[:, 8 * half + i, r0:r1],
                                                WKN[:, 8 * half + i, :], start=True, stop=True)
                last.then_inc(sem("p_wn"), 1)
            pe.wait_ge(sem("m_acc"), 8 * NE)
            for q in range(H1 // 2):
                for i in range(4):
                    last = nc.tensor.matmul(PS[:, 4 + q // 2, 256 * (q % 2):256 * (q % 2) + 256],
                                            WV[:, 2 * q + i // 2, i % 2, :], WO1[:, 2 * q + i // 2, i % 2, :],
                                            start=(i == 0), stop=(i == 3))
                if q % 2:
                    last.then_inc(sem("p_w2"), 1)

        def l1_products_out(act):
            for half in range(2):
                act.wait_ge(sem("p_wn"), half + 1)
                cols = slice(H1 * DR + 512 * half, H1 * DR + 512 * half + 512)
                nc.scalar.copy(WRN[:, 0, cols], PS[:, half, :]).then_inc(sem("wn"), 1)
                nc.scalar.copy(WRN[0:QR - P, 1, cols], PS[0:QR - P, 2 + half, :]).then_inc(sem("wn"), 1)
            for b in range(4):
                act.wait_ge(sem("p_w2"), b + 1)
                nc.scalar.copy(W2[:, 2 * b:2 * b + 2, :], PS[:, 4 + b, :].rearrange("p (q d) -> p q d", q=2))\
                    .then_inc(sem("w2"), 1)

        LN2_BANKS = (6, 7)

        def l1_latents(pe):
            pe.wait_ge(sem("wd_lo"), 1)
            pe.wait_ge(sem("wn"), 4)
            pe.wait_ge(sem("w2"), 4)
            for n in range(2):
                pe.wait_ge(sem("ln2_lo"), 2 * n + 2)
                for m in range(2):
                    for c in range(NC):
                        last = mm3(PS[:, 2 * m + n, :], (WDH[:, c, tile(m)], WDL[:, c, tile(m)]),
                                   xt(c, slice(512 * n, 512 * n + 512)), start=(c == 0), stop=(c == NC - 1))
                    last.then_inc(sem("lat"), 1)
            for tt in range(NT):
                for c in range(NC):
                    last = mm3(PS[:, 4, tt * KVR:(tt + 1) * KVR], xt(c, tile(tt)),
                               (WDH[:, c, QR:D], WDL[:, c, QR:D]), start=(c == 0), stop=(c == NC - 1))
            last.then_inc(sem("lat_kv"), 1)

        def l1_project(pe, tt):
            if tt == 0:
                pe.wait_ge(sem("lt"), 4)
                pe.wait_ge(sem("kv"), 1)
            for b in range(4):
                if tt:
                    if b == 0:
                        pe.wait_ge(sem("q_rot"), 3 * tt)
                    if b == 2:
                        pe.wait_ge(sem("q_un"), tt)
                for kt in range(2):
                    last = nc.tensor.matmul(PS[:, b, :], LT[:, kt, tile(tt)], WRN[:, kt, 512 * b:512 * b + 512],
                                            start=(kt == 0), stop=(kt == 1))
                if b % 2:
                    last.then_inc(sem("proj"), 1)
            if tt:
                pe.wait_ge(sem("k_rot"), 3 * tt)
            for b in range(2):
                last = nc.tensor.matmul(PS[:, 4 + b, :], LT[:, 1, tile(tt)], WKR[:, 512 * b:512 * b + 512],
                                        start=True, stop=True)
            last.then_inc(sem("proj"), 1)

        def l1_rotate(dve, tt):
            co = ROPE[:, 0, tt, :].unsqueeze(1).to_broadcast([P, H1, DR])
            h = DR // 2
            for name, banks, buf, ready in (("q_rot", (0, 2), TQ, 3 * tt + 1), ("k_rot", (4, 6), TK, 3 * tt + 3)):
                dve.wait_ge(sem("proj"), ready)
                if tt:
                    dve.wait_ge(sem(name[0] + "_sum"), (2 if name[0] == "q" else 1) * tt)
                src = PS[:, banks[0]:banks[1], :].rearrange("p b (h d) -> p (b h) d", d=DR)
                a, b = (buf[:, i, :].rearrange("p (h d) -> p h d", d=DR) for i in range(2))
                nc.vector.tensor_tensor(a, src, co, ALU.mult).then_inc(sem(name), 1)
                for j in range(2):
                    si = ROPE[:, 1, tt, j * h:(j + 1) * h].unsqueeze(1).to_broadcast([P, H1, h])
                    nc.vector.tensor_tensor(b[:, :, j * h:(j + 1) * h], src[:, :, (1 - j) * h:(2 - j) * h], si,
                                            ALU.mult).then_inc(sem(name), 1)

        def l1_sums(pool, tt):
            pool.wait_ge(sem("q_rot"), 3 * tt + 3)
            if tt >= 2:
                pool.wait_ge(sem("q_tr"), 4 * (tt - 1))
            dst = QTOK[:, tt % 2, :].rearrange("p (q r) -> p q r", r=2 * P)
            a, b = (TQ[:, i, :].rearrange("p (q e d) -> p q e d", e=2, d=DR) for i in range(2))
            for e, cols in ((0, slice(0, DR)), (1, slice(2 * P - DR, 2 * P))):
                nc.gpsimd.tensor_tensor(dst[:, :, cols], a[:, :, e], b[:, :, e], ALU.add).then_inc(sem("q_sum"), 1)
            pool.wait_ge(sem("k_rot"), 3 * tt + 3)
            if tt >= 2:
                pool.wait_ge(sem("k_tr"), 2 * (tt - 1))
            nc.gpsimd.tensor_tensor(KTOK[:, tt % 2, :], TK[:, 0, :], TK[:, 1, :], ALU.add).then_inc(sem("k_sum"), 1)

        def l1_unrotated(act, tt):
            act.wait_ge(sem("proj"), 3 * tt + 2)
            if tt >= 2:
                act.wait_ge(sem("q_tr"), 4 * (tt - 1))
            dst = QTOK[:, tt % 2, :].rearrange("p (q r) -> p q r", r=2 * P)[:, :, DR:2 * P - DR]
            nc.scalar.copy(dst, PS[:, 2:4, :].rearrange("p b (q d) -> p (b q) d", d=2 * DR)).then_inc(sem("q_un"), 1)

        def l1_transpose(pe, tt):
            pe.wait_ge(sem("q_sum"), 2 * tt + 2)
            pe.wait_ge(sem("q_un"), tt + 1)
            for g in range(6):
                n = 6 * tt + g
                if g == 4:
                    pe.wait_ge(sem("k_sum"), tt + 1)
                if n >= 2:
                    pe.wait_ge(sem("qk_t"), n - 1)
                src = QTOK if g < 4 else KTOK
                for i in range(4):
                    col = (4 * (g % 4) + i) * P
                    last = nc.tensor.transpose(PS[:, 6 + g % 2, i * P:(i + 1) * P], src[:, tt % 2, col:col + P], IDF[:, :])
                last.then_inc(sem("q_tr" if g < 4 else "k_tr"), 1)

        def l1_transposed(act, tt):
            for g in range(6):
                act.wait_ge(sem("q_tr" if g < 4 else "k_tr"), 4 * tt + g + 1 if g < 4 else 2 * tt + g - 3)
                dst = (QT if g < 4 else KT)[:, 4 * (g % 4):4 * (g % 4) + 4, tile(tt)]
                nc.scalar.activation(dst, PS[:, 6 + g % 2, :].rearrange("p (h t) -> p h t", h=4), ACT.Copy,
                                     scale=SCALE if g < 4 else 1.0).then_inc(sem("qk_t"), 1)

        GROUPS = 12

        def group(tt, b):
            return tt if tt < 4 else 4 + 2 * (tt - 4) + b

        def by_act(n):
            return n >= 4 and n % 2 == 1

        def unit_of(n):
            return n if n < 4 else 4 + (n - 4) // 2

        def back(h, n, k, total):
            if n - k >= 0:
                return h, n - k
            return None if isinstance(h, int) and h == 0 else (h - 1, n - k + total)

        def wait_group(eng, h, n):
            done = sum(by_act(m) == by_act(n) for m in range(n + 1))
            if by_act(n):
                eng.wait_ge(sem("a_pa"), 4 * h + done)
            else:
                eng.wait_ge(sem("a_pd"), 8 * h + done)

        def a_scores(pe, h, p, tt):
            if tt == 0:
                pe.wait_ge(sem("a_hi"), 2 * h + 2)
                pe.wait_ge(sem("a_lo"), 2 * h + 2)
            if prev := back(h, tt, 2, NT):
                pe.wait_ge(sem("a_p"), 8 * prev[0] + prev[1] + 1)
            keys = (tt + 1) * P
            for n0 in range(0, keys, 512):
                n1 = min(keys, n0 + 512)
                o = PS[:, 2 * (tt % 2) + n0 // 512, 0:n1 - n0]
                nc.tensor.matmul(o, QH[:, p, tile(tt)], KH[:, p, n0:n1], start=True, stop=False)
                nc.tensor.matmul(o, QH[:, p, tile(tt)], KL[:, p, n0:n1], start=False, stop=False)
                if n1 == keys:
                    nc.tensor.matmul(o[:, n1 - n0 - P:n1 - n0], IDB[:, :], MASKB[:, :], start=False, stop=False)
                last = nc.tensor.matmul(o, QL[:, p, tile(tt)], KH[:, p, n0:n1], start=False, stop=True)
            last.then_inc(sem("a_s"), 1)

        def s_view(tt):
            keys = (tt + 1) * P
            return PS[:, 2 * (tt % 2):2 * (tt % 2) + 2, :].rearrange("p b n -> p (b n)")[:, 0:keys]

        def a_transpose(pe, h, tt):
            pe.wait_ge(sem("a_p"), 8 * h + tt + 1)
            for b in range(1 + tt // 4):
                n = group(tt, b)
                if prev := back(h, n, 2, GROUPS):
                    wait_group(pe, *prev)
                for sb in range(4 * b, min(tt + 1, 4 * b + 4)):
                    last = nc.tensor.transpose(PS[:, 4 + n % 2, tile(sb % 4)], PB[:, tt % 2, tile(sb)], IDF[:, :])
                last.then_inc(sem("a_t"), 1)

        def a_values(pe, h, tt):
            if prev := back(h, tt, 2, NT):
                pe.wait_ge(sem("a_n"), 8 * prev[0] + prev[1] + 1)
            for sb in range(tt + 1):
                n = group(tt, sb // 4)
                if sb % 4 == 0:
                    wait_group(pe, h, n)
                last = nc.tensor.matmul(PS[:, 6 + tt % 2, 0:KVR], PT[:, n % 4, tile(sb % 4)], KV[:, sb, :],
                                        start=(sb == 0), stop=(sb == tt))
            last.then_inc(sem("a_o"), 1)

        def a_group_out(eng, h, n):
            tt = unit_of(n)
            b = 1 if by_act(n) else 0
            width = (min(tt + 1, 4 * b + 4) - 4 * b) * P
            eng.wait_ge(sem("a_t"), GROUPS * h + n + 1)
            if prev := back(h, n, 4, GROUPS):
                eng.wait_ge(sem("a_o"), 8 * prev[0] + unit_of(prev[1]) + 1)
            copy = nc.scalar.copy if by_act(n) else nc.vector.tensor_copy
            copy(PT[:, n % 4, 0:width], PS[:, 4 + n % 2, 0:width]).then_inc(sem("a_pa" if by_act(n) else "a_pd"), 1)

        def behind(h, p, tt, k):
            if u := back(h, tt, k, NT):
                return u[0], u[1], p if tt >= k else 1 - p

        def pe_unit(pe, h, p, tt):
            a_scores(pe, h, p, tt)
            if u := behind(h, p, tt, 1):
                a_transpose(pe, *u[:2])
            if u := behind(h, p, tt, 2):
                a_values(pe, *u[:2])

        def ring_rows(p):
            return slice(0, DR) if p == 0 else slice(DR, P)

        def key_rows(h, p):
            return KT[ring_rows(p), :, :].rearrange("p q t -> p (q t)")[:, bass.ds((h - p) * (T // 2), T)]

        def a_hi(act, h, p, what):
            if not (isinstance(h, int) and h < 2):
                act.wait_ge(sem("a_s"), 8 * (h - 1))
            if what == 0:
                nc.scalar.copy(QH[:, p, :], QT[:, bass.ds(h, 1), :].rearrange("p o t -> p (o t)"))\
                    .then_inc(sem("a_hi"), 1)
            else:
                r = ring_rows(p)
                nc.scalar.copy(KH[r, p, :], key_rows(h, p))\
                    .then_inc(sem("a_hi"), 1)

        def a_lo(pool, h, p):
            r = ring_rows(p)
            pool_wait(pool, "a_hi", 2 * h + 1)
            nc.gpsimd.tensor_tensor(QL[:, p, :], QT[:, bass.ds(h, 1), :].rearrange("p o t -> p (o t)"),
                                    f(QH[:, p, :]), ALU.subtract).then_inc(sem("a_lo"), 1)
            pool.wait_ge(sem("a_hi"), 2 * h + 2)
            pool_wait(pool, "a_lo", 2 * h + 1)
            nc.gpsimd.tensor_tensor(KL[r, p, :], key_rows(h, p), f(KH[r, p, :]), ALU.subtract).then_inc(sem("a_lo"), 1)
            pool_wait(pool, "a_lo", 2 * h + 2)

        def a_exp(act, h, tt):
            act.wait_ge(sem("a_m"), 8 * h + tt + 1)
            if prev := back(h, tt, 2, NT):
                act.wait_ge(sem("a_t"), GROUPS * prev[0] + group(prev[1], prev[1] // 4) + 1)
            keys = (tt + 1) * P
            nc.scalar.activation(PB[:, tt % 2, 0:keys], s_view(tt), ACT.Exp, bias=NM[:, bass.ds(8 * h + tt, 1)],
                                 accum_out=LS[:, bass.ds(8 * h + tt, 1)]).then_inc(sem("a_p"), 1)

        def act_unit(act, h, p, tt, final=False):
            a_exp(act, h, tt)
            u = behind(h, p, tt, 1)
            if u and u[1] >= 4:
                a_group_out(act, u[0], group(u[1], 1))
            if not final and tt in (1, 3):
                a_hi(act, h + 1, 1 - p, tt // 2)

        def a_max(dve, h, tt):
            dve.wait_ge(sem("a_s"), 8 * h + tt + 1)
            nc.vector.tensor_reduce(NM[:, bass.ds(8 * h + tt, 1)], s_view(tt), axis=AX.X, op=ALU.max, negate=True)\
                .then_inc(sem("a_m"), 1)

        def a_out(dve, h, tt, p):
            dve.wait_ge(sem("a_o"), 8 * h + tt + 1)
            c = tt * P + p * KVR
            nc.vector.tensor_copy(QT[:, bass.ds(h - p, 1), c:c + KVR].rearrange("p o d -> p (o d)"),
                                  PS[:, 6 + tt % 2, 0:KVR]).then_inc(sem("a_n"), 1)

        def dve_unit(dve, h, p, tt):
            a_max(dve, h, tt)
            if u := behind(h, p, tt, 1):
                a_group_out(dve, u[0], group(u[1], 0))
            if u := behind(h, p, tt, 2):
                a_out(dve, *u)

        def a_weights_sum(dve, h):
            dve.wait_ge(sem("a_p"), 8 * h + 8)
            nc.vector.reciprocal(RL[:, bass.ds(8 * h, NT)], LS[:, bass.ds(8 * h, NT)]).then_inc(sem("a_rl"), 1)

        def a_normalise(pool, h, p):
            pool_wait(pool, "a_rl", h + 1)
            pool_wait(pool, "a_n", 8 * h + 8)
            o = QT[:, bass.ds(h - p, 1), :].rearrange("p o (t d) -> p (o t) d", d=P)[:, :, p * KVR:(p + 1) * KVR]
            nc.gpsimd.tensor_tensor(o, o, RL[:, bass.ds(8 * h, NT)].unsqueeze(2).to_broadcast([P, NT, KVR]),
                                    ALU.mult).then_inc(sem("a_on"), 1)

        def o1_banks(tt):
            return (0, 1) if tt % 2 == 0 else (4, 5)

        def o1_transpose(pe, tt):
            if tt >= 2:
                pe.wait_ge(sem("o1_ta"), tt - 1)
                pe.wait_ge(sem("o1_td"), tt - 1)
            for q in range(H1 // 2):
                last = nc.tensor.transpose(PS[:, o1_banks(tt)[q // 4], tile(q % 4)],
                                           QT[:, 2 * q, tile(tt)], IDF[:, :])
                if q % 4 == 3:
                    last.then_inc(sem("o1_tr"), 1)

        def o1_project(pe, tt):
            pe.wait_ge(sem("o1_ta"), tt + 1)
            pe.wait_ge(sem("o1_td"), tt + 1)
            if tt >= 2:
                pe.wait_ge(sem("x3"), tt - 1)
            for q in range(H1 // 2):
                last = nc.tensor.matmul(PS[:, 2 + tt % 2, 0:D], OT1[:, tt % 2, q, :], W2[:, q, :],
                                        start=(q == 0), stop=(q == H1 // 2 - 1))
            last.then_inc(sem("o1"), 1)

        def o1_out(eng, tt, half):
            eng.wait_ge(sem("o1_tr"), 2 * tt + half + 1)
            if tt >= 2:
                eng.wait_ge(sem("o1"), tt - 1)
            copy = nc.scalar.copy if half == 0 else nc.vector.tensor_copy
            copy(OT1[:, tt % 2, 4 * half:4 * half + 4, :],
                 PS[:, o1_banks(tt)[half], :].rearrange("p (q t) -> p q t", q=4))\
                .then_inc(sem("o1_ta" if half == 0 else "o1_td"), 1)

        LN3_BANKS = (6, 7)

        def ff_split(pool, k):
            if k >= 2:
                pool.wait_ge(sem("ff_gu"), k - 1)
            nc.gpsimd.tensor_copy(GUH[:, k % 2], GU[:, k]).then_inc(sem("ff_hi"), 1)
            pool.wait_ge(sem("ff_hi"), k + 1)
            nc.gpsimd.tensor_tensor(GUL[:, k % 2], GU[:, k], f(GUH[:, k % 2]), ALU.subtract).then_inc(sem("ff_w"), 1)

        def ff_up(pe, k):
            pe.wait_ge(sem("ff_w"), k + 1)
            if k >= 2:
                pe.wait_ge(sem("ff_h"), k - 1)
            for j in range(2):
                for n in range(2):
                    if k == 0:
                        pe.wait_ge(sem("ln3_lo"), 2 * n + 2)
                    for c in range(NC):
                        last = mm3(PS[:, 4 * (k % 2) + 2 * j + n, :],
                                   (GUH[:, k % 2, NC * j + c, :], GUL[:, k % 2, NC * j + c, :]),
                                   xt(c, slice(512 * n, 512 * n + 512)), start=(c == 0), stop=(c == NC - 1))
            last.then_inc(sem("ff_gu"), 1)

        def gu_banks(k, j):
            b = 4 * (k % 2) + 2 * j
            return PS[:, b:b + 2, :].rearrange("p b n -> p (b n)")

        def ff_act(act, k):
            act.wait_ge(sem("ff_gu"), k + 1)
            if k >= 2:
                act.wait_ge(sem("ff_h"), k - 1)
            nc.scalar.activation(EX[:, k % 2, :], gu_banks(k, 0), ACT.Silu, scale=GSUS[:, 0, k:k + 1])\
                .then_inc(sem("ff_ex"), 1)

        def ff_gate(dve, k):
            dve.wait_ge(sem("ff_ex"), k + 1)
            nc.vector.scalar_tensor_tensor(out=HT[:, k, :], in0=gu_banks(k, 1), scalar=GSUS[:, 1, k:k + 1],
                                           in1=EX[:, k % 2, :], op0=ALU.mult, op1=ALU.mult).then_inc(sem("ff_h"), 1)

        def router(dve):
            count = [0]

            def step(ins):
                count[0] += 1
                ins.then_inc(sem("rt"), 1)
                dve.wait_ge(sem("rt"), count[0])

            def r3(i):
                return RT[:, i, :].rearrange("p (t e) -> p t e", t=NT)
            ex, sc, s, ms = r3(0), r3(1), r3(2), r3(3)
            V = nc.vector
            dve.wait_ge(sem("rt_exp"), 1)
            step(V.tensor_scalar(sc, ex, 1.0, None, ALU.add))
            step(V.reciprocal(sc, sc))
            step(V.tensor_tensor(s, sc, EBIAS.unsqueeze(1).to_broadcast([P, NT, NR]), ALU.add))
            s4 = RT[:, 2, :].rearrange("p (g a b) -> p g a b", a=2, b=2)
            hi = RT[:, 4, 0:64].rearrange("p (g a) -> p g a", a=2)
            lo = RT[:, 4, 64:128].rearrange("p (g a) -> p g a", a=2)
            V.tensor_tensor(hi, s4[:, :, :, 0], s4[:, :, :, 1], ALU.max)
            step(V.tensor_tensor(lo, s4[:, :, :, 0], s4[:, :, :, 1], ALU.min))
            t1, t2, t3, gs = (RT[:, 5, 32 * k:32 * k + 32] for k in range(4))
            V.tensor_tensor(t1, hi[:, :, 0], hi[:, :, 1], ALU.max)
            V.tensor_tensor(t2, hi[:, :, 0], hi[:, :, 1], ALU.min)
            step(V.tensor_tensor(t3, lo[:, :, 0], lo[:, :, 1], ALU.max))
            step(V.tensor_tensor(t2, t2, t3, ALU.max))
            step(V.tensor_tensor(gs, t1, t2, ALU.add))
            g3 = gs.rearrange("p (t g) -> p t g", g=NGRP)
            other = g3.unsqueeze(2).to_broadcast([P, NT, NGRP, NGRP])
            own = g3.unsqueeze(3).to_broadcast([P, NT, NGRP, NGRP])
            gt = RT[:, 6, :].rearrange("p (t g o) -> p t g o", t=NT, g=NGRP)
            eq = RT[:, 7, :].rearrange("p (t g o) -> p t g o", t=NT, g=NGRP)
            V.tensor_tensor(gt, other, own, ALU.is_gt)
            step(V.tensor_tensor(eq, other, own, ALU.is_equal))
            tri = LTRI.unsqueeze(1).to_broadcast([P, NT, NR])
            step(V.tensor_tensor(RT[:, 7, :].rearrange("p (t e) -> p t e", t=NT),
                                 RT[:, 7, :].rearrange("p (t e) -> p t e", t=NT), tri, ALU.mult))
            step(V.tensor_tensor(RT[:, 6, :], RT[:, 6, :], RT[:, 7, :], ALU.add))
            step(V.reduce_sum(t1, RT[:, 6, :].rearrange("p (g o) -> p g o", o=NGRP), axis=AX.X))
            step(V.tensor_scalar(t1, t1, 1.5, None, ALU.is_lt))
            step(V.tensor_tensor(RT[:, 3, :].rearrange("p (g o) -> p g o", o=4),
                                 RT[:, 2, :].rearrange("p (g o) -> p g o", o=4),
                                 t1.unsqueeze(2).to_broadcast([P, 32, 4]), ALU.mult))
            key = KEY.unsqueeze(1).to_broadcast([P, NT, NR])
            m = RT[:, 4, 0:NT]
            sel = [r3(6), r3(7)]
            for n in range(2):
                step(V.reduce_max(m, ms, axis=AX.X))
                step(V.tensor_tensor(sel[n], ms, m.unsqueeze(2).to_broadcast([P, NT, NR]), ALU.is_equal))
                step(V.tensor_tensor(sel[n], sel[n], key, ALU.mult))
                step(V.reduce_max(m, sel[n], axis=AX.X))
                step(V.tensor_tensor(sel[n], sel[n], m.unsqueeze(2).to_broadcast([P, NT, NR]), ALU.is_equal))
                if n == 0:
                    step(V.scalar_tensor_tensor(out=ms, in0=sel[0], scalar=NEG, in1=ms, op0=ALU.mult, op1=ALU.add))
            step(V.tensor_tensor(sel[0], sel[0], sel[1], ALU.add))
            step(V.tensor_tensor(sc, sc, sel[0], ALU.mult))
            step(V.reduce_sum(m, sc, axis=AX.X))
            step(V.tensor_scalar(m, m, 1e-20, None, ALU.add))
            step(V.reciprocal(m, m))
            step(V.tensor_tensor(CMB[:, :, NSH:NE], sc, m.unsqueeze(2).to_broadcast([P, NT, NR]), ALU.mult))

        @block.sync
        def _(sp):
            def load(name, dst, src):
                sp.dma_start(dst, src).then_inc(sem("ld_" + name), 16)
            for j in range(2):
                load("x", X[:, 4 * j:4 * j + 4, :], x.rearrange("(t p) d -> p t d", p=P)[:, 4 * j:4 * j + 4, :])
            load("wq", WQR[:], wqkv.rearrange("(c p) n -> p c n", p=P))
            load("cst", CST[:], consts)
            load("wo0", WO0[:], wo0.rearrange("(c p) n -> p c n", p=P))
            load("wr", WRR[:], wr.rearrange("(c p) n -> p c n", p=P))
            load("gsus", GSUS[:], gsus)
            load("ds", DS[:], ds)
            load("rope", ROPE[:], rope)
            sp.wait_ge(sem("l0_slots"), 4)
            load("up", UP[:], up)
            load("down", DOWN[:], down)
            sp.wait_ge(sem("x1"), NT)
            load("prod", WQN[:], wqn)
            load("prod", WKN[:], wkn)
            load("prod", WV[:], wv)
            load("prod", WO1[:], wo1)
            load("wrn", WRN[:, :, 0:H1 * DR], wqr.rearrange("p k h d -> p k (h d)"))
            load("wrn", WKR[:], wkr.rearrange("p h d -> p (h d)"))
            load("wd", WDR[:], wd.rearrange("(c p) n -> p c n", p=P))
            sp.wait_ge(sem("proj"), 3 * NT)
            load("gu", GU[:], gu.rearrange("p f j c i -> p f (j c) i"))
            load("dnw", DNW[:], dnw)
            for tt in range(NT):
                sp.wait_ge(sem("y"), tt + 1)
                sp.dma_start(out[tile(tt), :], XN[:, tt, :]).then_inc(sem("stored"), 16)
            sp.wait_ge(sem("stored"), 16 * NT)

        @block.gpsimd
        def _(pool):
            nc.gpsimd.memset(HALF[:], -0.5).then_inc(sem("half"), 1)
            nc.gpsimd.memset(IDF[:], 0.0).then_inc(sem("cst0"), 1)
            nc.gpsimd.memset(IDB[:], 0.0).then_inc(sem("cst0"), 1)
            nc.gpsimd.memset(MASKB[:], 0.0).then_inc(sem("cst0"), 1)
            nc.gpsimd.memset(VA[:, :, :, D0:D0 + 1], 1.0).then_inc(sem("ones"), 1)
            nc.gpsimd.memset(f(ONE[:]), 1.0).then_inc(sem("one"), 1)
            nc.gpsimd.memset(CMB[:, :, 0:NSH], 1.0).then_inc(sem("ones"), 1)
            pool.wait_ge(sem("cst0"), 3)
            for m in (IDF, IDB):
                nc.gpsimd.affine_select(out=m[:], in_=m[:], pattern=[[-1, P]], compare_op=ALU.not_equal, fill=1.0,
                                        base=0, channel_multiplier=1).then_inc(sem("ident"), 1)
            nc.gpsimd.affine_select(out=MASKB[:], in_=MASKB[:], pattern=[[-1, P]], compare_op=ALU.is_ge, fill=NEG,
                                    base=0, channel_multiplier=1).then_inc(sem("ident"), 1)
            ln_pool(pool, 0)
            pool.wait_ge(sem("l0_qkv"), NT)
            nc.gpsimd.memset(OT4[:], 0.0).then_inc(sem("ot4"), 1)
            for g in range(4):
                pool.wait_ge(sem("l0_p1"), 2 * g + 2)
                for qk in range(2):
                    z = Y[:, 2 * g:2 * g + 2, qk]
                    nc.gpsimd.tensor_tensor(z, z, SLT[:, qk, 2 * g:2 * g + 2, :, 0, :], ALU.subtract)\
                        .then_inc(sem("l0_r1"), 1)
            loop_heads4(pool, lambda h, r, **kw: pool_head(pool, h))
            ln_pool(pool, 1)
            pool.wait_ge(sem("ld_up"), 16)
            pool.wait_ge(sem("ld_down"), 16)
            pool.wait_ge(sem("x1"), NT)
            moe_split(pool, 0, 0)
            moe_split(pool, 1, 1)
            with pool.Fori(1, NE // 2) as i:
                moe_split(pool, 2 * i, 0)
                moe_split(pool, 2 * i + 1, 1)
            pool.wait_ge(sem("m_dsplit"), NE)
            nc.gpsimd.memset(WRN[QR - P:P, 1, H1 * DR:2 * H1 * DR], 0.0).then_inc(sem("wn0"), 1)
            pool.wait_ge(sem("wn0"), 1)
            ln_pool(pool, 2)
            for tt in range(NT):
                l1_sums(pool, tt)
            pool.wait_ge(sem("k_lo"), 2)
            a_lo(pool, 0, 0)

            def one(h, p, first=False, final=False):
                if not final:
                    a_lo(pool, h + 1, 1 - p)
                if not first:
                    a_normalise(pool, h - 1, 1 - p)
            loop_heads(pool, one)
            a_normalise(pool, H1 - 1, 1)
            ln_pool(pool, 3)
            pool.wait_ge(sem("ld_gu"), 16)
            for k in range(NF):
                ff_split(pool, k)

        @block.scalar
        def _(act):
            act.wait_ge(sem("ld_wq"), 16)
            nc.scalar.copy(WQH[:, :, 2 * D:], WQR[:, :, 2 * D:]).then_inc(sem("wq_hi"), 1)
            act.wait_ge(sem("wc"), 3)
            nc.scalar.copy(WQH[:, :, 0:2 * D], WC[:]).then_inc(sem("wq_hi"), 1)
            act.wait_ge(sem("betac"), 3)
            nc.scalar.copy(BH[:], BETAC[:].unsqueeze(1).to_broadcast([1, H0, 2, D0])).then_inc(sem("beta_hi"), 1)
            act.wait_ge(sem("ld_wr"), 16)
            nc.scalar.copy(WRH[:], WRR[:]).then_inc(sem("wr_hi"), 1)
            ln_act(act, 0, LN_BANKS)
            for tt in range(NT):
                act.wait_ge(sem("l0_qkv"), tt + 1)
                if tt >= 2:
                    act.wait_ge(sem("l0_vs"), tt - 1)
                nc.scalar.activation(SQ[:, tt % 2], qk_bank(tt).rearrange("p (n d) -> p n d", d=D0), ACT.Square)\
                    .then_inc(sem("l0_csq"), 1)
                nc.scalar.copy(VA[:, tt, :, 0:D0], PS[:, tt % 2, 0:D].rearrange("p (h d) -> p h d", h=H0))\
                    .then_inc(sem("l0_v"), 1)
                if tt % 2:
                    r = slice(tt - 1, tt + 1)
                    act.wait_ge(sem("l0_vs"), tt + 1)
                    nc.scalar.activation(SD[:, r, 0, :], VS[:, r, 0, :], ACT.Sqrt, scale=1.0).then_inc(sem("l0_sd"), 1)
                    nc.scalar.activation(SD[:, r, 1, :], VS[:, r, 1, :], ACT.Sqrt, scale=1.0 / D0)\
                        .then_inc(sem("l0_sd"), 1)
            for g in range(4):
                act.wait_ge(sem("l0_z"), 2 * g + 2)
                for qk in range(2):
                    nc.scalar.copy(SLT[:, qk, 2 * g:2 * g + 2, :, 0, :], Y[:, 2 * g:2 * g + 2, qk]).then_inc(sem("l0_p1"), 1)
            for g in range(4):
                act.wait_ge(sem("l0_r1"), 2 * g + 2)
                for qk, s in ((0, 1), (1, 3)):
                    nc.scalar.copy(SLT[:, qk, 2 * g:2 * g + 2, :, s, :], Y[:, 2 * g:2 * g + 2, qk]).then_inc(sem("l0_p2"), 1)
            loop_heads4(act, lambda h, r, first=False, **kw: act_head(act, h, r % 2, first))
            for j in range(4):
                act.wait_ge(sem("l0_ot"), j + 1)
                bank = PS[:, 6 + j % 2, :].rearrange("p (c t) -> p c t", c=NC)
                nc.scalar.copy(OT0[:, :, 256 * j:256 * j + 256], bank).then_inc(sem("l0_oT"), 1)
            ln_act(act, 1, LN_BANKS)
            act.wait_ge(sem("logits"), 1)
            nc.scalar.activation(RT[:, 0, :], PS[:, 4, 0:P], ACT.Exp, scale=-1.0).then_inc(sem("rt_exp"), 1)
            moe_act(act, 0, 0)
            moe_act(act, 1, 1)
            with act.Fori(1, NE // 2) as i:
                moe_act(act, 2 * i, 0)
                moe_act(act, 2 * i + 1, 1)
            act.wait_ge(sem("ld_wd"), 16)
            nc.scalar.copy(WDH[:], WDR[:]).then_inc(sem("wd_hi"), 1)
            l1_products_out(act)
            ln_act(act, 2, LN2_BANKS)
            for n in range(2):
                act.wait_ge(sem("lat"), 2 * n + 1)
                nc.scalar.copy(LT[:, 0, 512 * n:512 * n + 512], PS[:, n, :]).then_inc(sem("lt"), 1)
            act.wait_ge(sem("lat_kv"), 1)
            nc.scalar.copy(KV[:], PS[:, 4, :].rearrange("p (t d) -> p t d", t=NT)).then_inc(sem("kv"), 1)
            for tt in range(NT):
                l1_unrotated(act, tt)
                if tt:
                    l1_transposed(act, tt - 1)
            l1_transposed(act, NT - 1)
            act.wait_ge(sem("q_sum"), 2 * NT)
            nc.scalar.copy(PB[0:KVR, 0, :], LT[P - KVR:P, 1, :]).then_inc(sem("k_low"), 1)
            act.wait_ge(sem("k_low"), 1)
            nc.scalar.copy(KH[P - KVR:P, 0, :], LT[P - KVR:P, 1, :]).then_inc(sem("k_hi"), 1)
            nc.scalar.copy(KH[0:KVR, 1, :], PB[0:KVR, 0, :]).then_inc(sem("k_hi"), 1)
            act.wait_ge(sem("k_lo"), 2)
            a_hi(act, 0, 0, 0)
            a_hi(act, 0, 0, 1)

            def one(h, p, first=False, final=False):
                for tt in range(NT):
                    act_unit(act, h, p, tt, final)
            loop_heads(act, one)
            a_group_out(act, H1 - 1, group(NT - 1, 1))
            for tt in range(NT):
                o1_out(act, tt, 0)
            ln_act(act, 3, LN3_BANKS)
            act.wait_ge(sem("ld_gsus"), 16)
            for k in range(NF):
                ff_act(act, k)

        @block.vector
        def _(dve):
            def x_loaded(tt):
                if tt % 4 == 0:
                    dve.wait_ge(sem("ld_x"), 32)
            dve.wait_ge(sem("ld_wq"), 16)
            dve.wait_ge(sem("ld_cst"), 16)
            wc = WC[:].rearrange("p c (n d) -> p c n d", d=D0)
            ws = WS[:, 0:NC * 2 * H0].rearrange("p (c n) -> p c n", c=NC)
            nc.vector.tensor_tensor(wc, WQR[:, :, 0:2 * D].rearrange("p c (n d) -> p c n d", d=D0),
                                    GAMMA.unsqueeze(1).unsqueeze(1).to_broadcast([P, NC, 2 * H0, D0]), ALU.mult)\
                .then_inc(sem("wc"), 1)
            nc.vector.reduce_sum(WS[0:1, NC * 2 * H0:NC * 2 * H0 + 1], BETA[0:1, :], axis=AX.X).then_inc(sem("betac"), 1)
            dve.wait_ge(sem("wc"), 1)
            nc.vector.reduce_sum(ws, wc, axis=AX.X).then_inc(sem("wc"), 1)
            dve.wait_ge(sem("betac"), 1)
            for q in range(2):
                nc.vector.scalar_tensor_tensor(
                    out=BETAC[:, q, :], in0=WS[0:1, NC * 2 * H0:NC * 2 * H0 + 1].to_broadcast([1, D0]),
                    scalar=-1.0 / D0, in1=BETA[0:1, :], op0=ALU.mult, op1=ALU.add).then_inc(sem("betac"), 1)
            dve.wait_ge(sem("wc"), 2)
            nc.vector.scalar_tensor_tensor(out=wc, in0=ws.unsqueeze(3).to_broadcast([P, NC, 2 * H0, D0]),
                                           scalar=-1.0 / D0, in1=wc, op0=ALU.mult, op1=ALU.add).then_inc(sem("wc"), 1)
            ln_dve_stats(dve, 0, x_loaded)
            ln_dve_norm(dve, 0)
            dve.wait_ge(sem("wq_hi"), 2)
            nc.vector.tensor_tensor(WQL[:, :, 0:2 * D], WC[:], f(WQH[:, :, 0:2 * D]), ALU.subtract).then_inc(sem("wq_lo"), 1)
            nc.vector.tensor_tensor(WQL[:, :, 2 * D:], WQR[:, :, 2 * D:], f(WQH[:, :, 2 * D:]), ALU.subtract)\
                .then_inc(sem("wq_lo"), 1)
            dve.wait_ge(sem("beta_hi"), 1)
            nc.vector.tensor_tensor(BL[:].rearrange("p (h q d) -> p h q d", q=2, d=D0),
                                    BETAC[:].unsqueeze(1).to_broadcast([1, H0, 2, D0]),
                                    f(BH[:]).rearrange("p (h q d) -> p h q d", q=2, d=D0), ALU.subtract)\
                .then_inc(sem("beta_lo"), 1)
            dve.wait_ge(sem("wr_hi"), 1)
            nc.vector.tensor_tensor(WRL[:], WRR[:], f(WRH[:]), ALU.subtract).then_inc(sem("wr_lo"), 1)
            ln_dve_lo(dve, 0, LN_BANKS)
            for j in range(4):
                for tt in (2 * j, 2 * j + 1):
                    dve.wait_ge(sem("l0_csq"), tt + 1)
                    nc.vector.reduce_sum(VS[:, tt], SQ[:, tt % 2], axis=AX.X).then_inc(sem("l0_vr0"), 1)
                    dve.wait_ge(sem("l0_vr0"), tt + 1)
                    nc.vector.tensor_tensor(VS[:, tt], VS[:, tt], CST[:, 80:112].rearrange("p (q h) -> p q h", q=2),
                                            ALU.add).then_inc(sem("l0_vs"), 1)
                r = slice(2 * j, 2 * j + 2)
                dve.wait_ge(sem("l0_sd"), 2 * j + 2)
                nc.vector.reciprocal(SD[:, r], SD[:, r]).then_inc(sem("l0_rs"), 1)
                dve.wait_ge(sem("l0_rs"), j + 1)
                for tt in (2 * j, 2 * j + 1):
                    nc.vector.tensor_tensor(Y[:, tt].rearrange("p q h d -> p (q h) d"),
                                            qk_bank(tt).rearrange("p (n d) -> p n d", d=D0),
                                            SD[:, tt].rearrange("p q h -> p (q h)").unsqueeze(2)
                                            .to_broadcast([P, 2 * H0, D0]), ALU.mult).then_inc(sem("l0_z"), 1)
            for g in range(4):
                r = slice(2 * g, 2 * g + 2)
                dve.wait_ge(sem("l0_p2"), 2 * g + 2)
                nc.vector.tensor_tensor(SLT[:, 0, r, :, 2, :], Y[:, r, 0], SLT[:, 0, r, :, 1, :], ALU.subtract)\
                    .then_inc(sem("l0_p3"), 1)
                nc.vector.tensor_tensor(SLT[:, 1, r, :, 6, :], Y[:, r, 1], SLT[:, 1, r, :, 3, :], ALU.subtract)\
                    .then_inc(sem("l0_p3"), 1)

                def th(a):
                    return a.rearrange("p t h s d -> p (t h) s d")
                q, k = SLT[:, 0, r], SLT[:, 1, r]
                nc.vector.tensor_copy(th(k[:, :, :, 1:3]), th(k[:, :, :, 0:1]).to_broadcast([P, 32, 2, D0]))
                nc.vector.tensor_copy(th(k[:, :, :, 4:6]), th(k[:, :, :, 3:4]).to_broadcast([P, 32, 2, D0]))
                nc.vector.tensor_copy(th(q[:, :, :, 6:8]), th(q[:, :, :, 0:2]))
                dve.wait_ge(sem("l0_p3"), 2 * g + 2)
                nc.vector.tensor_copy(th(k[:, :, :, 7:8]), th(k[:, :, :, 6:7]))
                nc.vector.tensor_copy(th(q[:, :, :, 3:6]), th(q[:, :, :, 0:3])).then_inc(sem("l0_slots"), 1)
            dve_stack_out(dve, 0, 0, 0)
            dve_stack_out(dve, 0, 0, 1)
            dve_values(dve, 0, 0)
            loop_heads4(dve, lambda h, r, **kw: dve_head(dve, h, r, **kw))
            dve_out(dve, H0 - 1, 3, 3)
            for tt in range(NT):
                dve.wait_ge(sem("l0_tok"), tt + 1)
                o = PS[:, tt % 4, :].rearrange("p (h e) -> p h e", h=H0)
                z = RT[:, tt, 0:H0]
                nc.vector.tensor_scalar(z, o[:, :, D0], EPS, None, ALU.add).then_inc(sem("l0_z1"), 1)
                dve.wait_ge(sem("l0_z1"), tt + 1)
                nc.vector.reciprocal(z, z).then_inc(sem("l0_z2"), 1)
                dve.wait_ge(sem("l0_z2"), tt + 1)
                nc.vector.tensor_tensor(XN[:, tt].rearrange("p (h d) -> p h d", h=H0), o[:, :, 0:D0],
                                        z.unsqueeze(2).to_broadcast([P, H0, D0]), ALU.mult).then_inc(sem("l0_on"), 1)
            for tt in range(NT):
                dve.wait_ge(sem("l0_wo"), tt + 1)
                nc.vector.tensor_tensor(X[:, tt], PS[:, 4 + tt % 2, 0:D], X[:, tt], ALU.add).then_inc(sem("x1"), 1)
            ln_dve_stats(dve, 1, lambda tt: dve.wait_ge(sem("x1"), tt + 1))
            ln_dve_norm(dve, 1)
            ln_dve_lo(dve, 1, LN_BANKS)
            moe_lo(dve, 0, 0)
            moe_lo(dve, 1, 1)
            router(dve)
            dve.wait_ge(sem("ones"), 2)
            moe_acc(dve, 0)
            with dve.Fori(1, NE // 2) as i:
                moe_lo(dve, 2 * i, 0)
                moe_acc(dve, 2 * i - 1)
                moe_lo(dve, 2 * i + 1, 1)
                moe_acc(dve, 2 * i)
            moe_acc(dve, NE - 1)
            ln_dve_stats(dve, 2, lambda tt: dve.wait_ge(sem("m_acc"), 8 * NE - NT + tt + 1))
            ln_dve_norm(dve, 2)
            dve.wait_ge(sem("wd_hi"), 1)
            nc.vector.tensor_tensor(WDL[:], WDR[:], f(WDH[:]), ALU.subtract).then_inc(sem("wd_lo"), 1)
            ln_dve_lo(dve, 2, LN2_BANKS)
            for n in range(2):
                dve.wait_ge(sem("lat"), 2 * n + 2)
                nc.vector.tensor_copy(LT[:, 1, 512 * n:512 * n + 512], PS[:, 2 + n, :]).then_inc(sem("lt"), 1)
            dve.wait_ge(sem("ld_rope"), 16)
            for tt in range(NT):
                l1_rotate(dve, tt)
            dve.wait_ge(sem("k_hi"), 1)
            nc.vector.tensor_tensor(KL[P - KVR:P, 0, :], LT[P - KVR:P, 1, :], f(KH[P - KVR:P, 0, :]), ALU.subtract)\
                .then_inc(sem("k_lo"), 1)
            dve.wait_ge(sem("k_hi"), 2)
            nc.vector.tensor_tensor(KL[0:KVR, 1, :], PB[0:KVR, 0, :], f(KH[0:KVR, 1, :]), ALU.subtract)\
                .then_inc(sem("k_lo"), 1)

            def one(h, p, first=False, final=False):
                for tt in range(NT):
                    dve_unit(dve, h, p, tt)
                    if tt == 2 and not first:
                        a_weights_sum(dve, h - 1)
            loop_heads(dve, one)
            a_group_out(dve, H1 - 1, group(NT - 1, 0))
            a_out(dve, H1 - 1, NT - 2, 1)
            a_out(dve, H1 - 1, NT - 1, 1)
            a_weights_sum(dve, H1 - 1)
            o1_out(dve, 0, 1)
            for tt in range(NT):
                if tt + 1 < NT:
                    o1_out(dve, tt + 1, 1)
                dve.wait_ge(sem("o1"), tt + 1)
                nc.vector.tensor_tensor(X[:, tt], PS[:, 2 + tt % 2, 0:D], X[:, tt], ALU.add).then_inc(sem("x3"), 1)
            ln_dve_stats(dve, 3, lambda tt: dve.wait_ge(sem("x3"), tt + 1))
            ln_dve_norm(dve, 3)
            ln_dve_lo(dve, 3, LN3_BANKS)
            dve.wait_ge(sem("ld_ds"), 16)
            for k in range(NF):
                ff_gate(dve, k)
            for tt in range(NT):
                dve.wait_ge(sem("ff_y"), tt + 1)
                nc.vector.tensor_tensor(XN[:, tt], PS[:, tt, 0:D], DS[:], ALU.mult).then_inc(sem("y_ds"), 1)
                dve.wait_ge(sem("y_ds"), tt + 1)
                nc.vector.tensor_tensor(XN[:, tt], XN[:, tt], X[:, tt], ALU.add).then_inc(sem("y"), 1)

        @block.tensor
        def _(pe):
            pe.wait_ge(sem("ident"), 3)
            for j in range(4):
                ln_pe(pe, 0, LN_BANKS, j)
            pe.wait_ge(sem("wq_lo"), 2)
            pe.wait_ge(sem("beta_lo"), 1)
            pe.wait_ge(sem("one"), 1)
            for tt in range(NT):
                pe.wait_ge(sem("ln0_lo"), tt // 2 + 1 if tt < 2 else 4)
                if tt >= 6:
                    pe.wait_ge(sem("l0_z"), tt - 5)
                if tt >= 2:
                    pe.wait_ge(sem("l0_v"), tt - 1)
                for c in range(NC):
                    mm3(qk_bank(tt), xt(c, tile(tt)), (WQH[:, c, 0:2 * D], WQL[:, c, 0:2 * D]), start=(c == 0),
                        stop=False)
                nc.tensor.matmul(qk_bank(tt), ONE[:, :], BH[:, :], start=False, stop=False)
                nc.tensor.matmul(qk_bank(tt), ONE[:, :], BL[:, :], start=False, stop=True)
                pe.wait_ge(sem("ln0_lo"), 4)
                for c in range(NC):
                    last = mm3(PS[:, tt % 2, 0:D], xt(c, tile(tt)), (WQH[:, c, 2 * D:], WQL[:, c, 2 * D:]),
                               start=(c == 0), stop=(c == NC - 1))
                last.then_inc(sem("l0_qkv"), 1)
            pe.wait_ge(sem("l0_slots"), 4)
            pe.wait_ge(sem("ones"), 2)
            pe.wait_ge(sem("l0_v"), NT)
            pe.wait_ge(sem("ot4"), 1)
            l0_stack(pe, 0, 0)
            l0_stack(pe, 0, 1)
            loop_heads4(pe, lambda h, r, **kw: pe_head(pe, h, r % 2, **kw))
            l0_av(pe, H0 - 1, 1, 3)
            pe.wait_ge(sem("l0_oev"), 4 * H0)
            for tt in range(NT):
                if tt >= 4:
                    pe.wait_ge(sem("l0_on"), tt - 3)
                for q in range(H0 // 4):
                    last = nc.tensor.transpose(PS[:, tt % 4, q * P:(q + 1) * P], OT4[:, q, tile(tt)], IDF[:, :])
                last.then_inc(sem("l0_tok"), 1)
            for j in range(4):
                pe.wait_ge(sem("l0_on"), 2 * j + 2)
                if j >= 2:
                    pe.wait_ge(sem("l0_oT"), j - 1)
                bank = PS[:, 6 + j % 2, :].rearrange("p (c t) -> p c t", c=NC)
                for i in range(2):
                    for c in range(NC):
                        last = nc.tensor.transpose(bank[:, c, i * P:(i + 1) * P],
                                                   XN[:, 2 * j + i, c * P:(c + 1) * P], IDF[:, :])
                last.then_inc(sem("l0_ot"), 1)
            pe.wait_ge(sem("ld_wo0"), 16)
            for tt in range(NT):
                pe.wait_ge(sem("l0_oT"), tt // 2 + 1)
                if tt >= 2:
                    pe.wait_ge(sem("x1"), tt - 1)
                for c in range(NC):
                    last = nc.tensor.matmul(PS[:, 4 + tt % 2, 0:D], OT0[:, c, tile(tt)], WO0[:, c, :],
                                            start=(c == 0), stop=(c == NC - 1))
                last.then_inc(sem("l0_wo"), 1)
            for j in range(4):
                ln_pe(pe, 1, LN_BANKS, j)
            pe.wait_ge(sem("wr_lo"), 1)
            for tt in range(NT):
                pe.wait_ge(sem("ln1_lo"), tt // 2 + 1)
                for c in range(NC):
                    last = mm3(PS[:, 4, tt * NR:(tt + 1) * NR], xt(c, tile(tt)), (WRH[:, c, :], WRL[:, c, :]),
                               start=(c == 0), stop=(c == NC - 1))
            last.then_inc(sem("logits"), 1)
            moe_up(pe, 0, 0)
            moe_up(pe, 1, 1)
            pe.wait_ge(sem("rt_exp"), 1)
            moe_down(pe, 0, 0)
            with pe.Fori(1, NE // 2) as i:
                moe_up(pe, 2 * i, 0)
                moe_down(pe, 2 * i - 1, 1)
                moe_up(pe, 2 * i + 1, 1)
                moe_down(pe, 2 * i, 0)
            moe_down(pe, NE - 1, 1)
            l1_products(pe)
            for j in range(4):
                if j == 0:
                    pe.wait_ge(sem("w2"), 4)
                ln_pe(pe, 2, LN2_BANKS, j)
            l1_latents(pe)
            pe.wait_ge(sem("ld_wrn"), 32)
            pe.wait_ge(sem("wn0"), 1)
            for tt in range(NT):
                l1_project(pe, tt)
                if tt:
                    l1_transpose(pe, tt - 1)
            l1_transpose(pe, NT - 1)
            pe.wait_ge(sem("k_lo"), 2)
            pe.wait_ge(sem("qk_t"), 6 * NT)

            def one(h, p, first=False, final=False):
                for tt in range(NT):
                    pe_unit(pe, h, p, tt)
            loop_heads(pe, one)
            a_transpose(pe, H1 - 1, NT - 1)
            a_values(pe, H1 - 1, NT - 2)
            a_values(pe, H1 - 1, NT - 1)
            pe.wait_ge(sem("a_on"), H1)
            o1_transpose(pe, 0)
            for tt in range(NT):
                if tt + 1 < NT:
                    o1_transpose(pe, tt + 1)
                o1_project(pe, tt)
            for j in range(4):
                ln_pe(pe, 3, LN3_BANKS, j)
            for k in range(NF):
                ff_up(pe, k)
            pe.wait_ge(sem("ff_h"), NF)
            pe.wait_ge(sem("ld_dnw"), 16)
            for tt in range(NT):
                for k in range(NF):
                    last = nc.tensor.matmul(PS[:, tt, 0:D], HT[:, k, tile(tt)], DNW[:, k, :],
                                            start=(k == 0), stop=(k == NF - 1))
                last.then_inc(sem("ff_y"), 1)


def rope_tables():
    inv = 1.0 / (np.float32(10000.0) ** (np.arange(0, DR, 2, dtype=np.float32) / np.float32(DR)))
    fr = np.outer(np.arange(T, dtype=np.float32), inv.astype(np.float32)).astype(np.float32)
    c, s = np.cos(fr), np.sin(fr)
    tab = np.stack([np.concatenate([c, c], 1), np.concatenate([-s, s], 1)]).astype(np.float32)
    return np.ascontiguousarray(tab.reshape(2, NT, P, DR).transpose(2, 0, 1, 3))


def layout(i):
    z = np.zeros
    a = {}
    a["x"] = i["L0_attn_hidden_states"][0]
    cst = z((P, 208), np.float32)
    cst[:, 0:16], cst[:, 16:32] = i["L0_attn_gamma"], i["L0_attn_beta"]
    cst[:, 32:48] = i["L0_ffn_e_bias"]
    cst[:, 48:64] = 16 - np.arange(16)
    cst[:, 80:96], cst[:, 96:112] = EPS * D0, EPS * D0
    cst[:, 64:80] = np.tril(np.ones((4, 4), np.float32), -1).reshape(16)
    a["consts"] = cst
    a["wqkv"] = np.concatenate([i["L0_attn_Wq"].T, i["L0_attn_Wk"].T, i["L0_attn_Wv"].T], 1)
    a["wo0"] = i["L0_attn_Wo"].T
    a["wr"] = i["L0_ffn_router_weight"].T
    up = np.concatenate([i["L0_ffn_shared_up"].reshape(D, NSH, MI).transpose(1, 0, 2), i["L0_ffn_w_up"]], 0)
    a["up"] = up.reshape(NE, NC, P, MI).transpose(2, 0, 1, 3)
    down = np.concatenate([i["L0_ffn_shared_down"].reshape(NSH, MI, D), i["L0_ffn_w_down"]], 0)
    a["down"] = down.transpose(1, 0, 2)
    a["wd"] = np.concatenate([i["L1_attn_wq_down"], i["L1_attn_wkv_down"]], 1)
    order = np.concatenate([np.arange(0, DR, 2), np.arange(1, DR, 2)])
    a["wqn"] = i["L1_attn_wq_nope"].reshape(QR, H1, DN).transpose(2, 1, 0)
    a["wkn"] = i["L1_attn_wk_nope"].reshape(KVR, H1, DN).transpose(2, 1, 0)
    wqr = z((2, P, H1, DR), np.float32)
    q = i["L1_attn_wq_rope"].reshape(QR, H1, DR)[:, :, order]
    wqr[0], wqr[1, :QR - P] = q[:P], q[P:]
    a["wqr"] = wqr.transpose(1, 0, 2, 3)
    wkr = z((P, H1, DR), np.float32)
    wkr[P - KVR:] = i["L1_attn_wk_rope"].reshape(KVR, H1, DR)[:, :, order]
    a["wkr"] = wkr
    wv = z((96, H1, 2, P), np.float32)
    v = i["L1_attn_wv_up"].reshape(KVR, H1, 2, 96).transpose(3, 1, 2, 0)
    wv[:, 0::2, :, 0:64], wv[:, 1::2, :, 64:128] = v[:, 0::2], v[:, 1::2]
    a["wv"] = wv
    a["wo1"] = i["L1_attn_wo"].reshape(H1, 2, 96, D).transpose(2, 0, 1, 3)
    a["rope"] = rope_tables()
    pad = NF * P
    gu = z((2, pad, D), np.float32)
    gu[0, :FI], gu[1, :FI] = i["L1_ffn_gate_w"], i["L1_ffn_up_w"]
    a["gu"] = gu.reshape(2, NF, P, NC, P).transpose(4, 1, 0, 3, 2)
    gsus = z((2, pad), np.float32)
    gsus[0, :FI], gsus[1, :FI] = i["L1_ffn_gate_s"], i["L1_ffn_up_s"]
    a["gsus"] = gsus.reshape(2, NF, P).transpose(2, 0, 1)
    dn = z((pad, D), np.float32)
    dn[:FI] = i["L1_ffn_down_w"].T
    a["dnw"] = dn.reshape(NF, P, D).transpose(1, 0, 2)
    a["ds"] = np.broadcast_to(i["L1_ffn_down_s"], (P, D))
    return {k: np.ascontiguousarray(v) for k, v in a.items()}


def program(nc, arrays, **kw):
    args = {n: nc.dram_tensor("in_" + n, list(a.shape), mybir.dt.from_np(a.dtype), kind="ExternalInput").ap()
            for n, a in arrays.items()}
    out = nc.dram_tensor("out", [T, D], F32, kind="ExternalOutput").ap()
    build(nc, out=out, **args, **kw)


def kernel(**inputs):
    import concourse.bacc as bacc
    from concourse.bass_utils import run_bass_kernel_spmd

    arrays = layout({k: np.asarray(v) for k, v in inputs.items()})
    nc = bacc.Bacc("TRN2", target_bir_lowering=False, num_devices=1)
    program(nc, arrays)
    r = run_bass_kernel_spmd(nc, [{"in_" + k: v for k, v in arrays.items()}], core_ids=[0])
    return r.results[0]["out"].reshape(1, T, D)
```

```python
import numpy as np
import concourse.bass as bass
from concourse import mybir
from contextlib import ExitStack

F32 = mybir.dt.float32
F32R = mybir.dt.float32r
BF16 = mybir.dt.bfloat16
ALU = mybir.AluOpType
ACT = mybir.ActivationFunctionType
AX = mybir.AxisListType

P = 128
T = 1024
NT = T // P
D = 256
NC = D // P
EPS = 1e-5

H0, D0 = 16, 16
SLOTS = 8

NSH = 4
NR = 16
NE = NSH + NR
MI = 128
NGRP = 4

H1 = 16
DN, DR = 128, 64
QR, KVR = 192, 64
DV = DN + DR
SCALE = 1.0 / float(DN + DR) ** 0.5
NEG = -1.0e30

FI = 704
NF = 6

KB = 1024


def build(nc, x, consts, wqkv, wo0, wr, up, down, wd, wqn, wkn, wqr, wkr, wv, wo1, rope, gu, gsus, dnw, ds, out,
          stop_after=99, dbg=None):
    ctx = ExitStack()
    with ctx:
        def place(start_kb, *tensors):
            with ExitStack() as s:
                if start_kb:
                    s.enter_context(nc.sbuf_tensor(f"pad_{tensors[0][0]}", [P, int(start_kb * KB) // 4], F32))
                return [s.enter_context(nc.sbuf_tensor(n, shape, dt)) for n, shape, dt in tensors]

        X, XN, XTH, XTL = place(0, ("X", [P, NT, D], F32), ("XN", [P, NT, D], F32),
                                ("XTH", [P, NC, T], F32R), ("XTL", [P, NC, T], F32R))
        (IDF, IDB, MASKB, CST, STAT, MV, VE, RSTD, HALF, ROPE, WRR, WRH, WRL, RT, CMB, GSUS, DS) = place(
            32, ("IDF", [P, P], F32), ("IDB", [P, P], BF16), ("MASKB", [P, P], BF16), ("CST", [P, 208], F32),
            ("STAT", [P, NT, 6], F32), ("MV", [P, NT, 2], F32), ("VE", [P, 64], F32), ("RSTD", [P, 64], F32),
            ("HALF", [P, 64], F32), ("ROPE", [P, 2, NT, DR], F32), ("WRR", [P, NC, NR], F32),
            ("WRH", [P, NC, NR], F32R), ("WRL", [P, NC, NR], F32R), ("RT", [P, 8, P], F32),
            ("CMB", [P, NT, NE], F32), ("GSUS", [P, 2, NF], F32), ("DS", [P, D], F32))
        Y, SQ, WC, WS, BETAC, BH, BL, ONE = place(
            48, ("Y", [P, NT, 2, H0, D0], F32), ("SQ", [P, 2, 2 * H0, D0], F32), ("WC", [P, NC, 2 * D], F32),
            ("WS", [P, NC * 2 * H0 + 1], F32), ("BETAC", [1, 2, D0], F32), ("BH", [1, 2 * D], F32R),
            ("BL", [1, 2 * D], F32R), ("ONE", [1, P], F32R))
        WQH, WQL, WQR = place(88, ("WQH", [P, NC, 3 * D], F32R), ("WQL", [P, NC, 3 * D], F32R),
                              ("WQR", [P, NC, 3 * D], F32))
        (WO0,) = place(106, ("WO0", [P, NC, D], F32))
        SLT, VA = place(108, ("SLT", [P, 2, NT, H0, SLOTS, D0], BF16), ("VA", [P, NT, H0, D0 + 1], F32))
        VS, SD = place(181, ("VS", [P, NT, 2, H0], F32), ("SD", [P, NT, 2, H0], F32))
        AT, VR = place(181, ("AT", [P, 2, 2304], F32), ("VR", [P, 2, NT, D0 + 1], F32))
        (OT4,) = place(16, ("OT4", [P, H0 // 4, T], F32))
        STK = place(88, ("STK", [P, 2, 2, T], BF16))[0]
        (OT0,) = place(108, ("OT0", [P, NC, T], F32))
        UP, DOWN = place(48, ("UP", [P, NE, NC, MI], F32), ("DOWN", [P, NE, D], F32))
        UPH, UPL, RELU, AH, AL, DNH, DNL = place(
            88, ("UPH", [P, 2, NC, MI], F32R), ("UPL", [P, 2, NC, MI], F32R), ("RELU", [P, 2, T // 2], F32),
            ("AH", [P, 2, T], F32R), ("AL", [P, 2, T], F32R), ("DNH", [P, 2, D], F32R), ("DNL", [P, 2, D], F32R))

        W2, WRN, WKR, WDR, WDH, WDL = place(
            109, ("W2", [P, H1 // 2, D], F32), ("WRN", [P, 2, 2 * H1 * DR], F32), ("WKR", [P, H1 * DR], F32),
            ("WDR", [P, NC, D], F32), ("WDH", [P, NC, D], F32R), ("WDL", [P, NC, D], F32R))
        WRNL, WKRL = place(117, ("WRNL", [P, 2, 2 * H1 * DR], F32R), ("WKRL", [P, H1 * DR], F32R))
        WKRH, KV = place(137, ("WKRH", [P, H1 * DR], F32R), ("KV", [P, NT, KVR], F32))
        (WRH1,) = place(24, ("WRH1", [P, 2, H1 * DR], F32R))
        LTF, UNH, UNL = place(8, ("LTF", [P, T], F32), ("UNH", [P, 2, 2, P], F32R), ("UNL", [P, 2, 2, P], F32R))
        WQN, WKN, WV, WO1 = place(143, ("WQN", [P, H1, QR], F32), ("WKN", [P, H1, KVR], F32),
                                  ("WV", [96, H1, 2, P], F32), ("WO1", [96, H1, 2, D], F32))
        (QT,) = place(45, ("QT", [P, H1, T], F32))
        (KT,) = place(175, ("KT", [P, H1 // 2, T], F32))
        LTH, LTL, QTOK, KTOK = place(143, ("LTH", [P, 2, T], F32R), ("LTL", [P, 2, T], F32R),
                                     ("QTOK", [P, 2, H1 * DR], F32), ("KTOK", [P, 2, H1 * DR], F32))
        TQ, TK = place(8, ("TQ", [P, 2, H1 * DR], F32), ("TK", [P, 2, H1 * DR], F32))
        PB, PT, NM, LS, RL, PBS = place(
            8, ("PB", [P, 2, T], F32), ("PT", [P, 4, 512], F32), ("NM", [P, H1 * NT], F32),
            ("LS", [P, H1 * NT], F32), ("RL", [P, H1 * NT], F32), ("PBS", [P, 2, T // 2], F32))
        QH, QL, KH, KL = place(143, ("QH", [P, 2, T], F32R), ("QL", [P, 2, T], F32R),
                               ("KH", [P, 2, T], F32R), ("KL", [P, 2, T], F32R))
        (OT1,) = place(143, ("OT1", [P, 2, H1 // 2, P], F32))
        GU, DNW, GUH, GUL = place(117, ("GU", [P, NF, 2 * NC, P], F32), ("DNW", [P, NF, D], F32),
                                  ("GUH", [P, 2, 2 * NC, P], F32R), ("GUL", [P, 2, 2 * NC, P], F32R))
        HT, EX = place(151, ("HT", [P, NF, T], F32), ("EX", [P, 2, T], F32))

        PS = ctx.enter_context(nc.psum_tensor("PS", [P, 8, 512], F32))

        made = {}

        def sem(name):
            if name not in made:
                made[name] = ctx.enter_context(nc.semaphore(name))
            return made[name]

        loads = {}

        def mm3(o, left, right, start=True, stop=True):
            (lh, ll), (rh, rl) = left, right
            nc.tensor.matmul(o, lh, rh, start=start, stop=False)
            nc.tensor.matmul(o, lh, rl, start=False, stop=False)
            return nc.tensor.matmul(o, ll, rh, start=False, stop=stop)

        def f(ap):
            return ap.bitcast(F32)

        GAMMA, BETA = CST[:, 0:16], CST[:, 16:32]
        EBIAS, KEY, LTRI = CST[:, 32:48], CST[:, 48:64], CST[:, 64:80]

        block = ctx.enter_context(nc.Block())

        LN_COUNTS = dict(stat=NT, var=NT, ve=NT // 2, rstd=NT // 2, xn=NT, tr=NT // 2, hi=NT // 2, lo=NT // 2)

        def ln_wait(eng, k, what, count):
            eng.wait_ge(sem("ln_" + what), LN_COUNTS[what] * k + count)

        def ln_dve_stats(dve, k, x_ready, j):
            for tt in (2 * j, 2 * j + 1):
                x_ready(tt)
                nc.vector.bn_stats(STAT[:, tt, :], X[:, tt, :]).then_inc(sem("ln_stat"), 1)
            for tt in (2 * j, 2 * j + 1):
                ln_wait(dve, k, "stat", tt + 1)
                nc.vector.bn_aggr(MV[:, tt, :], STAT[:, tt, :]).then_inc(sem("ln_var"), 1)

        def ln_pool(pool, k):
            for j in range(NT // 2):
                ln_wait(pool, k, "var", 2 * j + 2)
                g = slice(2 * j, 2 * j + 2)
                nc.gpsimd.tensor_scalar(VE[:, g], MV[:, g, 1], 1.0, EPS, ALU.mult, ALU.add).then_inc(sem("ln_ve"), 1)
                ln_wait(pool, k, "ve", j + 1)
                if k == 0 and j == 0:
                    pool.wait_ge(sem("half"), 1)
                nc.gpsimd.tensor_tensor(RSTD[:, g], VE[:, g], HALF[:, g], ALU.pow).then_inc(sem("ln_rstd"), 1)

        def ln_dve_norm(dve, k, j):
            ln_wait(dve, k, "rstd", j + 1)
            for tt in (2 * j, 2 * j + 1):
                nc.vector.tensor_scalar(XN[:, tt, :], X[:, tt, :], MV[:, tt, 0:1], RSTD[:, tt:tt + 1],
                                        ALU.subtract, ALU.mult).then_inc(sem("ln_xn"), 1)

        def ln_pe(pe, k, banks, j):
            ln_wait(pe, k, "xn", 2 * j + 2)
            if j >= 2:
                ln_wait(pe, k, "lo", j - 1)
            bank = PS[:, banks[j % 2], :].rearrange("p (c t) -> p c t", c=NC)
            for i in range(2):
                for c in range(NC):
                    last = nc.tensor.transpose(bank[:, c, i * P:(i + 1) * P],
                                               XN[:, 2 * j + i, c * P:(c + 1) * P], IDF[:, :])
            last.then_inc(sem("ln_tr"), 1)

        def ln_act(act, k, banks):
            for j in range(NT // 2):
                ln_wait(act, k, "tr", j + 1)
                bank = PS[:, banks[j % 2], :].rearrange("p (c t) -> p c t", c=NC)
                nc.scalar.copy(XTH[:, :, 256 * j:256 * j + 256], bank).then_inc(sem("ln_hi"), 1)

        def ln_dve_lo(dve, k, banks, j):
            ln_wait(dve, k, "hi", j + 1)
            bank = PS[:, banks[j % 2], :].rearrange("p (c t) -> p c t", c=NC)
            cols = slice(256 * j, 256 * j + 256)
            nc.vector.tensor_tensor(XTL[:, :, cols], bank, f(XTH[:, :, cols]), ALU.subtract)\
                .then_inc(sem("ln_lo"), 1)

        def ln_dve(dve, k, banks, x_ready):
            for j in range(NT // 2 + 2):
                if j < NT // 2:
                    ln_dve_stats(dve, k, x_ready, j)
                if 1 <= j <= NT // 2:
                    ln_dve_norm(dve, k, j - 1)
                if j >= 2:
                    ln_dve_lo(dve, k, banks, j - 2)

        def xt(c, cols):
            return XTH[:, c, cols], XTL[:, c, cols]

        def pool_wait(pool, name, value):
            pool.wait_ge(sem(name), value)
            pool.sem_inc(sem("pool_waited"), 1)

        def tile(tt):
            return slice(tt * P, (tt + 1) * P)

        def qk_bank(tt):
            return PS[:, 2 + tt % 6, :]

        BASE = [0, 1, 3, 6]
        NB = 4
        OPS, SPB = 4, (6, 7)
        LN_BANKS = (0, 1)

        def l0_scores(pe, h, p, g):
            for j in range(g + 1):
                n = BASE[g] + j
                if not (isinstance(h, int) and 10 * h + n < NB):
                    pe.wait_ge(sem("l0_sq"), 10 * h + n - NB + 1)
                for i in range(2):
                    last = nc.tensor.matmul(PS[:, (10 * p + n) % NB, 256 * i:256 * i + 256],
                                            STK[:, p, 1, tile(2 * j + i)], STK[:, p, 0, 256 * g:256 * g + 256],
                                            start=True, stop=True)
                last.then_inc(sem("l0_score"), 1)

        def l0_stack(pe, h, qk):
            if not (isinstance(h, int) and 2 * h + qk == 0):
                pe.wait_ge(sem("l0_stke"), 2 * h + qk)
            for tt in range(NT):
                last = nc.tensor.matmul(PS[:, SPB[tt // 4], (tt % 4) * P:(tt % 4 + 1) * P],
                                        SLT[:, qk, tt, bass.ds(h, 1), :, :].rearrange("p o s d -> p (o s d)"),
                                        IDB[:, :], start=True, stop=True)
            last.then_inc(sem("l0_stk"), 1)

        def l0_av(pe, h, p, g):
            pe.wait_ge(sem("l0_sq"), 10 * h + BASE[g] + g + 1)
            pe.wait_ge(sem("l0_mask"), 4 * h + g + 1)
            pe.wait_ge(sem("l0_vr"), h + 1)
            if not (isinstance(h, int) and h == 0 and g < 2):
                pe.wait_ge(sem("l0_oev"), 4 * h + g - 1)
            at = AT[:, g % 2, 0:2048].rearrange("p (s t) -> p s t", s=8)
            o = PS[0:D0 + 1, OPS + g % 2, 0:256]
            for sb in range(2 * g + 2):
                skip = P if sb == 2 * g + 1 else 0
                last = nc.tensor.matmul(o[:, skip:], VR[:, p, sb, :], at[:, sb, skip:256],
                                        start=(sb == 0), stop=(sb == 2 * g + 1))
            last.then_inc(sem("l0_av"), 1)

        def pe_head(pe, h, p, first=False, final=False):
            pe.wait_ge(sem("l0_stke"), 2 * h + 2)
            l0_scores(pe, h, p, 0)
            if not final:
                l0_stack(pe, h + 1, 0)
            if not first:
                l0_av(pe, h - 1, 1 - p, 3)
            l0_scores(pe, h, p, 1)
            l0_av(pe, h, p, 0)
            l0_scores(pe, h, p, 2)
            if not final:
                l0_stack(pe, h + 1, 1)
            l0_av(pe, h, p, 1)
            l0_scores(pe, h, p, 3)
            l0_av(pe, h, p, 2)

        def act_head(act, h, p, first=False):
            for g in range(4):
                if not (first and g < 2):
                    act.wait_ge(sem("l0_av"), 4 * h + g - 1)
                for j in range(g + 1):
                    n = BASE[g] + j
                    act.wait_ge(sem("l0_score"), 10 * h + n + 1)
                    nc.scalar.activation(AT[:, g % 2, 512 * j:512 * j + 512], PS[:, (10 * p + n) % NB, :], ACT.Square)\
                        .then_inc(sem("l0_sq"), 1)

        def pool_head(pool, h):
            for g in range(4):
                pool_wait(pool, "l0_sq", 10 * h + BASE[g] + g + 1)
                v = AT[:, g % 2, 512 * g:512 * g + 768].rearrange("p (b t) -> p b t", b=2)[:, :, 0:P]
                nc.gpsimd.affine_select(out=v, in_=v, pattern=[[0, 2], [1, P]], compare_op=ALU.is_ge, fill=0.0,
                                        base=0, channel_multiplier=-1).then_inc(sem("l0_mask"), 1)

        def dve_stack_out(dve, h, p, qk):
            dve.wait_ge(sem("l0_stk"), 2 * h + qk + 1)
            if not (isinstance(h, int) and h < 2):
                dve.wait_ge(sem("l0_score"), 10 * (h - 1))
            nc.vector.tensor_copy(STK[:, p, qk, :].rearrange("p (b t) -> p b t", b=2), PS[:, SPB[0]:SPB[1] + 1, :])\
                .then_inc(sem("l0_stke"), 1)

        def dve_values(dve, h, p):
            if not (isinstance(h, int) and h < 2):
                dve.wait_ge(sem("l0_av"), 4 * (h - 1))
            nc.vector.tensor_copy(VR[:, p], VA[:, :, bass.ds(h, 1), :].rearrange("p t o e -> p t (o e)"))\
                .then_inc(sem("l0_vr"), 1)

        def dve_out(dve, h, r, g):
            dve.wait_ge(sem("l0_av"), 4 * h + g + 1)
            dst = OT4[32 * r:32 * r + D0 + 1, :, :].rearrange("p q t -> p (q t)")
            nc.vector.tensor_copy(dst[:, bass.ds((h - r) * (T // 4) + 256 * g, 256)], PS[0:D0 + 1, OPS + g % 2, 0:256])\
                .then_inc(sem("l0_oev"), 1)

        def dve_head(dve, h, r, first=False, final=False):
            if not final:
                dve_stack_out(dve, h + 1, 1 - r % 2, 0)
            if not first:
                dve_out(dve, h - 1, (r - 1) % 4, 3)
            if not final:
                dve_values(dve, h + 1, 1 - r % 2)
            dve_out(dve, h, r, 0)
            if not final:
                dve_stack_out(dve, h + 1, 1 - r % 2, 1)
            dve_out(dve, h, r, 1)
            dve_out(dve, h, r, 2)

        def loop_heads4(eng, one):
            one(0, 0, first=True)
            with eng.Fori(0, (H0 - 4) // 4) as i:
                for r in (1, 2, 3):
                    one(4 * i + r, r)
                one(4 * i + 4, 0)
            one(H0 - 3, 1)
            one(H0 - 2, 2)
            one(H0 - 1, 3, final=True)

        def loop_heads(eng, one):
            one(0, 0, first=True)
            with eng.Fori(0, H0 // 2 - 1) as i:
                one(2 * i + 1, 1)
                one(2 * i + 2, 0)
            one(H0 - 1, 1, final=True)

        def moe_split(pool, e, p):
            if not (isinstance(e, int) and e < 2):
                pool_wait(pool, "m_up", 2 * e - 2)
            src = UP[:, bass.ds(e, 1), :, :].rearrange("p o c i -> p (o c) i")
            nc.gpsimd.tensor_copy(UPH[:, p], src).then_inc(sem("m_hi"), 1)
            pool_wait(pool, "m_hi", 2 * e + 1)
            nc.gpsimd.tensor_tensor(UPL[:, p], src, f(UPH[:, p]), ALU.subtract).then_inc(sem("m_split"), 1)
            if not (isinstance(e, int) and e < 2):
                pool_wait(pool, "m_dn", 4 * e - 4)
            src = DOWN[:, bass.ds(e, 1), :].rearrange("p o d -> p (o d)")
            nc.gpsimd.tensor_copy(DNH[:, p], src).then_inc(sem("m_hi"), 1)
            pool_wait(pool, "m_hi", 2 * e + 2)
            nc.gpsimd.tensor_tensor(DNL[:, p], src, f(DNH[:, p]), ALU.subtract).then_inc(sem("m_dsplit"), 1)

        def moe_up(pe, e, p):
            pe.wait_ge(sem("m_split"), e + 1)
            for n in range(2):
                if not (isinstance(e, int) and e < 2):
                    pe.wait_ge(sem("m_relu"), 2 * (e - 2) + n + 1)
                for c in range(NC):
                    last = mm3(PS[:, 2 * p + n, :], (UPH[:, p, c, :], UPL[:, p, c, :]),
                               xt(c, slice(512 * n, 512 * n + 512)), start=(c == 0), stop=(c == NC - 1))
                last.then_inc(sem("m_up"), 1)

        def moe_down(pe, e, p):
            for b in range(4):
                if b == 0:
                    pe.wait_ge(sem("m_dsplit"), e + 1)
                if b % 2 == 0:
                    pe.wait_ge(sem("m_al"), 2 * e + b // 2 + 1)
                if not (isinstance(e, int) and e < 1):
                    pe.wait_ge(sem("m_acc"), 8 * (e - 1) + 2 * b + 2)
                for i in range(2):
                    last = mm3(PS[:, 4 + b, 256 * i:256 * i + 256], (AH[:, p, tile(2 * b + i)], AL[:, p, tile(2 * b + i)]),
                               (DNH[:, p, :], DNL[:, p, :]))
                last.then_inc(sem("m_dn"), 1)

        def moe_act(act, e, p):
            for n in range(2):
                act.wait_ge(sem("m_up"), 2 * e + n + 1)
                if not (isinstance(e, int) and e < 1):
                    act.wait_ge(sem("m_al"), 2 * e - 1 + n)
                nc.scalar.activation(RELU[:, n, :], PS[:, 2 * p + n, :], ACT.Relu).then_inc(sem("m_relu"), 1)
                act.wait_ge(sem("m_relu"), 2 * e + n + 1)
                if not (isinstance(e, int) and e < 2):
                    act.wait_ge(sem("m_dn"), 4 * e - 4)
                nc.scalar.activation(AH[:, p, 512 * n:512 * n + 512], RELU[:, n, :], ACT.Square).then_inc(sem("m_ah"), 1)
                act.wait_ge(sem("m_ah"), 2 * e + n + 1)
                nc.scalar.activation(RELU[:, n, :], RELU[:, n, :], ACT.Square).then_inc(sem("m_sq"), 1)

        def moe_lo(dve, e, p):
            for n in range(2):
                dve.wait_ge(sem("m_sq"), 2 * e + n + 1)
                nc.vector.tensor_tensor(AL[:, p, 512 * n:512 * n + 512], RELU[:, n, :],
                                        f(AH[:, p, 512 * n:512 * n + 512]), ALU.subtract).then_inc(sem("m_al"), 1)

        def moe_acc_bank(dve, e, b):
            dve.wait_ge(sem("m_dn"), 4 * e + b + 1)
            for i in range(2):
                tt = 2 * b + i
                if not (isinstance(e, int) and e < 1):
                    dve.wait_ge(sem("m_acc"), 8 * (e - 1) + tt + 1)
                nc.vector.scalar_tensor_tensor(
                    out=X[:, tt, :], in0=PS[:, 4 + b, 256 * i:256 * i + 256],
                    scalar=CMB[:, tt, bass.ds(e, 1)], in1=X[:, tt, :], op0=ALU.mult, op1=ALU.add)\
                    .then_inc(sem("m_acc"), 1)

        def moe_acc(dve, e):
            for b in range(4):
                moe_acc_bank(dve, e, b)

        def grab(bank, n, rows=slice(0, P)):
            return PS[rows, bank, 0:n]

        def l1_products(pe):
            pe.wait_ge(sem("ld_prod"), 64)
            for half in range(2):
                for m, (r0, r1) in enumerate(((0, P), (P, QR))):
                    bank = 2 * m + half
                    for i in range(8):
                        last = nc.tensor.matmul(PS[0:r1 - r0, bank, 64 * (i ^ 1):64 * (i ^ 1) + 64], WQN[:, 8 * half + i, r0:r1],
                                                WKN[:, 8 * half + i, :], start=True, stop=True)
                last.then_inc(sem("p_wn"), 1)
            pe.wait_ge(sem("m_acc"), 8 * NE)
            for q in range(H1 // 2):
                for i in range(4):
                    last = nc.tensor.matmul(PS[:, 4 + q // 2, 256 * (q % 2):256 * (q % 2) + 256],
                                            WV[:, 2 * q + i // 2, i % 2, :], WO1[:, 2 * q + i // 2, i % 2, :],
                                            start=(i == 0), stop=(i == 3))
                if q % 2:
                    last.then_inc(sem("p_w2"), 1)

        def l1_products_out(act):
            for half in range(2):
                act.wait_ge(sem("p_wn"), half + 1)
                cols = slice(H1 * DR + 512 * half, H1 * DR + 512 * half + 512)
                nc.scalar.copy(WRN[:, 0, cols], PS[:, half, :]).then_inc(sem("wn"), 1)
                nc.scalar.copy(WRN[0:QR - P, 1, cols], PS[0:QR - P, 2 + half, :]).then_inc(sem("wn"), 1)
            for b in range(4):
                act.wait_ge(sem("p_w2"), b + 1)
                nc.scalar.copy(W2[:, 2 * b:2 * b + 2, :], PS[:, 4 + b, :].rearrange("p (q d) -> p q d", q=2))\
                    .then_inc(sem("w2"), 1)

        LN2_BANKS = (6, 7)

        KVROWS, QROWS = slice(P - KVR, P), slice(0, QR - P)

        def l1_latents(pe):
            pe.wait_ge(sem("wd_lo"), 1)
            pe.wait_ge(sem("wn"), 4)
            for n in range(2):
                ln_wait(pe, 2, "lo", 2 * n + 2)
                for m in range(2):
                    for c in range(NC):
                        last = mm3(PS[:, 2 * m + n, :], (WDH[:, c, tile(m)], WDL[:, c, tile(m)]),
                                   xt(c, slice(512 * n, 512 * n + 512)), start=(c == 0), stop=(c == NC - 1))
                    last.then_inc(sem("lat"), 1)

        def l1_latents_act(act):
            for n in range(2):
                for m in range(2):
                    act.wait_ge(sem("lat"), 2 * n + m + 1)
                    cols = slice(512 * n, 512 * n + 512)
                    if m == 1:
                        nc.scalar.copy(LTF[KVROWS, cols], PS[KVROWS, 2 + n, :]).then_inc(sem("ltf"), 1)
                    nc.scalar.copy(LTH[:, m, cols], PS[:, 2 * m + n, :]).then_inc(sem("lth"), 1)
            nc.scalar.copy(WRH1[:], WRN[:, :, 0:H1 * DR]).then_inc(sem("rw_hi"), 1)
            nc.scalar.copy(WKRH[KVROWS], WKR[KVROWS]).then_inc(sem("rw_hi"), 1)
            act.wait_ge(sem("kv_tr"), 1)
            nc.scalar.copy(KV[:], PS[:, 0, :].rearrange("p (t d) -> p t d", t=NT)).then_inc(sem("kv"), 1)

        def l1_latents_dve(dve):
            for n in range(2):
                for m in range(2):
                    dve.wait_ge(sem("lth"), 2 * n + m + 1)
                    cols = slice(512 * n, 512 * n + 512)
                    nc.vector.tensor_tensor(LTL[:, m, cols], PS[:, 2 * m + n, :], f(LTH[:, m, cols]), ALU.subtract)\
                        .then_inc(sem("ltl"), 1)
            dve.wait_ge(sem("rw_hi"), 2)
            nc.vector.tensor_tensor(WRNL[:, :, 0:H1 * DR], WRN[:, :, 0:H1 * DR], f(WRH1[:]), ALU.subtract)\
                .then_inc(sem("rw_lo"), 1)
            nc.vector.tensor_tensor(WKRL[KVROWS], WKR[KVROWS], f(WKRH[KVROWS]), ALU.subtract).then_inc(sem("rw_lo"), 1)

        def l1_kv(pe):
            pe.wait_ge(sem("ltf"), 2)
            pe.wait_ge(sem("ltl"), 4)
            for tt in range(NT):
                last = nc.tensor.transpose(PS[:, 0, tt * KVR:(tt + 1) * KVR], LTF[KVROWS, tile(tt)],
                                           IDF[KVROWS, KVROWS])
            last.then_inc(sem("kv_tr"), 1)

        def un_split(pool, q):
            pool.wait_ge(sem("wn"), 4)
            if q >= 2:
                pool.wait_ge(sem("un"), q - 1)
            src = WRN[:, :, H1 * DR + P * q:H1 * DR + P * (q + 1)]
            for kt, rows in ((0, slice(0, P)), (1, QROWS)):
                nc.gpsimd.tensor_copy(UNH[rows, q % 2, kt], src[rows, kt]).then_inc(sem("un_hi"), 1)
                pool.wait_ge(sem("un_hi"), 2 * q + kt + 1)
                nc.gpsimd.tensor_tensor(UNL[rows, q % 2, kt], src[rows, kt], f(UNH[rows, q % 2, kt]), ALU.subtract)\
                    .then_inc(sem("un_w"), 1)
                pool.wait_ge(sem("un_w"), 2 * q + kt + 1)

        def un_banks(q):
            b = 4 + 2 * (q % 2)
            return PS[:, b:b + 2, :]

        def l1_unrotated(pe, q):
            pe.wait_ge(sem("un_w"), 2 * q + 2)
            if q >= 2:
                pe.wait_ge(sem("un_oa" if q % 2 == 0 else "un_od"), 2 * (q // 2))
            for n in range(2):
                cols = slice(512 * n, 512 * n + 512)
                for kt, rows in ((0, slice(0, P)), (1, QROWS)):
                    last = mm3(un_banks(q)[:, n, :], (UNH[rows, q % 2, kt], UNL[rows, q % 2, kt]),
                               (LTH[rows, kt, cols], LTL[rows, kt, cols]), start=(kt == 0), stop=(kt == 1))
            last.then_inc(sem("un"), 1)

        def l1_unrotated_out(eng, q):
            eng.wait_ge(sem("un"), q + 1)
            for h, rows in ((2 * q + 1, slice(0, DR)), (2 * q, slice(DR, P))):
                src, dst = un_banks(q)[rows].rearrange("p b n -> p (b n)"), QT[rows, h, :]
                if q % 2 == 0:
                    nc.scalar.activation(dst, src, ACT.Copy, scale=SCALE).then_inc(sem("un_oa"), 1)
                else:
                    nc.vector.tensor_scalar(dst, src, SCALE, None, ALU.mult).then_inc(sem("un_od"), 1)

        def l1_project(pe, tt):
            if tt:
                pe.wait_ge(sem("q_rot"), 3 * tt)
            for b in range(2):
                cols = slice(512 * b, 512 * b + 512)
                for kt, rows in ((0, slice(0, P)), (1, QROWS)):
                    last = mm3(PS[:, b, :], (LTH[rows, kt, tile(tt)], LTL[rows, kt, tile(tt)]),
                               (WRH1[rows, kt, cols], WRNL[rows, kt, cols]), start=(kt == 0), stop=(kt == 1))
            last.then_inc(sem("proj"), 1)
            if tt:
                pe.wait_ge(sem("k_rot"), 3 * tt)
            for b in range(2):
                cols = slice(512 * b, 512 * b + 512)
                last = mm3(PS[:, 2 + b, :], (LTH[KVROWS, 1, tile(tt)], LTL[KVROWS, 1, tile(tt)]),
                           (WKRH[KVROWS, cols], WKRL[KVROWS, cols]))
            last.then_inc(sem("proj"), 1)

        def l1_rotate(dve, tt):
            co = ROPE[:, 0, tt, :].unsqueeze(1).to_broadcast([P, H1, DR])
            h = DR // 2
            for name, bank, buf, ready in (("q_rot", 0, TQ, 2 * tt + 1), ("k_rot", 2, TK, 2 * tt + 2)):
                dve.wait_ge(sem("proj"), ready)
                if tt:
                    dve.wait_ge(sem(name[0] + "_sum"), tt)
                src = PS[:, bank:bank + 2, :].rearrange("p b (h d) -> p (b h) d", d=DR)
                a, b = (buf[:, i, :].rearrange("p (h d) -> p h d", d=DR) for i in range(2))
                nc.vector.tensor_tensor(a, src, co, ALU.mult).then_inc(sem(name), 1)
                for j in range(2):
                    si = ROPE[:, 1, tt, j * h:(j + 1) * h].unsqueeze(1).to_broadcast([P, H1, h])
                    nc.vector.tensor_tensor(b[:, :, j * h:(j + 1) * h], src[:, :, (1 - j) * h:(2 - j) * h], si,
                                            ALU.mult).then_inc(sem(name), 1)

        def l1_sums(pool, tt):
            for name, buf, dst in (("q", TQ, QTOK), ("k", TK, KTOK)):
                pool.wait_ge(sem(name + "_rot"), 3 * tt + 3)
                if tt >= 2:
                    pool.wait_ge(sem(name + "_tr"), 2 * (tt - 1))
                nc.gpsimd.tensor_tensor(dst[:, tt % 2, :], buf[:, 0, :], buf[:, 1, :], ALU.add)\
                    .then_inc(sem(name + "_sum"), 1)

        def l1_transpose(pe, tt):
            for g in range(4):
                name, src = ("q", QTOK) if g < 2 else ("k", KTOK)
                n = 4 * tt + g
                if g % 2 == 0:
                    pe.wait_ge(sem(name + "_sum"), tt + 1)
                if n >= 2:
                    pe.wait_ge(sem("qk_t"), n - 1)
                for i in range(4):
                    col = (4 * (g % 2) + i) * P
                    last = nc.tensor.transpose(PS[:, 6 + g % 2, i * P:(i + 1) * P], src[:, tt % 2, col:col + P], IDF[:, :])
                last.then_inc(sem(name + "_tr"), 1)

        def l1_transposed(act, tt):
            for g in range(4):
                src = PS[:, 6 + g % 2, :].rearrange("p (q t) -> p q t", q=4)
                if g < 2:
                    act.wait_ge(sem("q_tr"), 2 * tt + g + 1)
                    for e, rows in ((0, slice(0, DR)), (1, slice(DR, P))):
                        dst = QT[rows, 8 * g:8 * g + 8, tile(tt)].rearrange("p (q e) t -> p q e t", e=2)[:, :, e]
                        last = nc.scalar.activation(dst, src[rows], ACT.Copy, scale=SCALE)
                        last.then_inc(sem("qk_q"), 1)
                    act.wait_ge(sem("qk_q"), 4 * tt + 2 * g + 2)
                    act.sem_inc(sem("qk_t"), 1)
                else:
                    act.wait_ge(sem("k_tr"), 2 * tt + g - 1)
                    nc.scalar.copy(KT[:, 4 * (g - 2):4 * (g - 2) + 4, tile(tt)], src).then_inc(sem("qk_t"), 1)

        ORDER = (7, 0, 6, 1, 5, 2, 4, 3)
        GROUPS = 12
        S_SMALL, PT_BANKS, O_BANK = 4, 5, 7

        def group(i, b):
            return 3 * (i // 2) + (b if i % 2 == 0 else 2)

        def by_act(n):
            return n % 3 == 1

        def unit_of(n):
            return 2 * (n // 3) + (n % 3) // 2

        def back(h, n, k, total):
            if n - k >= 0:
                return h, n - k
            return None if isinstance(h, int) and h == 0 else (h - 1, n - k + total)

        def wait_group(eng, h, n):
            done = sum(by_act(m) == by_act(n) for m in range(n + 1))
            if by_act(n):
                eng.wait_ge(sem("a_pa"), 4 * h + done)
            else:
                eng.wait_ge(sem("a_pd"), 8 * h + done)

        def s_view(i):
            keys = (ORDER[i] + 1) * P
            if i % 2:
                return PS[:, S_SMALL, 0:keys]
            b = i % 4
            return PS[:, b:b + 2, :].rearrange("p b n -> p (b n)")[:, 0:keys]

        def p_view(i):
            keys = (ORDER[i] + 1) * P
            return (PBS if i % 2 else PB)[:, i // 2 % 2, 0:keys]

        def a_scores(pe, h, p, i):
            if i == 0:
                pe.wait_ge(sem("a_hi"), 2 * h + 2)
                pe.wait_ge(sem("a_lo"), 2 * h + 2)
            if prev := back(h, i, 2 if i % 2 else 4, NT):
                pe.wait_ge(sem("a_p"), 8 * prev[0] + prev[1] + 1)
            s, keys, tt = s_view(i), (ORDER[i] + 1) * P, ORDER[i]
            for n0 in range(0, keys, 512):
                n1 = min(keys, n0 + 512)
                o = s[:, n0:n1]
                nc.tensor.matmul(o, QH[:, p, tile(tt)], KH[:, p, n0:n1], start=True, stop=False)
                nc.tensor.matmul(o, QH[:, p, tile(tt)], KL[:, p, n0:n1], start=False, stop=False)
                if n1 == keys:
                    nc.tensor.matmul(o[:, n1 - n0 - P:n1 - n0], IDB[:, :], MASKB[:, :], start=False, stop=False)
                last = nc.tensor.matmul(o, QL[:, p, tile(tt)], KH[:, p, n0:n1], start=False, stop=True)
            last.then_inc(sem("a_s"), 1)

        def a_transpose(pe, h, i):
            pe.wait_ge(sem("a_p"), 8 * h + i + 1)
            tt, w = ORDER[i], p_view(i)
            for b in range(1 + tt // 4):
                n = group(i, b)
                if prev := back(h, n, 2, GROUPS):
                    wait_group(pe, *prev)
                for sb in range(4 * b, min(tt + 1, 4 * b + 4)):
                    last = nc.tensor.transpose(PS[:, PT_BANKS + n % 2, tile(sb % 4)], w[:, tile(sb)], IDF[:, :])
                last.then_inc(sem("a_t"), 1)

        def a_values(pe, h, i):
            if prev := back(h, i, 1, NT):
                pe.wait_ge(sem("a_n"), 8 * prev[0] + prev[1] + 1)
            tt = ORDER[i]
            for sb in range(tt + 1):
                n = group(i, sb // 4)
                if sb % 4 == 0:
                    wait_group(pe, h, n)
                last = nc.tensor.matmul(PS[:, O_BANK, 0:KVR], PT[:, n % 4, tile(sb % 4)], KV[:, sb, :],
                                        start=(sb == 0), stop=(sb == tt))
            last.then_inc(sem("a_o"), 1)

        def a_group_out(eng, h, i, b):
            n = group(i, b)
            width = (min(ORDER[i] + 1, 4 * b + 4) - 4 * b) * P
            eng.wait_ge(sem("a_t"), GROUPS * h + n + 1)
            if prev := back(h, n, 4, GROUPS):
                eng.wait_ge(sem("a_o"), 8 * prev[0] + unit_of(prev[1]) + 1)
            copy = nc.scalar.copy if by_act(n) else nc.vector.tensor_copy
            copy(PT[:, n % 4, 0:width], PS[:, PT_BANKS + n % 2, 0:width]).then_inc(sem("a_pa" if by_act(n) else "a_pd"), 1)

        def behind(h, p, i, k):
            if u := back(h, i, k, NT):
                return u[0], u[1], p if i >= k else 1 - p

        def pe_unit(pe, h, p, i):
            turned, summed = behind(h, p, i, 3), behind(h, p, i, 4)
            a_scores(pe, h, p, i)
            if turned:
                a_transpose(pe, *turned[:2])
            if summed:
                a_values(pe, *summed[:2])

        def ring_rows(p):
            return slice(0, DR) if p == 0 else slice(DR, P)

        def key_rows(h, p):
            return KT[ring_rows(p), :, :].rearrange("p q t -> p (q t)")[:, bass.ds((h - p) * (T // 2), T)]

        def a_hi(act, h, p, what):
            if not (isinstance(h, int) and h < 2):
                act.wait_ge(sem("a_s"), 8 * (h - 1))
            if what == 0:
                nc.scalar.copy(QH[:, p, :], QT[:, bass.ds(h, 1), :].rearrange("p o t -> p (o t)"))\
                    .then_inc(sem("a_hi"), 1)
            else:
                r = ring_rows(p)
                nc.scalar.copy(KH[r, p, :], key_rows(h, p))\
                    .then_inc(sem("a_hi"), 1)

        def a_lo(pool, h, p):
            r = ring_rows(p)
            pool_wait(pool, "a_hi", 2 * h + 1)
            nc.gpsimd.tensor_tensor(QL[:, p, :], QT[:, bass.ds(h, 1), :].rearrange("p o t -> p (o t)"),
                                    f(QH[:, p, :]), ALU.subtract).then_inc(sem("a_lo"), 1)
            pool.wait_ge(sem("a_hi"), 2 * h + 2)
            pool_wait(pool, "a_lo", 2 * h + 1)
            nc.gpsimd.tensor_tensor(KL[r, p, :], key_rows(h, p), f(KH[r, p, :]), ALU.subtract).then_inc(sem("a_lo"), 1)
            pool_wait(pool, "a_lo", 2 * h + 2)

        def a_exp(act, h, i):
            act.wait_ge(sem("a_m"), 8 * h + i + 1)
            if prev := back(h, i, 4, NT):
                act.wait_ge(sem("a_t"), GROUPS * prev[0] + group(prev[1], 1) + 1)
            col = bass.ds(8 * h + ORDER[i], 1)
            nc.scalar.activation(p_view(i), s_view(i), ACT.Exp, bias=NM[:, col], accum_out=LS[:, col])\
                .then_inc(sem("a_p"), 1)

        def act_unit(act, h, p, i, final=False):
            turned = behind(h, p, i, 3)
            a_exp(act, h, i)
            if turned and i % 2:
                a_group_out(act, *turned[:2], 1)
            if not final and i in (1, 3):
                a_hi(act, h + 1, 1 - p, i // 2)

        def a_max(dve, h, i):
            dve.wait_ge(sem("a_s"), 8 * h + i + 1)
            nc.vector.tensor_reduce(NM[:, bass.ds(8 * h + ORDER[i], 1)], s_view(i), axis=AX.X, op=ALU.max, negate=True)\
                .then_inc(sem("a_m"), 1)

        def a_out(dve, h, i, p):
            dve.wait_ge(sem("a_o"), 8 * h + i + 1)
            c = ORDER[i] * P + p * KVR
            nc.vector.tensor_copy(QT[:, bass.ds(h - p, 1), c:c + KVR].rearrange("p o d -> p (o d)"),
                                  PS[:, O_BANK, 0:KVR]).then_inc(sem("a_n"), 1)

        def dve_unit(dve, h, p, i):
            turned, summed = behind(h, p, i, 3), behind(h, p, i, 4)
            a_max(dve, h, i)
            if turned:
                a_group_out(dve, *turned[:2], 0)
            if summed:
                a_out(dve, *summed)

        def a_weights_sum(dve, h):
            dve.wait_ge(sem("a_p"), 8 * h + 8)
            nc.vector.reciprocal(RL[:, bass.ds(8 * h, NT)], LS[:, bass.ds(8 * h, NT)]).then_inc(sem("a_rl"), 1)

        def a_normalise(pool, h, p):
            pool_wait(pool, "a_rl", h + 1)
            pool_wait(pool, "a_n", 8 * h + 8)
            o = QT[:, bass.ds(h - p, 1), :].rearrange("p o (t d) -> p (o t) d", d=P)[:, :, p * KVR:(p + 1) * KVR]
            nc.gpsimd.tensor_tensor(o, o, RL[:, bass.ds(8 * h, NT)].unsqueeze(2).to_broadcast([P, NT, KVR]),
                                    ALU.mult).then_inc(sem("a_on"), 1)

        def o1_banks(tt):
            return (0, 1) if tt % 2 == 0 else (4, 5)

        def o1_transpose(pe, tt):
            if tt >= 2:
                pe.wait_ge(sem("o1_ta"), tt - 1)
                pe.wait_ge(sem("o1_td"), tt - 1)
            for q in range(H1 // 2):
                last = nc.tensor.transpose(PS[:, o1_banks(tt)[q // 4], tile(q % 4)],
                                           QT[:, 2 * q, tile(tt)], IDF[:, :])
                if q % 4 == 3:
                    last.then_inc(sem("o1_tr"), 1)

        def o1_project(pe, tt):
            pe.wait_ge(sem("o1_ta"), tt + 1)
            pe.wait_ge(sem("o1_td"), tt + 1)
            if tt >= 2:
                pe.wait_ge(sem("x3"), tt - 1)
            for q in range(H1 // 2):
                last = nc.tensor.matmul(PS[:, 2 + tt % 2, 0:D], OT1[:, tt % 2, q, :], W2[:, q, :],
                                        start=(q == 0), stop=(q == H1 // 2 - 1))
            last.then_inc(sem("o1"), 1)

        def o1_out(eng, tt, half):
            eng.wait_ge(sem("o1_tr"), 2 * tt + half + 1)
            if tt >= 2:
                eng.wait_ge(sem("o1"), tt - 1)
            copy = nc.scalar.copy if half == 0 else nc.vector.tensor_copy
            copy(OT1[:, tt % 2, 4 * half:4 * half + 4, :],
                 PS[:, o1_banks(tt)[half], :].rearrange("p (q t) -> p q t", q=4))\
                .then_inc(sem("o1_ta" if half == 0 else "o1_td"), 1)

        LN3_BANKS = (6, 7)

        def ff_split(pool, k):
            if k >= 2:
                pool.wait_ge(sem("ff_gu"), k - 1)
            nc.gpsimd.tensor_copy(GUH[:, k % 2], GU[:, k]).then_inc(sem("ff_hi"), 1)
            pool.wait_ge(sem("ff_hi"), k + 1)
            nc.gpsimd.tensor_tensor(GUL[:, k % 2], GU[:, k], f(GUH[:, k % 2]), ALU.subtract).then_inc(sem("ff_w"), 1)

        def ff_up(pe, k):
            pe.wait_ge(sem("ff_w"), k + 1)
            if k >= 2:
                pe.wait_ge(sem("ff_h"), k - 1)
            for j in range(2):
                for n in range(2):
                    if k == 0:
                        ln_wait(pe, 3, "lo", 2 * n + 2)
                    for c in range(NC):
                        last = mm3(PS[:, 4 * (k % 2) + 2 * j + n, :],
                                   (GUH[:, k % 2, NC * j + c, :], GUL[:, k % 2, NC * j + c, :]),
                                   xt(c, slice(512 * n, 512 * n + 512)), start=(c == 0), stop=(c == NC - 1))
            last.then_inc(sem("ff_gu"), 1)

        def gu_banks(k, j):
            b = 4 * (k % 2) + 2 * j
            return PS[:, b:b + 2, :].rearrange("p b n -> p (b n)")

        def ff_act(act, k):
            act.wait_ge(sem("ff_gu"), k + 1)
            if k >= 2:
                act.wait_ge(sem("ff_h"), k - 1)
            nc.scalar.activation(EX[:, k % 2, :], gu_banks(k, 0), ACT.Silu, scale=GSUS[:, 0, k:k + 1])\
                .then_inc(sem("ff_ex"), 1)

        def ff_gate(dve, k):
            dve.wait_ge(sem("ff_ex"), k + 1)
            nc.vector.scalar_tensor_tensor(out=HT[:, k, :], in0=gu_banks(k, 1), scalar=GSUS[:, 1, k:k + 1],
                                           in1=EX[:, k % 2, :], op0=ALU.mult, op1=ALU.mult).then_inc(sem("ff_h"), 1)

        def router(dve, between):
            count = [0]

            def step(ins):
                count[0] += 1
                ins.then_inc(sem("rt"), 1)
                if count[0] in between:
                    between[count[0]]()
                dve.wait_ge(sem("rt"), count[0])

            def r3(i):
                return RT[:, i, :].rearrange("p (t e) -> p t e", t=NT)
            sc, s, ms = r3(1), r3(2), r3(3)
            V = nc.vector
            dve.wait_ge(sem("rt_tok"), 1)
            step(V.tensor_scalar(RT[:, 1, :], PS[:, 6, 0:P], 1.0, None, ALU.add))
            step(V.reciprocal(sc, sc))
            step(V.tensor_tensor(s, sc, EBIAS.unsqueeze(1).to_broadcast([P, NT, NR]), ALU.add))
            s4 = RT[:, 2, :].rearrange("p (g a b) -> p g a b", a=2, b=2)
            hi = RT[:, 4, 0:64].rearrange("p (g a) -> p g a", a=2)
            lo = RT[:, 4, 64:128].rearrange("p (g a) -> p g a", a=2)
            V.tensor_tensor(hi, s4[:, :, :, 0], s4[:, :, :, 1], ALU.max)
            step(V.tensor_tensor(lo, s4[:, :, :, 0], s4[:, :, :, 1], ALU.min))
            t1, t2, t3, gs = (RT[:, 5, 32 * k:32 * k + 32] for k in range(4))
            V.tensor_tensor(t1, hi[:, :, 0], hi[:, :, 1], ALU.max)
            V.tensor_tensor(t2, hi[:, :, 0], hi[:, :, 1], ALU.min)
            step(V.tensor_tensor(t3, lo[:, :, 0], lo[:, :, 1], ALU.max))
            step(V.tensor_tensor(t2, t2, t3, ALU.max))
            step(V.tensor_tensor(gs, t1, t2, ALU.add))
            g3 = gs.rearrange("p (t g) -> p t g", g=NGRP)
            other = g3.unsqueeze(2).to_broadcast([P, NT, NGRP, NGRP])
            own = g3.unsqueeze(3).to_broadcast([P, NT, NGRP, NGRP])
            gt = RT[:, 6, :].rearrange("p (t g o) -> p t g o", t=NT, g=NGRP)
            eq = RT[:, 7, :].rearrange("p (t g o) -> p t g o", t=NT, g=NGRP)
            V.tensor_tensor(gt, other, own, ALU.is_gt)
            step(V.tensor_tensor(eq, other, own, ALU.is_equal))
            tri = LTRI.unsqueeze(1).to_broadcast([P, NT, NR])
            step(V.tensor_tensor(RT[:, 7, :].rearrange("p (t e) -> p t e", t=NT),
                                 RT[:, 7, :].rearrange("p (t e) -> p t e", t=NT), tri, ALU.mult))
            step(V.tensor_tensor(RT[:, 6, :], RT[:, 6, :], RT[:, 7, :], ALU.add))
            step(V.reduce_sum(t1, RT[:, 6, :].rearrange("p (g o) -> p g o", o=NGRP), axis=AX.X))
            step(V.tensor_scalar(t1, t1, 1.5, None, ALU.is_lt))
            step(V.tensor_tensor(RT[:, 3, :].rearrange("p (g o) -> p g o", o=4),
                                 RT[:, 2, :].rearrange("p (g o) -> p g o", o=4),
                                 t1.unsqueeze(2).to_broadcast([P, 32, 4]), ALU.mult))
            key = KEY.unsqueeze(1).to_broadcast([P, NT, NR])
            m = RT[:, 4, 0:NT]
            sel = [r3(6), r3(7)]
            for n in range(2):
                step(V.reduce_max(m, ms, axis=AX.X))
                step(V.tensor_tensor(sel[n], ms, m.unsqueeze(2).to_broadcast([P, NT, NR]), ALU.is_equal))
                step(V.tensor_tensor(sel[n], sel[n], key, ALU.mult))
                step(V.reduce_max(m, sel[n], axis=AX.X))
                step(V.tensor_tensor(sel[n], sel[n], m.unsqueeze(2).to_broadcast([P, NT, NR]), ALU.is_equal))
                if n == 0:
                    step(V.scalar_tensor_tensor(out=ms, in0=sel[0], scalar=NEG, in1=ms, op0=ALU.mult, op1=ALU.add))
            step(V.tensor_tensor(sel[0], sel[0], sel[1], ALU.add))
            step(V.tensor_tensor(sc, sc, sel[0], ALU.mult))
            step(V.reduce_sum(m, sc, axis=AX.X))
            step(V.tensor_scalar(m, m, 1e-20, None, ALU.add))
            step(V.reciprocal(m, m))
            step(V.tensor_tensor(CMB[:, :, NSH:NE], sc, m.unsqueeze(2).to_broadcast([P, NT, NR]), ALU.mult))

        @block.sync
        def _(sp):
            def load(name, dst, src):
                sp.dma_start(dst, src).then_inc(sem("ld_" + name), 16)
            for j in range(2):
                load("x", X[:, 4 * j:4 * j + 4, :], x.rearrange("(t p) d -> p t d", p=P)[:, 4 * j:4 * j + 4, :])
            load("wq", WQR[:], wqkv.rearrange("(c p) n -> p c n", p=P))
            load("cst", CST[:], consts)
            load("wo0", WO0[:], wo0.rearrange("(c p) n -> p c n", p=P))
            load("wr", WRR[:], wr.rearrange("(c p) n -> p c n", p=P))
            load("gsus", GSUS[:], gsus)
            load("ds", DS[:], ds)
            load("rope", ROPE[:], rope)
            sp.wait_ge(sem("l0_slots"), 4)
            load("up", UP[:], up)
            load("down", DOWN[:], down)
            sp.wait_ge(sem("x1"), NT)
            load("prod", WQN[:], wqn)
            load("prod", WKN[:], wkn)
            load("prod", WV[:], wv)
            load("prod", WO1[:], wo1)
            load("wrn", WRN[:, :, 0:H1 * DR], wqr.rearrange("p k h d -> p k (h d)"))
            load("wrn", WKR[:], wkr.rearrange("p h d -> p (h d)"))
            load("wd", WDR[:], wd.rearrange("(c p) n -> p c n", p=P))
            sp.wait_ge(sem("proj"), 2 * NT)
            load("gu", GU[:], gu.rearrange("p f j c i -> p f (j c) i"))
            load("dnw", DNW[:], dnw)
            for tt in range(NT):
                sp.wait_ge(sem("y"), tt + 1)
                sp.dma_start(out[tile(tt), :], XN[:, tt, :]).then_inc(sem("stored"), 16)
            sp.wait_ge(sem("stored"), 16 * NT)

        @block.gpsimd
        def _(pool):
            nc.gpsimd.memset(HALF[:], -0.5).then_inc(sem("half"), 1)
            nc.gpsimd.memset(IDF[:], 0.0).then_inc(sem("cst0"), 1)
            nc.gpsimd.memset(IDB[:], 0.0).then_inc(sem("cst0"), 1)
            nc.gpsimd.memset(MASKB[:], 0.0).then_inc(sem("cst0"), 1)
            nc.gpsimd.memset(VA[:, :, :, D0:D0 + 1], 1.0).then_inc(sem("ones"), 1)
            nc.gpsimd.memset(f(ONE[:]), 1.0).then_inc(sem("one"), 1)
            nc.gpsimd.memset(CMB[:, :, 0:NSH], 1.0).then_inc(sem("ones"), 1)
            pool.wait_ge(sem("cst0"), 3)
            for m in (IDF, IDB):
                nc.gpsimd.affine_select(out=m[:], in_=m[:], pattern=[[-1, P]], compare_op=ALU.not_equal, fill=1.0,
                                        base=0, channel_multiplier=1).then_inc(sem("ident"), 1)
            nc.gpsimd.affine_select(out=MASKB[:], in_=MASKB[:], pattern=[[-1, P]], compare_op=ALU.is_ge, fill=NEG,
                                    base=0, channel_multiplier=1).then_inc(sem("ident"), 1)
            ln_pool(pool, 0)
            pool.wait_ge(sem("l0_qkv"), NT)
            nc.gpsimd.memset(OT4[:], 0.0).then_inc(sem("ot4"), 1)
            for g in range(4):
                pool.wait_ge(sem("l0_p1"), 2 * g + 2)
                for qk in range(2):
                    z = Y[:, 2 * g:2 * g + 2, qk]
                    nc.gpsimd.tensor_tensor(z, z, SLT[:, qk, 2 * g:2 * g + 2, :, 0, :], ALU.subtract)\
                        .then_inc(sem("l0_r1"), 1)
            loop_heads4(pool, lambda h, r, **kw: pool_head(pool, h))
            ln_pool(pool, 1)
            pool.wait_ge(sem("ld_up"), 16)
            pool.wait_ge(sem("ld_down"), 16)
            pool.wait_ge(sem("x1"), NT)
            moe_split(pool, 0, 0)
            moe_split(pool, 1, 1)
            with pool.Fori(1, NE // 2) as i:
                moe_split(pool, 2 * i, 0)
                moe_split(pool, 2 * i + 1, 1)
            pool.wait_ge(sem("m_dsplit"), NE)
            ln_pool(pool, 2)
            ln_wait(pool, 2, "tr", 4)
            for q in range(H1 // 2):
                un_split(pool, q)
            for tt in range(NT):
                l1_sums(pool, tt)
            pool.wait_ge(sem("k_lo"), 2)

            def one(h, p, first=False, final=False):
                if not final:
                    a_lo(pool, h + 1, 1 - p)
                if not first:
                    a_normalise(pool, h - 1, 1 - p)
            loop_heads(pool, one)
            a_normalise(pool, H1 - 1, 1)
            ln_pool(pool, 3)
            pool.wait_ge(sem("ld_gu"), 16)
            for k in range(NF):
                ff_split(pool, k)

        @block.scalar
        def _(act):
            act.wait_ge(sem("ld_wq"), 16)
            nc.scalar.copy(WQH[:, :, 2 * D:], WQR[:, :, 2 * D:]).then_inc(sem("wq_hi"), 1)
            act.wait_ge(sem("wc"), 3)
            nc.scalar.copy(WQH[:, :, 0:2 * D], WC[:]).then_inc(sem("wq_hi"), 1)
            act.wait_ge(sem("betac"), 3)
            nc.scalar.copy(BH[:], BETAC[:].unsqueeze(1).to_broadcast([1, H0, 2, D0])).then_inc(sem("beta_hi"), 1)
            act.wait_ge(sem("ld_wr"), 16)
            nc.scalar.copy(WRH[:], WRR[:]).then_inc(sem("wr_hi"), 1)
            ln_act(act, 0, LN_BANKS)
            for tt in range(NT):
                act.wait_ge(sem("l0_qkv"), tt + 1)
                if tt >= 2:
                    act.wait_ge(sem("l0_vs"), tt - 1)
                nc.scalar.activation(SQ[:, tt % 2], qk_bank(tt).rearrange("p (n d) -> p n d", d=D0), ACT.Square)\
                    .then_inc(sem("l0_csq"), 1)
                nc.scalar.copy(VA[:, tt, :, 0:D0], PS[:, tt % 2, 0:D].rearrange("p (h d) -> p h d", h=H0))\
                    .then_inc(sem("l0_v"), 1)
                if tt % 2:
                    r = slice(tt - 1, tt + 1)
                    act.wait_ge(sem("l0_vs"), tt + 1)
                    nc.scalar.activation(SD[:, r, 0, :], VS[:, r, 0, :], ACT.Sqrt, scale=1.0).then_inc(sem("l0_sd"), 1)
                    nc.scalar.activation(SD[:, r, 1, :], VS[:, r, 1, :], ACT.Sqrt, scale=1.0 / D0)\
                        .then_inc(sem("l0_sd"), 1)
            for g in range(4):
                act.wait_ge(sem("l0_z"), 2 * g + 2)
                for qk in range(2):
                    nc.scalar.copy(SLT[:, qk, 2 * g:2 * g + 2, :, 0, :], Y[:, 2 * g:2 * g + 2, qk]).then_inc(sem("l0_p1"), 1)
            for g in range(4):
                act.wait_ge(sem("l0_r1"), 2 * g + 2)
                for qk, s in ((0, 1), (1, 3)):
                    nc.scalar.copy(SLT[:, qk, 2 * g:2 * g + 2, :, s, :], Y[:, 2 * g:2 * g + 2, qk]).then_inc(sem("l0_p2"), 1)
            loop_heads4(act, lambda h, r, first=False, **kw: act_head(act, h, r % 2, first))
            for j in range(4):
                act.wait_ge(sem("l0_ot"), j + 1)
                bank = PS[:, 6 + j % 2, :].rearrange("p (c t) -> p c t", c=NC)
                nc.scalar.copy(OT0[:, :, 256 * j:256 * j + 256], bank).then_inc(sem("l0_oT"), 1)
            ln_act(act, 1, LN_BANKS)
            act.wait_ge(sem("logits"), 1)
            nc.scalar.activation(RT[0:NR].rearrange("p a b -> p (a b)"), PS[0:NR, 4:6, :].rearrange("p b n -> p (b n)"),
                                 ACT.Exp, scale=-1.0).then_inc(sem("rt_exp"), 1)
            moe_act(act, 0, 0)
            moe_act(act, 1, 1)
            with act.Fori(1, NE // 2) as i:
                moe_act(act, 2 * i, 0)
                moe_act(act, 2 * i + 1, 1)
            act.wait_ge(sem("ld_wd"), 16)
            nc.scalar.copy(WDH[:], WDR[:]).then_inc(sem("wd_hi"), 1)
            l1_products_out(act)
            ln_act(act, 2, LN2_BANKS)
            act.wait_ge(sem("ld_wrn"), 32)
            l1_latents_act(act)
            for q in range(0, H1 // 2, 2):
                l1_unrotated_out(act, q)
            for tt in range(NT - 1):
                l1_transposed(act, tt)
            act.wait_ge(sem("q_tr"), 2 * NT - 2)
            nc.scalar.copy(KH[KVROWS, 0, :], f(LTH[KVROWS, 1, :])).then_inc(sem("k_hi"), 1)
            l1_transposed(act, NT - 1)
            act.wait_ge(sem("qk_t"), 4 * NT)
            a_hi(act, 0, 0, 0)
            a_hi(act, 0, 0, 1)
            nc.scalar.copy(KH[0:KVR, 1, :], f(LTH[KVROWS, 1, :])).then_inc(sem("k_hi"), 1)
            act.wait_ge(sem("k_hi"), 2)

            def one(h, p, first=False, final=False):
                for i in range(NT):
                    act_unit(act, h, p, i, final)
            loop_heads(act, one)
            a_group_out(act, H1 - 1, NT - 2, 1)
            for tt in range(NT):
                o1_out(act, tt, 0)
            ln_act(act, 3, LN3_BANKS)
            act.wait_ge(sem("ld_gsus"), 16)
            for k in range(NF):
                ff_act(act, k)

        @block.vector
        def _(dve):
            def x_loaded(tt):
                if tt % 4 == 0:
                    dve.wait_ge(sem("ld_x"), 32)
            dve.wait_ge(sem("ld_wq"), 16)
            dve.wait_ge(sem("ld_cst"), 16)
            wc = WC[:].rearrange("p c (n d) -> p c n d", d=D0)
            ws = WS[:, 0:NC * 2 * H0].rearrange("p (c n) -> p c n", c=NC)
            nc.vector.tensor_tensor(wc, WQR[:, :, 0:2 * D].rearrange("p c (n d) -> p c n d", d=D0),
                                    GAMMA.unsqueeze(1).unsqueeze(1).to_broadcast([P, NC, 2 * H0, D0]), ALU.mult)\
                .then_inc(sem("wc"), 1)
            nc.vector.reduce_sum(WS[0:1, NC * 2 * H0:NC * 2 * H0 + 1], BETA[0:1, :], axis=AX.X).then_inc(sem("betac"), 1)
            dve.wait_ge(sem("wc"), 1)
            nc.vector.reduce_sum(ws, wc, axis=AX.X).then_inc(sem("wc"), 1)
            dve.wait_ge(sem("betac"), 1)
            for q in range(2):
                nc.vector.scalar_tensor_tensor(
                    out=BETAC[:, q, :], in0=WS[0:1, NC * 2 * H0:NC * 2 * H0 + 1].to_broadcast([1, D0]),
                    scalar=-1.0 / D0, in1=BETA[0:1, :], op0=ALU.mult, op1=ALU.add).then_inc(sem("betac"), 1)
            dve.wait_ge(sem("wc"), 2)
            nc.vector.scalar_tensor_tensor(out=wc, in0=ws.unsqueeze(3).to_broadcast([P, NC, 2 * H0, D0]),
                                           scalar=-1.0 / D0, in1=wc, op0=ALU.mult, op1=ALU.add).then_inc(sem("wc"), 1)
            for j in range(NT // 2):
                ln_dve_stats(dve, 0, x_loaded, j)
            for j in range(NT // 2):
                ln_dve_norm(dve, 0, j)
            dve.wait_ge(sem("wq_hi"), 2)
            nc.vector.tensor_tensor(WQL[:, :, 0:2 * D], WC[:], f(WQH[:, :, 0:2 * D]), ALU.subtract).then_inc(sem("wq_lo"), 1)
            nc.vector.tensor_tensor(WQL[:, :, 2 * D:], WQR[:, :, 2 * D:], f(WQH[:, :, 2 * D:]), ALU.subtract)\
                .then_inc(sem("wq_lo"), 1)
            dve.wait_ge(sem("beta_hi"), 1)
            nc.vector.tensor_tensor(BL[:].rearrange("p (h q d) -> p h q d", q=2, d=D0),
                                    BETAC[:].unsqueeze(1).to_broadcast([1, H0, 2, D0]),
                                    f(BH[:]).rearrange("p (h q d) -> p h q d", q=2, d=D0), ALU.subtract)\
                .then_inc(sem("beta_lo"), 1)
            dve.wait_ge(sem("wr_hi"), 1)
            nc.vector.tensor_tensor(WRL[:], WRR[:], f(WRH[:]), ALU.subtract).then_inc(sem("wr_lo"), 1)
            for j in range(NT // 2):
                ln_dve_lo(dve, 0, LN_BANKS, j)
            for j in range(4):
                for tt in (2 * j, 2 * j + 1):
                    dve.wait_ge(sem("l0_csq"), tt + 1)
                    nc.vector.reduce_sum(VS[:, tt], SQ[:, tt % 2], axis=AX.X).then_inc(sem("l0_vr0"), 1)
                    dve.wait_ge(sem("l0_vr0"), tt + 1)
                    nc.vector.tensor_tensor(VS[:, tt], VS[:, tt], CST[:, 80:112].rearrange("p (q h) -> p q h", q=2),
                                            ALU.add).then_inc(sem("l0_vs"), 1)
                r = slice(2 * j, 2 * j + 2)
                dve.wait_ge(sem("l0_sd"), 2 * j + 2)
                nc.vector.reciprocal(SD[:, r], SD[:, r]).then_inc(sem("l0_rs"), 1)
                dve.wait_ge(sem("l0_rs"), j + 1)
                for tt in (2 * j, 2 * j + 1):
                    nc.vector.tensor_tensor(Y[:, tt].rearrange("p q h d -> p (q h) d"),
                                            qk_bank(tt).rearrange("p (n d) -> p n d", d=D0),
                                            SD[:, tt].rearrange("p q h -> p (q h)").unsqueeze(2)
                                            .to_broadcast([P, 2 * H0, D0]), ALU.mult).then_inc(sem("l0_z"), 1)
            for g in range(4):
                r = slice(2 * g, 2 * g + 2)
                dve.wait_ge(sem("l0_p2"), 2 * g + 2)
                nc.vector.tensor_tensor(SLT[:, 0, r, :, 2, :], Y[:, r, 0], SLT[:, 0, r, :, 1, :], ALU.subtract)\
                    .then_inc(sem("l0_p3"), 1)
                nc.vector.tensor_tensor(SLT[:, 1, r, :, 6, :], Y[:, r, 1], SLT[:, 1, r, :, 3, :], ALU.subtract)\
                    .then_inc(sem("l0_p3"), 1)

                def th(a):
                    return a.rearrange("p t h s d -> p (t h) s d")
                q, k = SLT[:, 0, r], SLT[:, 1, r]
                nc.vector.tensor_copy(th(k[:, :, :, 1:3]), th(k[:, :, :, 0:1]).to_broadcast([P, 32, 2, D0]))
                nc.vector.tensor_copy(th(k[:, :, :, 4:6]), th(k[:, :, :, 3:4]).to_broadcast([P, 32, 2, D0]))
                nc.vector.tensor_copy(th(q[:, :, :, 6:8]), th(q[:, :, :, 0:2]))
                dve.wait_ge(sem("l0_p3"), 2 * g + 2)
                nc.vector.tensor_copy(th(k[:, :, :, 7:8]), th(k[:, :, :, 6:7]))
                nc.vector.tensor_copy(th(q[:, :, :, 3:6]), th(q[:, :, :, 0:3])).then_inc(sem("l0_slots"), 1)
            dve_stack_out(dve, 0, 0, 0)
            dve_stack_out(dve, 0, 0, 1)
            dve_values(dve, 0, 0)
            loop_heads4(dve, lambda h, r, **kw: dve_head(dve, h, r, **kw))
            dve_out(dve, H0 - 1, 3, 3)
            for b in range(2):
                dve.wait_ge(sem("l0_tok"), 4 * b + 4)
                o = PS[:, 0:4, :].rearrange("p b (h e) -> p b h e", h=H0)
                z = RT[:, 4 * b:4 * b + 4, 0:H0]
                nc.vector.tensor_scalar(z, o[:, :, :, D0], EPS, None, ALU.add).then_inc(sem("l0_z1"), 1)
                dve.wait_ge(sem("l0_z1"), b + 1)
                nc.vector.reciprocal(z, z).then_inc(sem("l0_z2"), 1)
                dve.wait_ge(sem("l0_z2"), b + 1)
                for i in range(4):
                    nc.vector.tensor_tensor(XN[:, 4 * b + i].rearrange("p (h d) -> p h d", h=H0), o[:, i, :, 0:D0],
                                            z[:, i].unsqueeze(2).to_broadcast([P, H0, D0]), ALU.mult)\
                        .then_inc(sem("l0_on"), 1)

            def x1(tt):
                dve.wait_ge(sem("l0_wo"), tt + 1)
                nc.vector.tensor_tensor(X[:, tt], PS[:, 4 + tt % 2, 0:D], X[:, tt], ALU.add).then_inc(sem("x1"), 1)
                dve.wait_ge(sem("x1"), tt + 1)
            ln_dve(dve, 1, LN_BANKS, x1)
            between = {1: lambda: moe_lo(dve, 0, 0), 5: lambda: moe_lo(dve, 1, 1), 13: lambda: moe_lo(dve, 2, 0),
                       21: lambda: moe_lo(dve, 3, 1)}
            for e in range(NSH - 1):
                for b in range(4):
                    between[8 * e + 8 + b] = lambda e=e, b=b: moe_acc_bank(dve, e, b)
            router(dve, between)
            dve.wait_ge(sem("ones"), 2)

            def experts(i):
                moe_lo(dve, 2 * i, 0)
                moe_acc(dve, 2 * i - 1)
                moe_lo(dve, 2 * i + 1, 1)
                moe_acc(dve, 2 * i)
            experts(NSH // 2)
            with dve.Fori(NSH // 2 + 1, NE // 2) as i:
                experts(i)
            dve.wait_ge(sem("wd_hi"), 1)
            nc.vector.tensor_tensor(WDL[:], WDR[:], f(WDH[:]), ALU.subtract).then_inc(sem("wd_lo"), 1)

            def x2(tt):
                if tt % 2 == 0:
                    moe_acc_bank(dve, NE - 1, tt // 2)
                dve.wait_ge(sem("m_acc"), 8 * NE - NT + tt + 1)
            for j in range(NT // 2):
                ln_dve_stats(dve, 2, x2, j)
            for j in range(NT // 2):
                ln_dve_norm(dve, 2, j)
            for j in range(NT // 2):
                ln_dve_lo(dve, 2, LN2_BANKS, j)
            dve.wait_ge(sem("ld_wrn"), 32)
            l1_latents_dve(dve)
            for q in range(1, H1 // 2, 2):
                l1_unrotated_out(dve, q)
            dve.wait_ge(sem("ld_rope"), 16)
            for tt in range(NT):
                l1_rotate(dve, tt)
            dve.wait_ge(sem("k_tr"), 2 * NT - 2)
            nc.vector.tensor_copy(KL[KVROWS, 0, :], f(LTL[KVROWS, 1, :])).then_inc(sem("k_lo"), 1)
            dve.wait_ge(sem("proj"), 2 * NT)
            dve.wait_ge(sem("a_hi"), 1)
            nc.vector.tensor_tensor(QL[:, 0, :], QT[:, 0, :], f(QH[:, 0, :]), ALU.subtract).then_inc(sem("a_lo"), 1)
            dve.wait_ge(sem("a_hi"), 2)
            nc.vector.tensor_tensor(KL[0:DR, 0, :], KT[0:DR, 0, :],
                                    f(KH[0:DR, 0, :]), ALU.subtract).then_inc(sem("a_lo"), 1)
            dve.wait_ge(sem("k_tr"), 2 * NT)
            nc.vector.tensor_copy(KL[0:KVR, 1, :], f(LTL[KVROWS, 1, :])).then_inc(sem("k_lo"), 1)

            def one(h, p, first=False, final=False):
                for i in range(NT):
                    dve_unit(dve, h, p, i)
                    if i == 2 and not first:
                        a_weights_sum(dve, h - 1)
            loop_heads(dve, one)
            for i in range(NT - 3, NT):
                a_group_out(dve, H1 - 1, i, 0)
                a_out(dve, H1 - 1, i - 1, 1)
            a_out(dve, H1 - 1, NT - 1, 1)
            a_weights_sum(dve, H1 - 1)
            o1_out(dve, 0, 1)

            def x3(tt):
                if tt + 1 < NT:
                    o1_out(dve, tt + 1, 1)
                dve.wait_ge(sem("o1"), tt + 1)
                nc.vector.tensor_tensor(X[:, tt], PS[:, 2 + tt % 2, 0:D], X[:, tt], ALU.add).then_inc(sem("x3"), 1)
                dve.wait_ge(sem("x3"), tt + 1)
            ln_dve(dve, 3, LN3_BANKS, x3)
            dve.wait_ge(sem("ld_ds"), 16)
            for k in range(NF):
                ff_gate(dve, k)
            for tt in range(NT):
                dve.wait_ge(sem("ff_y"), tt + 1)
                nc.vector.tensor_tensor(XN[:, tt], PS[:, tt, 0:D], DS[:], ALU.mult).then_inc(sem("y_ds"), 1)
                dve.wait_ge(sem("y_ds"), tt + 1)
                nc.vector.tensor_tensor(XN[:, tt], XN[:, tt], X[:, tt], ALU.add).then_inc(sem("y"), 1)

        @block.tensor
        def _(pe):
            pe.wait_ge(sem("ident"), 3)
            for j in range(4):
                ln_pe(pe, 0, LN_BANKS, j)
            pe.wait_ge(sem("wq_lo"), 2)
            pe.wait_ge(sem("beta_lo"), 1)
            pe.wait_ge(sem("one"), 1)
            for tt in range(NT):
                ln_wait(pe, 0, "lo", tt // 2 + 1 if tt < 2 else 4)
                if tt >= 6:
                    pe.wait_ge(sem("l0_z"), tt - 5)
                if tt >= 2:
                    pe.wait_ge(sem("l0_v"), tt - 1)
                for c in range(NC):
                    mm3(qk_bank(tt), xt(c, tile(tt)), (WQH[:, c, 0:2 * D], WQL[:, c, 0:2 * D]), start=(c == 0),
                        stop=False)
                nc.tensor.matmul(qk_bank(tt), ONE[:, :], BH[:, :], start=False, stop=False)
                nc.tensor.matmul(qk_bank(tt), ONE[:, :], BL[:, :], start=False, stop=True)
                ln_wait(pe, 0, "lo", 4)
                for c in range(NC):
                    last = mm3(PS[:, tt % 2, 0:D], xt(c, tile(tt)), (WQH[:, c, 2 * D:], WQL[:, c, 2 * D:]),
                               start=(c == 0), stop=(c == NC - 1))
                last.then_inc(sem("l0_qkv"), 1)
            pe.wait_ge(sem("l0_slots"), 4)
            pe.wait_ge(sem("ones"), 2)
            pe.wait_ge(sem("l0_v"), NT)
            pe.wait_ge(sem("ot4"), 1)
            l0_stack(pe, 0, 0)
            l0_stack(pe, 0, 1)
            loop_heads4(pe, lambda h, r, **kw: pe_head(pe, h, r % 2, **kw))
            l0_av(pe, H0 - 1, 1, 3)
            pe.wait_ge(sem("l0_oev"), 4 * H0)
            for tt in range(NT):
                if tt >= 4:
                    pe.wait_ge(sem("l0_on"), tt - 3)
                for q in range(H0 // 4):
                    last = nc.tensor.transpose(PS[:, tt % 4, q * P:(q + 1) * P], OT4[:, q, tile(tt)], IDF[:, :])
                last.then_inc(sem("l0_tok"), 1)
            for j in range(4):
                pe.wait_ge(sem("l0_on"), 2 * j + 2)
                if j >= 2:
                    pe.wait_ge(sem("l0_oT"), j - 1)
                bank = PS[:, 6 + j % 2, :].rearrange("p (c t) -> p c t", c=NC)
                for i in range(2):
                    for c in range(NC):
                        last = nc.tensor.transpose(bank[:, c, i * P:(i + 1) * P],
                                                   XN[:, 2 * j + i, c * P:(c + 1) * P], IDF[:, :])
                last.then_inc(sem("l0_ot"), 1)
            pe.wait_ge(sem("ld_wo0"), 16)
            for tt in range(NT):
                pe.wait_ge(sem("l0_oT"), tt // 2 + 1)
                if tt >= 2:
                    pe.wait_ge(sem("x1"), tt - 1)
                for c in range(NC):
                    last = nc.tensor.matmul(PS[:, 4 + tt % 2, 0:D], OT0[:, c, tile(tt)], WO0[:, c, :],
                                            start=(c == 0), stop=(c == NC - 1))
                last.then_inc(sem("l0_wo"), 1)
                if tt in (5, 7):
                    ln_pe(pe, 1, LN_BANKS, (tt - 5) // 2)
            ln_pe(pe, 1, LN_BANKS, 2)
            ln_pe(pe, 1, LN_BANKS, 3)
            pe.wait_ge(sem("wr_lo"), 1)
            pe.wait_ge(sem("x1"), NT)
            for n in range(2):
                ln_wait(pe, 1, "lo", 2 * n + 2)
                for c in range(NC):
                    last = mm3(PS[0:NR, 4 + n, :], (WRH[:, c, :], WRL[:, c, :]), xt(c, slice(512 * n, 512 * n + 512)),
                               start=(c == 0), stop=(c == NC - 1))
            last.then_inc(sem("logits"), 1)
            moe_up(pe, 0, 0)
            pe.wait_ge(sem("rt_exp"), 1)
            for tt in range(NT):
                last = nc.tensor.transpose(PS[:, 6, tt * NR:(tt + 1) * NR], RT[0:NR, tt, :], IDF[0:NR, 0:NR])
            last.then_inc(sem("rt_tok"), 1)
            moe_up(pe, 1, 1)
            pe.wait_ge(sem("rt"), 1)
            moe_down(pe, 0, 0)

            def experts(i):
                moe_up(pe, 2 * i, 0)
                moe_down(pe, 2 * i - 1, 1)
                moe_up(pe, 2 * i + 1, 1)
                moe_down(pe, 2 * i, 0)
            experts(1)
            experts(NSH // 2)
            with pe.Fori(NSH // 2 + 1, NE // 2) as i:
                experts(i)
            moe_down(pe, NE - 1, 1)
            l1_products(pe)
            for j in range(4):
                if j == 0:
                    pe.wait_ge(sem("w2"), 4)
                ln_pe(pe, 2, LN2_BANKS, j)
            l1_latents(pe)
            pe.wait_ge(sem("ltl"), 4)
            l1_unrotated(pe, 0)
            l1_unrotated(pe, 1)
            l1_kv(pe)
            for q in range(2, H1 // 2):
                l1_unrotated(pe, q)
            pe.wait_ge(sem("rw_lo"), 2)
            pe.wait_ge(sem("kv"), 1)
            for tt in range(NT):
                l1_project(pe, tt)
                if tt == 0:
                    pe.wait_ge(sem("un_od"), H1 // 2)
                else:
                    l1_transpose(pe, tt - 1)
            l1_transpose(pe, NT - 1)
            pe.wait_ge(sem("k_lo"), 1)
            pe.wait_ge(sem("k_hi"), 1)
            pe.wait_ge(sem("qk_t"), 4 * NT)

            def one(h, p, first=False, final=False):
                for i in range(NT):
                    pe_unit(pe, h, p, i)
                if first:
                    pe.wait_ge(sem("k_lo"), 2)
                    pe.wait_ge(sem("k_hi"), 2)
            loop_heads(pe, one)
            for i in range(NT - 3, NT):
                a_transpose(pe, H1 - 1, i)
                a_values(pe, H1 - 1, i - 1)
            a_values(pe, H1 - 1, NT - 1)
            pe.wait_ge(sem("a_on"), H1)
            o1_transpose(pe, 0)
            for tt in range(NT):
                if tt + 1 < NT:
                    o1_transpose(pe, tt + 1)
                o1_project(pe, tt)
                if tt in (5, 7):
                    ln_pe(pe, 3, LN3_BANKS, (tt - 5) // 2)
            ln_pe(pe, 3, LN3_BANKS, 2)
            ln_pe(pe, 3, LN3_BANKS, 3)
            for k in range(NF):
                ff_up(pe, k)
            pe.wait_ge(sem("ff_h"), NF)
            pe.wait_ge(sem("ld_dnw"), 16)
            for tt in range(NT):
                for k in range(NF):
                    last = nc.tensor.matmul(PS[:, tt, 0:D], HT[:, k, tile(tt)], DNW[:, k, :],
                                            start=(k == 0), stop=(k == NF - 1))
                last.then_inc(sem("ff_y"), 1)


def rope_tables():
    inv = 1.0 / (np.float32(10000.0) ** (np.arange(0, DR, 2, dtype=np.float32) / np.float32(DR)))
    fr = np.outer(np.arange(T, dtype=np.float32), inv.astype(np.float32)).astype(np.float32)
    c, s = np.cos(fr), np.sin(fr)
    tab = np.stack([np.concatenate([c, c], 1), np.concatenate([-s, s], 1)]).astype(np.float32)
    return np.ascontiguousarray(tab.reshape(2, NT, P, DR).transpose(2, 0, 1, 3))


def layout(i):
    z = np.zeros
    a = {}
    a["x"] = i["L0_attn_hidden_states"][0]
    cst = z((P, 208), np.float32)
    cst[:, 0:16], cst[:, 16:32] = i["L0_attn_gamma"], i["L0_attn_beta"]
    cst[:, 32:48] = i["L0_ffn_e_bias"]
    cst[:, 48:64] = 16 - np.arange(16)
    cst[:, 80:96], cst[:, 96:112] = EPS * D0, EPS * D0
    cst[:, 64:80] = np.tril(np.ones((4, 4), np.float32), -1).reshape(16)
    a["consts"] = cst
    a["wqkv"] = np.concatenate([i["L0_attn_Wq"].T, i["L0_attn_Wk"].T, i["L0_attn_Wv"].T], 1)
    a["wo0"] = i["L0_attn_Wo"].T
    a["wr"] = i["L0_ffn_router_weight"].T
    up = np.concatenate([i["L0_ffn_shared_up"].reshape(D, NSH, MI).transpose(1, 0, 2), i["L0_ffn_w_up"]], 0)
    a["up"] = up.reshape(NE, NC, P, MI).transpose(2, 0, 1, 3)
    down = np.concatenate([i["L0_ffn_shared_down"].reshape(NSH, MI, D), i["L0_ffn_w_down"]], 0)
    a["down"] = down.transpose(1, 0, 2)
    a["wd"] = np.concatenate([i["L1_attn_wq_down"], i["L1_attn_wkv_down"]], 1)
    order = np.concatenate([np.arange(0, DR, 2), np.arange(1, DR, 2)])
    a["wqn"] = i["L1_attn_wq_nope"].reshape(QR, H1, DN).transpose(2, 1, 0)
    a["wkn"] = i["L1_attn_wk_nope"].reshape(KVR, H1, DN).transpose(2, 1, 0)
    wqr = z((2, P, H1, DR), np.float32)
    q = i["L1_attn_wq_rope"].reshape(QR, H1, DR)[:, :, order]
    wqr[0], wqr[1, :QR - P] = q[:P], q[P:]
    a["wqr"] = wqr.transpose(1, 0, 2, 3)
    wkr = z((P, H1, DR), np.float32)
    wkr[P - KVR:] = i["L1_attn_wk_rope"].reshape(KVR, H1, DR)[:, :, order]
    a["wkr"] = wkr
    wv = z((96, H1, 2, P), np.float32)
    v = i["L1_attn_wv_up"].reshape(KVR, H1, 2, 96).transpose(3, 1, 2, 0)
    wv[:, 0::2, :, 0:64], wv[:, 1::2, :, 64:128] = v[:, 0::2], v[:, 1::2]
    a["wv"] = wv
    a["wo1"] = i["L1_attn_wo"].reshape(H1, 2, 96, D).transpose(2, 0, 1, 3)
    a["rope"] = rope_tables()
    pad = NF * P
    gu = z((2, pad, D), np.float32)
    gu[0, :FI], gu[1, :FI] = i["L1_ffn_gate_w"], i["L1_ffn_up_w"]
    a["gu"] = gu.reshape(2, NF, P, NC, P).transpose(4, 1, 0, 3, 2)
    gsus = z((2, pad), np.float32)
    gsus[0, :FI], gsus[1, :FI] = i["L1_ffn_gate_s"], i["L1_ffn_up_s"]
    a["gsus"] = gsus.reshape(2, NF, P).transpose(2, 0, 1)
    dn = z((pad, D), np.float32)
    dn[:FI] = i["L1_ffn_down_w"].T
    a["dnw"] = dn.reshape(NF, P, D).transpose(1, 0, 2)
    a["ds"] = np.broadcast_to(i["L1_ffn_down_s"], (P, D))
    return {k: np.ascontiguousarray(v) for k, v in a.items()}


def program(nc, arrays, **kw):
    args = {n: nc.dram_tensor("in_" + n, list(a.shape), mybir.dt.from_np(a.dtype), kind="ExternalInput").ap()
            for n, a in arrays.items()}
    out = nc.dram_tensor("out", [T, D], F32, kind="ExternalOutput").ap()
    build(nc, out=out, **args, **kw)


def kernel(**inputs):
    import concourse.bacc as bacc
    from concourse.bass_utils import run_bass_kernel_spmd

    arrays = layout({k: np.asarray(v) for k, v in inputs.items()})
    nc = bacc.Bacc("TRN2", target_bir_lowering=False, num_devices=1)
    program(nc, arrays)
    r = run_bass_kernel_spmd(nc, [{"in_" + k: v for k, v in arrays.items()}], core_ids=[0])
    return r.results[0]["out"].reshape(1, T, D)
```

```python
import numpy as np
import concourse.bass as bass
from concourse import mybir
from contextlib import ExitStack

F32 = mybir.dt.float32
F32R = mybir.dt.float32r
BF16 = mybir.dt.bfloat16
ALU = mybir.AluOpType
ACT = mybir.ActivationFunctionType
AX = mybir.AxisListType

P = 128
T = 1024
NT = T // P
D = 256
NC = D // P
EPS = 1e-5

H0, D0 = 16, 16
SLOTS = 8

NSH = 4
NR = 16
NE = NSH + NR
MI = 128
NGRP = 4

H1 = 16
DN, DR = 128, 64
QR, KVR = 192, 64
DV = DN + DR
SCALE = 1.0 / float(DN + DR) ** 0.5
NEG = -1.0e30

FI = 704
NF = 6
LAST = FI - (NF - 1) * 128

KB = 1024


def build(nc, x, consts, wqkv, wo0, wr, up, down, wd, wqn, wkn, wqr, wkr, wv, wo1, rope, gu, gsus, dnw, ds, out,
          stop_after=99, dbg=None):
    ctx = ExitStack()
    with ctx:
        def place(start_kb, *tensors):
            with ExitStack() as s:
                if start_kb:
                    s.enter_context(nc.sbuf_tensor(f"pad_{tensors[0][0]}", [P, int(start_kb * KB) // 4], F32))
                return [s.enter_context(nc.sbuf_tensor(n, shape, dt)) for n, shape, dt in tensors]

        X, XN, XTH, XTL = place(0, ("X", [P, NT, D], F32), ("XN", [P, NT, D], F32),
                                ("XTH", [P, NC, T], F32R), ("XTL", [P, NC, T], F32R))
        (IDF, IDB, MASKB, CST, STAT, MV, VE, RSTD, HALF, SHIFT, ROPE, WRR, WRH, WRL, RT, CMB, GSUS, DS) = place(
            32, ("IDF", [P, P], F32), ("IDB", [P, P], BF16), ("MASKB", [P, P], BF16), ("CST", [P, 208], F32),
            ("STAT", [P, NT, 6], F32), ("MV", [P, NT, 2], F32), ("VE", [P, 64], F32), ("RSTD", [P, 64], F32),
            ("HALF", [P, 56], F32), ("SHIFT", [P, NT], F32), ("ROPE", [P, 2, NT, DR], F32), ("WRR", [P, NC, NR], F32),
            ("WRH", [P, NC, NR], F32R), ("WRL", [P, NC, NR], F32R), ("RT", [P, 8, P], F32),
            ("CMB", [P, NT, NE], F32), ("GSUS", [P, 2, NF], F32), ("DS", [P, D], F32))
        Y, SQ, WC, WS, BETAC, BH, BL, ONE = place(
            48, ("Y", [P, NT, 2, H0, D0], F32), ("SQ", [P, 2, 2 * H0, D0], F32), ("WC", [P, NC, 2 * D], F32),
            ("WS", [P, NC * 2 * H0 + 1], F32), ("BETAC", [1, 2, D0], F32), ("BH", [1, 2 * D], F32R),
            ("BL", [1, 2 * D], F32R), ("ONE", [1, P], F32R))
        WQH, WQL, WQR = place(88, ("WQH", [P, NC, 3 * D], F32R), ("WQL", [P, NC, 3 * D], F32R),
                              ("WQR", [P, NC, 3 * D], F32))
        (WO0,) = place(106, ("WO0", [P, NC, D], F32))
        SLT, VA = place(108, ("SLT", [P, 2, NT, H0, SLOTS, D0], BF16), ("VA", [P, NT, H0, D0 + 1], F32))
        VS, SD = place(181, ("VS", [P, NT, 2, H0], F32), ("SD", [P, NT, 2, H0], F32))
        AT = place(181, *((f"AT{g}", [P, 512 * (g + 1)], F32) for g in range(4)))
        ATL = dict(zip((2, 3), place(187, *((f"AL{g}", [P, 512 * (g + 1)], F32R) for g in (2, 3)))))
        AHI = {2: place(8, ("AH2", [P, 3 * 512], F32R))[0], 3: place(96, ("AH3", [P, 4 * 512], F32R))[0]}
        VR, VRS = place(201, ("VR", [P, 2, NT, D0 + 1], F32), ("VRS", [P, 2, NT, 32 + D0 + 1], F32R))
        (OT4,) = place(16, ("OT4", [P, H0 // 4, T], F32))
        STK = place(88, ("STK", [P, 2, 2, T], BF16))[0]
        (OT0,) = place(108, ("OT0", [P, NC, T], F32))
        UP, DOWN = place(48, ("UP", [P, NE, NC, MI], F32), ("DOWN", [P, NE, D], F32))
        UPH, UPL, RELU, AH, AL, DNH, DNL = place(
            88, ("UPH", [P, 2, NC, MI], F32R), ("UPL", [P, 2, NC, MI], F32R), ("RELU", [P, 2, T // 2], F32),
            ("AH", [P, 2, T], F32R), ("AL", [P, 2, T], F32R), ("DNH", [P, 2, D], F32R), ("DNL", [P, 2, D], F32R))

        W2, WRN, WKR, WDR, WDH, WDL = place(
            109, ("W2", [P, H1 // 2, D], F32), ("WRN", [P, 2, 2 * H1 * DR], F32), ("WKR", [P, H1 * DR], F32),
            ("WDR", [P, NC, D], F32), ("WDH", [P, NC, D], F32R), ("WDL", [P, NC, D], F32R))
        WRNL, WKRL = place(117, ("WRNL", [P, 2, 2 * H1 * DR], F32R), ("WKRL", [P, H1 * DR], F32R))
        WKRH, KV = place(137, ("WKRH", [P, H1 * DR], F32R), ("KV", [P, NT, KVR], F32))
        (WRH1,) = place(24, ("WRH1", [P, 2, H1 * DR], F32R))
        (LTF,) = place(8, ("LTF", [P, T], F32))
        WQN, WKN, WV, WO1 = place(143, ("WQN", [P, H1, QR], F32), ("WKN", [P, H1, KVR], F32),
                                  ("WV", [96, H1, 2, P], F32), ("WO1", [96, H1, 2, D], F32))
        (QT,) = place(45, ("QT", [P, H1, T], F32))
        UNH, UNL = place(105, ("UNH", [P, 2, 2, P], F32R), ("UNL", [P, 2, 2, P], F32R))
        (KT,) = place(175, ("KT", [P, H1 // 2, T], F32))
        LTH, LTL, QTOK, KTOK = place(143, ("LTH", [P, 2, T], F32R), ("LTL", [P, 2, T], F32R),
                                     ("QTOK", [P, 2, H1 * DR], F32), ("KTOK", [P, 2, H1 * DR], F32))
        TQ, TK = place(8, ("TQ", [P, 2, H1 * DR], F32), ("TK", [P, 2, H1 * DR], F32))
        PB, PT, NM, LS, RL, PBS = place(
            8, ("PB", [P, 2, T], F32), ("PT", [P, 4, 512], F32), ("NM", [P, H1 * NT], F32),
            ("LS", [P, H1 * NT], F32), ("RL", [P, H1 * NT], F32), ("PBS", [P, 2, T // 2], F32))
        QH, QL, KH, KL = place(143, ("QH", [P, 2, T], F32R), ("QL", [P, 2, T], F32R),
                               ("KH", [P, 2, T], F32R), ("KL", [P, 2, T], F32R))
        OTH, OTL = place(143, ("OTH", [P, 2, H1 // 2, P], F32R), ("OTL", [P, 2, H1 // 2, P], F32R))
        W2H, W2L = place(175, ("W2H", [P, H1 // 2, D], F32R), ("W2L", [P, H1 // 2, D], F32R))
        GU, DNW, GUH, GUL = place(117, ("GU", [P, NF, 2 * NC, P], F32), ("DNW", [P, NF, D], F32),
                                  ("GUH", [P, 2, 2 * NC, P], F32R), ("GUL", [P, 2, 2 * NC, P], F32R))
        HT, EX, HTH = place(151, ("HT", [P, NF, T], F32), ("EX", [P, 2, T], F32), ("HTH", [P, NF, T], F32R))
        (HTL,) = place(151, ("HTL", [P, NF, T], F32R))
        DNWH, DNWL = place(45, ("DNWH", [P, NF, D], F32R), ("DNWL", [P, NF, D], F32R))

        PS = ctx.enter_context(nc.psum_tensor("PS", [P, 8, 512], F32))

        made = {}

        def sem(name):
            if name not in made:
                made[name] = ctx.enter_context(nc.semaphore(name))
            return made[name]

        loads = {}

        def mm3(o, left, right, start=True, stop=True):
            (lh, ll), (rh, rl) = left, right
            nc.tensor.matmul(o, lh, rh, start=start, stop=False)
            nc.tensor.matmul(o, lh, rl, start=False, stop=False)
            return nc.tensor.matmul(o, ll, rh, start=False, stop=stop)

        def f(ap):
            return ap.bitcast(F32)

        GAMMA, BETA = CST[:, 0:16], CST[:, 16:32]
        EBIAS, KEY, LTRI = CST[:, 32:48], CST[:, 48:64], CST[:, 64:80]

        block = ctx.enter_context(nc.Block())

        LN_COUNTS = dict(stat=NT, var=NT, ve=NT // 2, rstd=NT // 2, xn=NT, tr=NT // 2, hi=NT // 2, lo=NT // 2)

        def ln_wait(eng, k, what, count):
            eng.wait_ge(sem("ln_" + what), LN_COUNTS[what] * k + count)

        def ln_dve_stats(dve, k, x_ready, j):
            for tt in (2 * j, 2 * j + 1):
                x_ready(tt)
                nc.vector.bn_stats(STAT[:, tt, :], X[:, tt, :]).then_inc(sem("ln_stat"), 1)
            for tt in (2 * j, 2 * j + 1):
                ln_wait(dve, k, "stat", tt + 1)
                nc.vector.bn_aggr(MV[:, tt, :], STAT[:, tt, :]).then_inc(sem("ln_var"), 1)

        def ln_pool(pool, k, shift=None):
            for j in range(NT // 2):
                ln_wait(pool, k, "var", 2 * j + 2)
                g = slice(2 * j, 2 * j + 2)
                nc.gpsimd.tensor_scalar(VE[:, g], MV[:, g, 1], 1.0, EPS, ALU.mult, ALU.add).then_inc(sem("ln_ve"), 1)
                ln_wait(pool, k, "ve", j + 1)
                if k == 0 and j == 0:
                    pool.wait_ge(sem("half"), 1)
                nc.gpsimd.tensor_tensor(RSTD[:, g], VE[:, g], HALF[:, g], ALU.pow).then_inc(sem("ln_rstd"), 1)
                if shift is not None:
                    ln_wait(pool, k, "rstd", j + 1)
                    for tt in (2 * j, 2 * j + 1):
                        nc.gpsimd.tensor_scalar(shift[:, tt:tt + 1], MV[:, tt, 0:1], RSTD[:, tt:tt + 1], -1.0,
                                                ALU.mult, ALU.mult).then_inc(sem("ln_shift"), 1)

        def ln_dve_norm(dve, k, j):
            ln_wait(dve, k, "rstd", j + 1)
            for tt in (2 * j, 2 * j + 1):
                nc.vector.tensor_scalar(XN[:, tt, :], X[:, tt, :], MV[:, tt, 0:1], RSTD[:, tt:tt + 1],
                                        ALU.subtract, ALU.mult).then_inc(sem("ln_xn"), 1)

        def ln_pe(pe, k, banks, j):
            ln_wait(pe, k, "xn", 2 * j + 2)
            if j >= 2:
                ln_wait(pe, k, "lo", j - 1)
            bank = PS[:, banks[j % 2], :].rearrange("p (c t) -> p c t", c=NC)
            for i in range(2):
                for c in range(NC):
                    last = nc.tensor.transpose(bank[:, c, i * P:(i + 1) * P],
                                               XN[:, 2 * j + i, c * P:(c + 1) * P], IDF[:, :])
            last.then_inc(sem("ln_tr"), 1)

        def ln_act(act, k, banks, pairs=range(NT // 2)):
            for j in pairs:
                ln_wait(act, k, "tr", j + 1)
                bank = PS[:, banks[j % 2], :].rearrange("p (c t) -> p c t", c=NC)
                nc.scalar.copy(XTH[:, :, 256 * j:256 * j + 256], bank).then_inc(sem("ln_hi"), 1)

        def ln_dve_lo(dve, k, banks, j):
            ln_wait(dve, k, "hi", j + 1)
            bank = PS[:, banks[j % 2], :].rearrange("p (c t) -> p c t", c=NC)
            cols = slice(256 * j, 256 * j + 256)
            nc.vector.tensor_tensor(XTL[:, :, cols], bank, f(XTH[:, :, cols]), ALU.subtract)\
                .then_inc(sem("ln_lo"), 1)

        def ln_dve(dve, k, banks, x_ready):
            for j in range(NT // 2 + 2):
                if j < NT // 2:
                    ln_dve_stats(dve, k, x_ready, j)
                if 1 <= j <= NT // 2:
                    ln_dve_norm(dve, k, j - 1)
                if j >= 2:
                    ln_dve_lo(dve, k, banks, j - 2)

        def xt(c, cols):
            return XTH[:, c, cols], XTL[:, c, cols]

        def pool_wait(pool, name, value):
            pool.wait_ge(sem(name), value)
            pool.sem_inc(sem("pool_waited"), 1)

        def tile(tt):
            return slice(tt * P, (tt + 1) * P)

        def qk_bank(tt):
            return PS[:, 2 + tt % 6, :]

        BASE = [0, 1, 3, 6]
        NB = 4
        OPS, SPB = 4, (6, 7)
        LN_BANKS = (0, 1)

        def l0_scores(pe, h, p, g, loads):
            for j in loads:
                n = BASE[g] + j
                if not (isinstance(h, int) and 10 * h + n < NB):
                    pe.wait_ge(sem("l0_sq"), 10 * h + n - NB + 1)
                for i in range(2):
                    last = nc.tensor.matmul(PS[:, (10 * p + n) % NB, 256 * i:256 * i + 256],
                                            STK[:, p, 1, tile(2 * j + i)], STK[:, p, 0, 256 * g:256 * g + 256],
                                            start=True, stop=True)
                last.then_inc(sem("l0_score"), 1)

        def l0_stack(pe, h, qk):
            if not (isinstance(h, int) and 2 * h + qk == 0):
                pe.wait_ge(sem("l0_stke"), 2 * h + qk)
            for tt in range(NT):
                last = nc.tensor.matmul(PS[:, SPB[tt // 4], (tt % 4) * P:(tt % 4 + 1) * P],
                                        SLT[:, qk, tt, bass.ds(h, 1), :, :].rearrange("p o s d -> p (o s d)"),
                                        IDB[:, :], start=True, stop=True)
            last.then_inc(sem("l0_stk"), 1)

        MASKS = (1, 2, 4, 6)

        def l0_av(pe, h, p, g):
            if g < 2:
                pe.wait_ge(sem("l0_sq"), 10 * h + BASE[g] + g + 1)
                pe.wait_ge(sem("l0_mask"), 6 * h + MASKS[g])
            else:
                pe.wait_ge(sem("l0_al"), 5 * h + (2 if g == 2 else 5))
                pe.wait_ge(sem("l0_alp"), 2 * h + g - 1)
            pe.wait_ge(sem("l0_vr"), h + 1)
            if not (isinstance(h, int) and h == 0 and g < 2):
                pe.wait_ge(sem("l0_oev"), 4 * h + g - 1)
            for sb in range(2 * g + 2):
                skip = P if sb == 2 * g + 1 else 0
                first, final = sb == 0, sb == 2 * g + 1
                cols = slice(256 * sb + skip, 256 * sb + 256)
                if g < 2:
                    last = nc.tensor.matmul(PS[0:D0 + 1, OPS + g % 2, skip:256], VR[:, p, sb, :], AT[g][:, cols],
                                            start=first, stop=final)
                else:
                    o = PS[0:32 + D0 + 1, OPS + g % 2, skip:256]
                    nc.tensor.matmul(o, VRS[:, p, sb, :], AHI[g][:, cols], start=first, stop=False)
                    last = nc.tensor.matmul(o, VRS[:, p, sb, :], ATL[g][:, cols], start=False, stop=final)
            last.then_inc(sem("l0_av"), 1)

        def pe_head(pe, h, p, first=False, final=False):
            pe.wait_ge(sem("l0_stke"), 2 * h + 2)
            l0_scores(pe, h, p, 0, (0,))
            l0_scores(pe, h, p, 1, (0, 1))
            if not first:
                l0_av(pe, h - 1, 1 - p, 2)
            l0_scores(pe, h, p, 2, (0,))
            if not final:
                l0_stack(pe, h + 1, 0)
            l0_scores(pe, h, p, 2, (1,))
            l0_scores(pe, h, p, 2, (2,))
            if not first:
                l0_av(pe, h - 1, 1 - p, 3)
            l0_scores(pe, h, p, 3, (0,))
            l0_scores(pe, h, p, 3, (1,))
            l0_av(pe, h, p, 0)
            if not final:
                l0_stack(pe, h + 1, 1)
            l0_scores(pe, h, p, 3, (2,))
            l0_scores(pe, h, p, 3, (3,))
            l0_av(pe, h, p, 1)

        def act_head(act, h, p, first=False):
            for g in range(4):
                if not first:
                    act.wait_ge(sem("l0_av"), 4 * (h - 1) + g + 1)
                for j in range(g + 1):
                    n = BASE[g] + j
                    act.wait_ge(sem("l0_score"), 10 * h + n + 1)
                    cols, bank = slice(512 * j, 512 * j + 512), PS[:, (10 * p + n) % NB, :]
                    if g >= 2:
                        nc.scalar.activation(AHI[g][:, cols], bank, ACT.Square)
                    nc.scalar.activation(AT[g][:, cols], bank, ACT.Square).then_inc(sem("l0_sq"), 1)

        def pool_head(pool, h):
            for g in range(4):
                if g >= 2:
                    pool_wait(pool, "l0_sq", 10 * h + BASE[g] + 2)
                    cols = slice(512, 1024)
                    nc.gpsimd.tensor_tensor(ATL[g][:, cols], AT[g][:, cols], f(AHI[g][:, cols]), ALU.subtract)\
                        .then_inc(sem("l0_alp"), 1)
                pool_wait(pool, "l0_sq", 10 * h + BASE[g] + g + 1)
                for a in (AT[g],) if g < 2 else (AT[g], AHI[g]):
                    v = a[:, 512 * g:512 * g + 512].rearrange("p (b t) -> p b t", b=4)[:, 0:4:3, :]
                    nc.gpsimd.affine_select(out=v, in_=v, pattern=[[0, 2], [1, P]], compare_op=ALU.is_ge, fill=0.0,
                                            base=0, channel_multiplier=-1).then_inc(sem("l0_mask"), 1)

        def dve_lo(dve, h, g, j):
            dve.wait_ge(sem("l0_sq"), 10 * h + BASE[g] + j + 1)
            if j == g:
                dve.wait_ge(sem("l0_mask"), 6 * h + MASKS[g])
            cols = slice(512 * j, 512 * j + 512)
            nc.vector.tensor_tensor(ATL[g][:, cols], AT[g][:, cols], f(AHI[g][:, cols]), ALU.subtract)\
                .then_inc(sem("l0_al"), 1)

        def l0_slots(dve, g):
            r = slice(2 * g, 2 * g + 2)
            dve.wait_ge(sem("l0_p2"), 2 * g + 1)
            nc.vector.tensor_tensor(SLT[:, 0, r, :, 2, :], Y[:, r, 0], SLT[:, 0, r, :, 1, :], ALU.subtract)\
                .then_inc(sem("l0_p3"), 1)

            def th(a):
                return a.rearrange("p t h s d -> p (t h) s d")
            q, k = SLT[:, 0, r], SLT[:, 1, r]
            nc.vector.tensor_copy(th(q[:, :, :, 6:8]), th(q[:, :, :, 0:2]))
            dve.wait_ge(sem("l0_p3"), g + 1)
            nc.vector.tensor_copy(th(q[:, :, :, 3:6]), th(q[:, :, :, 0:3])).then_inc(sem("l0_qslots"), 1)
            nc.vector.tensor_copy(th(k[:, :, :, 1:3]), th(k[:, :, :, 0:1]).to_broadcast([P, 32, 2, D0]))
            dve.wait_ge(sem("l0_p2"), 2 * g + 2)
            nc.vector.tensor_copy(th(k[:, :, :, 4:6]), th(k[:, :, :, 3:4]).to_broadcast([P, 32, 2, D0]))
            dve.wait_ge(sem("l0_p3k"), g + 1)
            nc.vector.tensor_copy(th(k[:, :, :, 7:8]), th(k[:, :, :, 6:7])).then_inc(sem("l0_slots"), 1)

        def dve_stack_out(dve, h, p, qk):
            dve.wait_ge(sem("l0_stk"), 2 * h + qk + 1)
            if not (isinstance(h, int) and h < 2):
                dve.wait_ge(sem("l0_score"), 10 * (h - 1))
            nc.vector.tensor_copy(STK[:, p, qk, :].rearrange("p (b t) -> p b t", b=2), PS[:, SPB[0]:SPB[1] + 1, :])\
                .then_inc(sem("l0_stke"), 1)

        def dve_values(dve, h, p):
            if not (isinstance(h, int) and h < 2):
                dve.wait_ge(sem("l0_av"), 4 * (h - 1))
            v = VA[:, :, bass.ds(h, 1), :].rearrange("p t o e -> p t (o e)")
            nc.vector.tensor_copy(VR[:, p], v)
            nc.vector.tensor_copy(VRS[:, p, :, 0:D0 + 1], v).then_inc(sem("l0_vh"), 1)
            dve.wait_ge(sem("l0_vh"), h + 1)
            nc.vector.tensor_tensor(VRS[:, p, :, 32:], v, f(VRS[:, p, :, 0:D0 + 1]), ALU.subtract)\
                .then_inc(sem("l0_vr"), 1)

        def out_rows(h, r, g):
            rows = OT4[32 * r:32 * r + D0 + 1, :, :].rearrange("p q t -> p (q t)")
            return rows[:, bass.ds((h - r) * (T // 4) + 256 * g, 256)]

        def dve_out(dve, h, r, g):
            dve.wait_ge(sem("l0_av"), 4 * h + g + 1)
            done = sem("l0_oev" if g < 2 else "l0_oh")
            nc.vector.tensor_copy(out_rows(h, r, g), PS[0:D0 + 1, OPS + g % 2, 0:256]).then_inc(done, 1)

        def dve_out_add(dve, h, r, g):
            dve.wait_ge(sem("l0_oh"), 2 * h + g - 1)
            nc.vector.tensor_tensor(out_rows(h, r, g), PS[32:32 + D0 + 1, OPS + g % 2, 0:256], out_rows(h, r, g),
                                    ALU.add).then_inc(sem("l0_oev"), 1)

        def dve_head(dve, h, r, first=False, final=False):
            if not first:
                dve_lo(dve, h - 1, 3, 3)
            if not first:
                dve_out(dve, h - 1, (r - 1) % 4, 2)
            if not final:
                dve_stack_out(dve, h + 1, 1 - r % 2, 0)
            if not first:
                dve_out_add(dve, h - 1, (r - 1) % 4, 2)
            dve_lo(dve, h, 2, 0)
            if not final:
                dve_values(dve, h + 1, 1 - r % 2)
            if not first:
                dve_out(dve, h - 1, (r - 1) % 4, 3)
            if not first:
                dve_out_add(dve, h - 1, (r - 1) % 4, 3)
            if not final:
                dve_stack_out(dve, h + 1, 1 - r % 2, 1)
            dve_lo(dve, h, 2, 2)
            dve_out(dve, h, r, 0)
            dve_lo(dve, h, 3, 0)
            dve_lo(dve, h, 3, 2)
            dve_out(dve, h, r, 1)

        def loop_heads4(eng, one):
            one(0, 0, first=True)
            with eng.Fori(0, (H0 - 4) // 4) as i:
                for r in (1, 2, 3):
                    one(4 * i + r, r)
                one(4 * i + 4, 0)
            one(H0 - 3, 1)
            one(H0 - 2, 2)
            one(H0 - 1, 3, final=True)

        def loop_heads(eng, one):
            one(0, 0, first=True)
            with eng.Fori(0, H0 // 2 - 1) as i:
                one(2 * i + 1, 1)
                one(2 * i + 2, 0)
            one(H0 - 1, 1, final=True)

        def moe_split(pool, e, p):
            if not (isinstance(e, int) and e < 2):
                pool_wait(pool, "m_up", 2 * e - 2)
            src = UP[:, bass.ds(e, 1), :, :].rearrange("p o c i -> p (o c) i")
            nc.gpsimd.tensor_copy(UPH[:, p], src).then_inc(sem("m_hi"), 1)
            pool_wait(pool, "m_hi", 2 * e + 1)
            nc.gpsimd.tensor_tensor(UPL[:, p], src, f(UPH[:, p]), ALU.subtract).then_inc(sem("m_split"), 1)
            if not (isinstance(e, int) and e < 2):
                pool_wait(pool, "m_dn", 4 * e - 4)
            src = DOWN[:, bass.ds(e, 1), :].rearrange("p o d -> p (o d)")
            nc.gpsimd.tensor_copy(DNH[:, p], src).then_inc(sem("m_hi"), 1)
            pool_wait(pool, "m_hi", 2 * e + 2)
            nc.gpsimd.tensor_tensor(DNL[:, p], src, f(DNH[:, p]), ALU.subtract).then_inc(sem("m_dsplit"), 1)

        def moe_up(pe, e, p):
            pe.wait_ge(sem("m_split"), e + 1)
            for n in range(2):
                if not (isinstance(e, int) and e < 2):
                    pe.wait_ge(sem("m_relu"), 2 * (e - 2) + n + 1)
                for c in range(NC):
                    last = mm3(PS[:, 2 * p + n, :], (UPH[:, p, c, :], UPL[:, p, c, :]),
                               xt(c, slice(512 * n, 512 * n + 512)), start=(c == 0), stop=(c == NC - 1))
                last.then_inc(sem("m_up"), 1)

        def moe_down(pe, e, p):
            for b in range(4):
                if b == 0:
                    pe.wait_ge(sem("m_dsplit"), e + 1)
                if b % 2 == 0:
                    pe.wait_ge(sem("m_al"), 2 * e + b // 2 + 1)
                if not (isinstance(e, int) and e < 1):
                    pe.wait_ge(sem("m_acc"), 8 * (e - 1) + 2 * b + 2)
                for i in range(2):
                    last = mm3(PS[:, 4 + b, 256 * i:256 * i + 256], (AH[:, p, tile(2 * b + i)], AL[:, p, tile(2 * b + i)]),
                               (DNH[:, p, :], DNL[:, p, :]))
                last.then_inc(sem("m_dn"), 1)

        def moe_act(act, e, p):
            for n in range(2):
                act.wait_ge(sem("m_up"), 2 * e + n + 1)
                if not (isinstance(e, int) and e < 1):
                    act.wait_ge(sem("m_al"), 2 * e - 1 + n)
                nc.scalar.activation(RELU[:, n, :], PS[:, 2 * p + n, :], ACT.Relu).then_inc(sem("m_relu"), 1)
                act.wait_ge(sem("m_relu"), 2 * e + n + 1)
                if not (isinstance(e, int) and e < 2):
                    act.wait_ge(sem("m_dn"), 4 * e - 4)
                nc.scalar.activation(AH[:, p, 512 * n:512 * n + 512], RELU[:, n, :], ACT.Square).then_inc(sem("m_ah"), 1)
                act.wait_ge(sem("m_ah"), 2 * e + n + 1)
                nc.scalar.activation(RELU[:, n, :], RELU[:, n, :], ACT.Square).then_inc(sem("m_sq"), 1)

        def moe_lo(dve, e, p):
            for n in range(2):
                dve.wait_ge(sem("m_sq"), 2 * e + n + 1)
                nc.vector.tensor_tensor(AL[:, p, 512 * n:512 * n + 512], RELU[:, n, :],
                                        f(AH[:, p, 512 * n:512 * n + 512]), ALU.subtract).then_inc(sem("m_al"), 1)

        def moe_acc_bank(dve, e, b):
            dve.wait_ge(sem("m_dn"), 4 * e + b + 1)
            for i in range(2):
                tt = 2 * b + i
                if not (isinstance(e, int) and e < 1):
                    dve.wait_ge(sem("m_acc"), 8 * (e - 1) + tt + 1)
                nc.vector.scalar_tensor_tensor(
                    out=X[:, tt, :], in0=PS[:, 4 + b, 256 * i:256 * i + 256],
                    scalar=CMB[:, tt, bass.ds(e, 1)], in1=X[:, tt, :], op0=ALU.mult, op1=ALU.add)\
                    .then_inc(sem("m_acc"), 1)

        def moe_acc(dve, e):
            for b in range(4):
                moe_acc_bank(dve, e, b)

        def grab(bank, n, rows=slice(0, P)):
            return PS[rows, bank, 0:n]

        def l1_products(pe):
            pe.wait_ge(sem("ld_prod"), 64)
            for half in range(2):
                for m, (r0, r1) in enumerate(((0, P), (P, QR))):
                    bank = 2 * m + half
                    for i in range(8):
                        last = nc.tensor.matmul(PS[0:r1 - r0, bank, 64 * (i ^ 1):64 * (i ^ 1) + 64], WQN[:, 8 * half + i, r0:r1],
                                                WKN[:, 8 * half + i, :], start=True, stop=True)
                last.then_inc(sem("p_wn"), 1)
            pe.wait_ge(sem("m_acc"), 8 * NE)
            for q in range(H1 // 2):
                for i in range(4):
                    last = nc.tensor.matmul(PS[:, 4 + q // 2, 256 * (q % 2):256 * (q % 2) + 256],
                                            WV[:, 2 * q + i // 2, i % 2, :], WO1[:, 2 * q + i // 2, i % 2, :],
                                            start=(i == 0), stop=(i == 3))
                if q % 2:
                    last.then_inc(sem("p_w2"), 1)
                if q in (3, 5, 7):
                    if q == 3:
                        pe.wait_ge(sem("wn"), 4)
                    ln_pe(pe, 2, LN2_BANKS, (q - 3) // 2)
            ln_pe(pe, 2, LN2_BANKS, 3)

        def l1_products_out(act):
            for half in range(2):
                act.wait_ge(sem("p_wn"), half + 1)
                cols = slice(H1 * DR + 512 * half, H1 * DR + 512 * half + 512)
                nc.scalar.copy(WRN[:, 0, cols], PS[:, half, :]).then_inc(sem("wn"), 1)
                nc.scalar.copy(WRN[0:QR - P, 1, cols], PS[0:QR - P, 2 + half, :]).then_inc(sem("wn"), 1)
            for b in range(4):
                act.wait_ge(sem("p_w2"), b + 1)
                nc.scalar.copy(W2[:, 2 * b:2 * b + 2, :], PS[:, 4 + b, :].rearrange("p (q d) -> p q d", q=2))\
                    .then_inc(sem("w2"), 1)

        LN2_BANKS = (0, 1)

        SOFAR = slice(0, T - P)
        KVROWS, QROWS = slice(P - KVR, P), slice(0, QR - P)

        def l1_latents(pe):
            pe.wait_ge(sem("wd_lo"), 1)
            pe.wait_ge(sem("w2"), 4)
            for n in range(2):
                ln_wait(pe, 2, "lo", 2 * n + 2)
                for m in range(2):
                    for c in range(NC):
                        last = mm3(PS[:, 4 + 2 * m + n, :], (WDH[:, c, tile(m)], WDL[:, c, tile(m)]),
                                   xt(c, slice(512 * n, 512 * n + 512)), start=(c == 0), stop=(c == NC - 1))
                    last.then_inc(sem("lat"), 1)

        def l1_latents_act(act):
            for n in range(2):
                for m in range(2):
                    act.wait_ge(sem("lat"), 2 * n + m + 1)
                    cols = slice(512 * n, 512 * n + 512)
                    if m == 1:
                        nc.scalar.copy(LTF[KVROWS, cols], PS[KVROWS, 6 + n, :]).then_inc(sem("ltf"), 1)
                    nc.scalar.copy(LTH[:, m, cols], PS[:, 4 + 2 * m + n, :]).then_inc(sem("lth"), 1)

        def l1_rotary_hi(act):
            nc.scalar.copy(WRH1[:], WRN[:, :, 0:H1 * DR]).then_inc(sem("rw_hi"), 1)
            nc.scalar.copy(WKRH[KVROWS], WKR[KVROWS]).then_inc(sem("rw_hi"), 1)
            act.wait_ge(sem("kv_tr"), 1)
            nc.scalar.copy(KV[:], PS[:, 4, :].rearrange("p (t d) -> p t d", t=NT)).then_inc(sem("kv"), 1)

        def l1_latents_dve(dve):
            for n in range(2):
                for m in range(2):
                    dve.wait_ge(sem("lth"), 2 * n + m + 1)
                    cols = slice(512 * n, 512 * n + 512)
                    nc.vector.tensor_tensor(LTL[:, m, cols], PS[:, 4 + 2 * m + n, :], f(LTH[:, m, cols]), ALU.subtract)\
                        .then_inc(sem("ltl"), 1)

        def l1_rotary_lo(dve):
            dve.wait_ge(sem("rw_hi"), 2)
            nc.vector.tensor_tensor(WRNL[:, :, 0:H1 * DR], WRN[:, :, 0:H1 * DR], f(WRH1[:]), ALU.subtract)\
                .then_inc(sem("rw_lo"), 1)
            nc.vector.tensor_tensor(WKRL[KVROWS], WKR[KVROWS], f(WKRH[KVROWS]), ALU.subtract).then_inc(sem("rw_lo"), 1)

        def l1_kv(pe):
            pe.wait_ge(sem("ltf"), 2)
            pe.wait_ge(sem("ltl"), 4)
            for tt in range(NT):
                last = nc.tensor.transpose(PS[:, 4, tt * KVR:(tt + 1) * KVR], LTF[KVROWS, tile(tt)],
                                           IDF[KVROWS, KVROWS])
            last.then_inc(sem("kv_tr"), 1)

        def un_split(pool, q):
            pool.wait_ge(sem("wn"), 4)
            if q >= 2:
                pool.wait_ge(sem("un"), q - 1)
            src = WRN[:, :, H1 * DR + P * q:H1 * DR + P * (q + 1)]
            for kt, rows in ((0, slice(0, P)), (1, QROWS)):
                nc.gpsimd.tensor_copy(UNH[rows, q % 2, kt], src[rows, kt]).then_inc(sem("un_hi"), 1)
                pool.wait_ge(sem("un_hi"), 2 * q + kt + 1)
                nc.gpsimd.tensor_tensor(UNL[rows, q % 2, kt], src[rows, kt], f(UNH[rows, q % 2, kt]), ALU.subtract)\
                    .then_inc(sem("un_w"), 1)
                pool.wait_ge(sem("un_w"), 2 * q + kt + 1)

        def un_banks(q):
            b = 2 * (q % 2)
            return PS[:, b:b + 2, :]

        def l1_unrotated(pe, q):
            pe.wait_ge(sem("un_w"), 2 * q + 2)
            if q >= 2:
                pe.wait_ge(sem("un_oa" if q % 2 == 0 else "un_od"), 2 * (q // 2))
            for n in range(2):
                cols = slice(512 * n, 512 * n + 512)
                for kt, rows in ((0, slice(0, P)), (1, QROWS)):
                    last = mm3(un_banks(q)[:, n, :], (UNH[rows, q % 2, kt], UNL[rows, q % 2, kt]),
                               (LTH[rows, kt, cols], LTL[rows, kt, cols]), start=(kt == 0), stop=(kt == 1))
            last.then_inc(sem("un"), 1)

        def l1_unrotated_out(eng, q):
            eng.wait_ge(sem("un"), q + 1)
            for h, rows in ((2 * q + 1, slice(0, DR)), (2 * q, slice(DR, P))):
                src, dst = un_banks(q)[rows].rearrange("p b n -> p (b n)"), QT[rows, h, :]
                if q % 2 == 0:
                    nc.scalar.activation(dst, src, ACT.Copy, scale=SCALE).then_inc(sem("un_oa"), 1)
                else:
                    nc.vector.tensor_scalar(dst, src, SCALE, None, ALU.mult).then_inc(sem("un_od"), 1)

        def l1_project(pe, tt):
            if tt:
                pe.wait_ge(sem("q_rot"), 3 * tt)
            for b in range(2):
                cols = slice(512 * b, 512 * b + 512)
                for kt, rows in ((0, slice(0, P)), (1, QROWS)):
                    last = mm3(PS[:, 4 + b, :], (LTH[rows, kt, tile(tt)], LTL[rows, kt, tile(tt)]),
                               (WRH1[rows, kt, cols], WRNL[rows, kt, cols]), start=(kt == 0), stop=(kt == 1))
            last.then_inc(sem("proj"), 1)
            if tt:
                pe.wait_ge(sem("k_rot"), 3 * tt)
            for b in range(2):
                cols = slice(512 * b, 512 * b + 512)
                last = mm3(PS[:, 6 + b, :], (LTH[KVROWS, 1, tile(tt)], LTL[KVROWS, 1, tile(tt)]),
                           (WKRH[KVROWS, cols], WKRL[KVROWS, cols]))
            last.then_inc(sem("proj"), 1)

        def l1_rotate(dve, tt):
            co = ROPE[:, 0, tt, :].unsqueeze(1).to_broadcast([P, H1, DR])
            h = DR // 2
            for name, bank, buf, ready in (("q_rot", 4, TQ, 2 * tt + 1), ("k_rot", 6, TK, 2 * tt + 2)):
                dve.wait_ge(sem("proj"), ready)
                if tt:
                    dve.wait_ge(sem(name[0] + "_sum"), tt)
                src = PS[:, bank:bank + 2, :].rearrange("p b (h d) -> p (b h) d", d=DR)
                a, b = (buf[:, i, :].rearrange("p (h d) -> p h d", d=DR) for i in range(2))
                nc.vector.tensor_tensor(a, src, co, ALU.mult).then_inc(sem(name), 1)
                for j in range(2):
                    si = ROPE[:, 1, tt, j * h:(j + 1) * h].unsqueeze(1).to_broadcast([P, H1, h])
                    nc.vector.tensor_tensor(b[:, :, j * h:(j + 1) * h], src[:, :, (1 - j) * h:(2 - j) * h], si,
                                            ALU.mult).then_inc(sem(name), 1)

        def l1_sums(pool, tt):
            for name, buf, dst in (("q", TQ, QTOK), ("k", TK, KTOK))[:1 if tt == NT - 1 else 2]:
                pool.wait_ge(sem(name + "_rot"), 3 * tt + 3)
                if tt >= 2:
                    pool.wait_ge(sem(name + "_tr"), 2 * (tt - 1))
                nc.gpsimd.tensor_tensor(dst[:, tt % 2, :], buf[:, 0, :], buf[:, 1, :], ALU.add)\
                    .then_inc(sem(name + "_sum"), 1)

        def l1_transpose(pe, tt):
            for g in range(4):
                name, src = ("q", QTOK) if g < 2 else ("k", KTOK)
                if g % 2 == 0:
                    pe.wait_ge(sem(name + "_sum"), tt + 1)
                if tt:
                    pe.wait_ge(sem("qk_t"), 4 * tt - 3 + g)
                for i in range(4):
                    col = (4 * (g % 2) + i) * P
                    last = nc.tensor.transpose(PS[:, g, i * P:(i + 1) * P], src[:, tt % 2, col:col + P], IDF[:, :])
                last.then_inc(sem(name + "_tr"), 1)

        def l1_transposed(act, tt):
            for g in range(4):
                src = PS[:, g, :].rearrange("p (q t) -> p q t", q=4)
                if g < 2:
                    act.wait_ge(sem("q_tr"), 2 * tt + g + 1)
                    for e, rows in ((0, slice(0, DR)), (1, slice(DR, P))):
                        dst = QT[rows, 8 * g:8 * g + 8, tile(tt)].rearrange("p (q e) t -> p q e t", e=2)[:, :, e]
                        last = nc.scalar.activation(dst, src[rows], ACT.Copy, scale=SCALE)
                        last.then_inc(sem("qk_q"), 1)
                    act.wait_ge(sem("qk_q"), 4 * tt + 2 * g + 2)
                    act.sem_inc(sem("qk_t"), 1)
                else:
                    act.wait_ge(sem("k_tr"), 2 * tt + g - 1)
                    nc.scalar.copy(KT[:, 4 * (g - 2):4 * (g - 2) + 4, tile(tt)], src).then_inc(sem("qk_t"), 1)

        ORDER = (7, 0, 6, 1, 5, 2, 4, 3)
        GROUPS = 12
        S_SMALL, PT_BANKS, O_BANK = 4, 5, 7

        def group(i, b):
            return 3 * (i // 2) + (b if i % 2 == 0 else 2)

        def by_act(n):
            return n % 3 == 1

        def unit_of(n):
            return 2 * (n // 3) + (n % 3) // 2

        def back(h, n, k, total):
            if n - k >= 0:
                return h, n - k
            return None if isinstance(h, int) and h == 0 else (h - 1, n - k + total)

        def wait_group(eng, h, n):
            done = sum(by_act(m) == by_act(n) for m in range(n + 1))
            if by_act(n):
                eng.wait_ge(sem("a_pa"), 4 * h + done)
            else:
                eng.wait_ge(sem("a_pd"), 8 * h + done)

        def s_view(i):
            keys = (ORDER[i] + 1) * P
            if i % 2:
                return PS[:, S_SMALL, 0:keys]
            b = i % 4
            return PS[:, b:b + 2, :].rearrange("p b n -> p (b n)")[:, 0:keys]

        def p_view(i):
            keys = (ORDER[i] + 1) * P
            return (PBS if i % 2 else PB)[:, i // 2 % 2, 0:keys]

        def a_scores(pe, h, p, i):
            if i == 0:
                pe.wait_ge(sem("a_hi"), 2 * h + 2)
                pe.wait_ge(sem("a_lo"), 2 * h + 2)
            if prev := back(h, i, 2 if i % 2 else 4, NT):
                pe.wait_ge(sem("a_p"), 8 * prev[0] + prev[1] + 1)
            s, keys, tt = s_view(i), (ORDER[i] + 1) * P, ORDER[i]
            for n0 in range(0, keys, 512):
                n1 = min(keys, n0 + 512)
                o = s[:, n0:n1]
                nc.tensor.matmul(o, QH[:, p, tile(tt)], KH[:, p, n0:n1], start=True, stop=False)
                nc.tensor.matmul(o, QH[:, p, tile(tt)], KL[:, p, n0:n1], start=False, stop=False)
                if n1 == keys:
                    nc.tensor.matmul(o[:, n1 - n0 - P:n1 - n0], IDB[:, :], MASKB[:, :], start=False, stop=False)
                last = nc.tensor.matmul(o, QL[:, p, tile(tt)], KH[:, p, n0:n1], start=False, stop=True)
            last.then_inc(sem("a_s"), 1)

        def a_transpose(pe, h, i):
            pe.wait_ge(sem("a_p"), 8 * h + i + 1)
            tt, w = ORDER[i], p_view(i)
            for b in range(1 + tt // 4):
                n = group(i, b)
                if prev := back(h, n, 2, GROUPS):
                    wait_group(pe, *prev)
                for sb in range(4 * b, min(tt + 1, 4 * b + 4)):
                    last = nc.tensor.transpose(PS[:, PT_BANKS + n % 2, tile(sb % 4)], w[:, tile(sb)], IDF[:, :])
                last.then_inc(sem("a_t"), 1)

        def a_values(pe, h, i):
            if prev := back(h, i, 1, NT):
                pe.wait_ge(sem("a_n"), 8 * prev[0] + prev[1] + 1)
            tt = ORDER[i]
            for sb in range(tt + 1):
                n = group(i, sb // 4)
                if sb % 4 == 0:
                    wait_group(pe, h, n)
                last = nc.tensor.matmul(PS[:, O_BANK, 0:KVR], PT[:, n % 4, tile(sb % 4)], KV[:, sb, :],
                                        start=(sb == 0), stop=(sb == tt))
            last.then_inc(sem("a_o"), 1)

        def a_group_out(eng, h, i, b):
            n = group(i, b)
            width = (min(ORDER[i] + 1, 4 * b + 4) - 4 * b) * P
            eng.wait_ge(sem("a_t"), GROUPS * h + n + 1)
            if prev := back(h, n, 4, GROUPS):
                eng.wait_ge(sem("a_o"), 8 * prev[0] + unit_of(prev[1]) + 1)
            copy = nc.scalar.copy if by_act(n) else nc.vector.tensor_copy
            copy(PT[:, n % 4, 0:width], PS[:, PT_BANKS + n % 2, 0:width]).then_inc(sem("a_pa" if by_act(n) else "a_pd"), 1)

        def behind(h, p, i, k):
            if u := back(h, i, k, NT):
                return u[0], u[1], p if i >= k else 1 - p

        def pe_unit(pe, h, p, i):
            turned, summed = behind(h, p, i, 3), behind(h, p, i, 4)
            a_scores(pe, h, p, i)
            if turned:
                a_transpose(pe, *turned[:2])
            if summed:
                a_values(pe, *summed[:2])

        def ring_rows(p):
            return slice(0, DR) if p == 0 else slice(DR, P)

        def key_rows(h, p):
            return KT[ring_rows(p), :, :].rearrange("p q t -> p (q t)")[:, bass.ds((h - p) * (T // 2), T)]

        def a_hi(act, h, p, what):
            if not (isinstance(h, int) and h < 2):
                act.wait_ge(sem("a_s"), 8 * (h - 1))
            if what == 0:
                nc.scalar.copy(QH[:, p, :], QT[:, bass.ds(h, 1), :].rearrange("p o t -> p (o t)"))\
                    .then_inc(sem("a_hi"), 1)
            else:
                r = ring_rows(p)
                nc.scalar.copy(KH[r, p, :], key_rows(h, p))\
                    .then_inc(sem("a_hi"), 1)

        def a_lo(pool, h, p):
            r = ring_rows(p)
            pool_wait(pool, "a_hi", 2 * h + 1)
            nc.gpsimd.tensor_tensor(QL[:, p, :], QT[:, bass.ds(h, 1), :].rearrange("p o t -> p (o t)"),
                                    f(QH[:, p, :]), ALU.subtract).then_inc(sem("a_lo"), 1)
            pool.wait_ge(sem("a_hi"), 2 * h + 2)
            pool_wait(pool, "a_lo", 2 * h + 1)
            nc.gpsimd.tensor_tensor(KL[r, p, :], key_rows(h, p), f(KH[r, p, :]), ALU.subtract).then_inc(sem("a_lo"), 1)
            pool_wait(pool, "a_lo", 2 * h + 2)

        def a_exp(act, h, i):
            act.wait_ge(sem("a_m"), 8 * h + i + 1)
            if prev := back(h, i, 4, NT):
                act.wait_ge(sem("a_t"), GROUPS * prev[0] + group(prev[1], 1) + 1)
            col = bass.ds(8 * h + ORDER[i], 1)
            nc.scalar.activation(p_view(i), s_view(i), ACT.Exp, bias=NM[:, col], accum_out=LS[:, col])\
                .then_inc(sem("a_p"), 1)

        def act_unit(act, h, p, i, final=False):
            turned = behind(h, p, i, 3)
            a_exp(act, h, i)
            if turned and i % 2:
                a_group_out(act, *turned[:2], 1)
            if not final and i in (1, 3):
                a_hi(act, h + 1, 1 - p, i // 2)

        def a_max(dve, h, i):
            dve.wait_ge(sem("a_s"), 8 * h + i + 1)
            nc.vector.tensor_reduce(NM[:, bass.ds(8 * h + ORDER[i], 1)], s_view(i), axis=AX.X, op=ALU.max, negate=True)\
                .then_inc(sem("a_m"), 1)

        def a_out(dve, h, i, p):
            dve.wait_ge(sem("a_o"), 8 * h + i + 1)
            c = ORDER[i] * P + p * KVR
            nc.vector.tensor_copy(QT[:, bass.ds(h - p, 1), c:c + KVR].rearrange("p o d -> p (o d)"),
                                  PS[:, O_BANK, 0:KVR]).then_inc(sem("a_n"), 1)

        def dve_unit(dve, h, p, i):
            turned, summed = behind(h, p, i, 3), behind(h, p, i, 4)
            a_max(dve, h, i)
            if turned:
                a_group_out(dve, *turned[:2], 0)
            if summed:
                a_out(dve, *summed)

        def a_weights_sum(dve, h):
            dve.wait_ge(sem("a_p"), 8 * h + 8)
            nc.vector.reciprocal(RL[:, bass.ds(8 * h, NT)], LS[:, bass.ds(8 * h, NT)]).then_inc(sem("a_rl"), 1)

        def a_normalise(pool, h, p):
            pool_wait(pool, "a_rl", h + 1)
            pool_wait(pool, "a_n", 8 * h + 8)
            o = QT[:, bass.ds(h - p, 1), :].rearrange("p o (t d) -> p (o t) d", d=P)[:, :, p * KVR:(p + 1) * KVR]
            nc.gpsimd.tensor_tensor(o, o, RL[:, bass.ds(8 * h, NT)].unsqueeze(2).to_broadcast([P, NT, KVR]),
                                    ALU.mult).then_inc(sem("a_on"), 1)

        def o1_banks(tt):
            return (0, 1) if tt % 2 == 0 else (4, 5)

        def o1_transpose(pe, tt):
            if tt >= 2:
                pe.wait_ge(sem("o1_lo"), 2 * (tt - 1))
            for q in range(H1 // 2):
                last = nc.tensor.transpose(PS[:, o1_banks(tt)[q // 4], tile(q % 4)],
                                           QT[:, 2 * q, tile(tt)], IDF[:, :])
                if q % 4 == 3:
                    last.then_inc(sem("o1_tr"), 1)

        def o1_project(pe, tt):
            pe.wait_ge(sem("o1_lo"), 2 * tt + 2)
            if tt >= 2:
                pe.wait_ge(sem("x3"), tt - 1)
            for q in range(H1 // 2):
                last = mm3(PS[:, 2 + tt % 2, 0:D], (OTH[:, tt % 2, q, :], OTL[:, tt % 2, q, :]), (W2H[:, q, :], W2L[:, q, :]),
                           start=(q == 0), stop=(q == H1 // 2 - 1))
            last.then_inc(sem("o1"), 1)

        def o1_half(tt, half):
            return slice(4 * half, 4 * half + 4), PS[:, o1_banks(tt)[half], :].rearrange("p (q t) -> p q t", q=4)

        def o1_hi(act, tt):
            for half in range(2):
                act.wait_ge(sem("o1_tr"), 2 * tt + half + 1)
                if tt >= 2:
                    act.wait_ge(sem("o1"), tt - 1)
                q, bank = o1_half(tt, half)
                nc.scalar.copy(OTH[:, tt % 2, q, :], bank).then_inc(sem("o1_hi"), 1)

        def o1_lo(dve, tt):
            for half in range(2):
                dve.wait_ge(sem("o1_hi"), 2 * tt + half + 1)
                q, bank = o1_half(tt, half)
                nc.vector.tensor_tensor(OTL[:, tt % 2, q, :], bank, f(OTH[:, tt % 2, q, :]), ALU.subtract)\
                    .then_inc(sem("o1_lo"), 1)

        LN3_BANKS = (6, 7)

        def ff_parts(k):
            return 2 if k < NF - 1 else 1

        def ff_split(pool, k):
            if k >= 2:
                pool.wait_ge(sem("ff_gu"), 2 * (k - 1))
            c = slice(0, NC * ff_parts(k))
            nc.gpsimd.tensor_copy(GUH[:, k % 2, c], GU[:, k, c]).then_inc(sem("ff_whi"), 1)
            pool.wait_ge(sem("ff_whi"), k + 1)
            nc.gpsimd.tensor_tensor(GUL[:, k % 2, c], GU[:, k, c], f(GUH[:, k % 2, c]), ALU.subtract)\
                .then_inc(sem("ff_w"), 1)

        def ff_up(pe, k):
            pe.wait_ge(sem("ff_w"), k + 1)
            if k >= 2:
                pe.wait_ge(sem("ff_h"), 2 * (k - 1))
            for n in range(2):
                if k == 0:
                    ln_wait(pe, 3, "lo", 2 * n + 2)
                for j in range(ff_parts(k)):
                    for c in range(NC):
                        last = mm3(PS[:, 4 * (k % 2) + 2 * j + n, :],
                                   (GUH[:, k % 2, NC * j + c, :], GUL[:, k % 2, NC * j + c, :]),
                                   xt(c, slice(512 * n, 512 * n + 512)), start=(c == 0), stop=(c == NC - 1))
                last.then_inc(sem("ff_gu"), 1)

        def ff_gate_up(k, n):
            b = 4 * (k % 2) + n
            if k < NF - 1:
                return PS[:, b, :], PS[:, b + 2, :], P
            return PS[0:LAST, b, :], PS[P - LAST:P, b, :], LAST

        def ff_act(act, k, n):
            act.wait_ge(sem("ff_gu"), 2 * k + n + 1)
            if k >= 2:
                act.wait_ge(sem("ff_h"), 2 * (k - 2) + n + 1)
            gate, _, rows = ff_gate_up(k, n)
            nc.scalar.activation(EX[0:rows, k % 2, 512 * n:512 * n + 512], gate, ACT.Silu, scale=GSUS[0:rows, 0, k:k + 1])\
                .then_inc(sem("ff_ex"), 1)

        def ff_gate(dve, k, n):
            dve.wait_ge(sem("ff_ex"), 2 * k + n + 1)
            _, up_, rows = ff_gate_up(k, n)
            cols = slice(512 * n, 512 * n + 512)
            nc.vector.scalar_tensor_tensor(out=HT[0:rows, k, cols], in0=EX[0:rows, k % 2, cols],
                                           scalar=GSUS[0:rows, 1, k:k + 1], in1=up_, op0=ALU.mult, op1=ALU.mult)\
                .then_inc(sem("ff_h"), 1)

        def ff_hi(act, k, n):
            act.wait_ge(sem("ff_h"), 2 * k + n + 1)
            r, cols = slice(0, ff_gate_up(k, n)[2]), slice(512 * n, 512 * n + 512)
            nc.scalar.copy(HTH[r, k, cols], HT[r, k, cols]).then_inc(sem("ff_hh"), 1)

        def ff_lo(dve, k, n):
            dve.wait_ge(sem("ff_hh"), 2 * k + n + 1)
            r, cols = slice(0, ff_gate_up(k, n)[2]), slice(512 * n, 512 * n + 512)
            nc.vector.tensor_tensor(HTL[r, k, cols], HT[r, k, cols], f(HTH[r, k, cols]), ALU.subtract)\
                .then_inc(sem("ff_hl"), 1)

        FF_STEPS = [(k, n) for k in range(NF) for n in range(2)]

        def router(dve, between):
            count = [0]

            def step(ins):
                count[0] += 1
                ins.then_inc(sem("rt"), 1)
                if count[0] in between:
                    between[count[0]]()
                dve.wait_ge(sem("rt"), count[0])

            def r3(i):
                return RT[:, i, :].rearrange("p (t e) -> p t e", t=NT)
            sc, s, ms = r3(1), r3(2), r3(3)
            V = nc.vector
            dve.wait_ge(sem("rt_tok"), 1)
            step(V.tensor_scalar(RT[:, 1, :], PS[:, 6, 0:P], 1.0, None, ALU.add))
            step(V.reciprocal(sc, sc))
            step(V.tensor_tensor(s, sc, EBIAS.unsqueeze(1).to_broadcast([P, NT, NR]), ALU.add))
            s4 = RT[:, 2, :].rearrange("p (g a b) -> p g a b", a=2, b=2)
            hi = RT[:, 4, 0:64].rearrange("p (g a) -> p g a", a=2)
            lo = RT[:, 4, 64:128].rearrange("p (g a) -> p g a", a=2)
            V.tensor_tensor(hi, s4[:, :, :, 0], s4[:, :, :, 1], ALU.max)
            step(V.tensor_tensor(lo, s4[:, :, :, 0], s4[:, :, :, 1], ALU.min))
            t1, t2, t3, gs = (RT[:, 5, 32 * k:32 * k + 32] for k in range(4))
            V.tensor_tensor(t1, hi[:, :, 0], hi[:, :, 1], ALU.max)
            V.tensor_tensor(t2, hi[:, :, 0], hi[:, :, 1], ALU.min)
            step(V.tensor_tensor(t3, lo[:, :, 0], lo[:, :, 1], ALU.max))
            step(V.tensor_tensor(t2, t2, t3, ALU.max))
            step(V.tensor_tensor(gs, t1, t2, ALU.add))
            g3 = gs.rearrange("p (t g) -> p t g", g=NGRP)
            other = g3.unsqueeze(2).to_broadcast([P, NT, NGRP, NGRP])
            own = g3.unsqueeze(3).to_broadcast([P, NT, NGRP, NGRP])
            gt = RT[:, 6, :].rearrange("p (t g o) -> p t g o", t=NT, g=NGRP)
            eq = RT[:, 7, :].rearrange("p (t g o) -> p t g o", t=NT, g=NGRP)
            V.tensor_tensor(gt, other, own, ALU.is_gt)
            step(V.tensor_tensor(eq, other, own, ALU.is_equal))
            tri = LTRI.unsqueeze(1).to_broadcast([P, NT, NR])
            step(V.tensor_tensor(RT[:, 7, :].rearrange("p (t e) -> p t e", t=NT),
                                 RT[:, 7, :].rearrange("p (t e) -> p t e", t=NT), tri, ALU.mult))
            step(V.tensor_tensor(RT[:, 6, :], RT[:, 6, :], RT[:, 7, :], ALU.add))
            step(V.reduce_sum(t1, RT[:, 6, :].rearrange("p (g o) -> p g o", o=NGRP), axis=AX.X))
            step(V.tensor_scalar(t1, t1, 1.5, None, ALU.is_lt))
            step(V.tensor_tensor(RT[:, 3, :].rearrange("p (g o) -> p g o", o=4),
                                 RT[:, 2, :].rearrange("p (g o) -> p g o", o=4),
                                 t1.unsqueeze(2).to_broadcast([P, 32, 4]), ALU.mult))
            key = KEY.unsqueeze(1).to_broadcast([P, NT, NR])
            m = RT[:, 4, 0:NT]
            sel = [r3(6), r3(7)]
            for n in range(2):
                step(V.reduce_max(m, ms, axis=AX.X))
                step(V.tensor_tensor(sel[n], ms, m.unsqueeze(2).to_broadcast([P, NT, NR]), ALU.is_equal))
                step(V.tensor_tensor(sel[n], sel[n], key, ALU.mult))
                step(V.reduce_max(m, sel[n], axis=AX.X))
                step(V.tensor_tensor(sel[n], sel[n], m.unsqueeze(2).to_broadcast([P, NT, NR]), ALU.is_equal))
                if n == 0:
                    step(V.scalar_tensor_tensor(out=ms, in0=sel[0], scalar=NEG, in1=ms, op0=ALU.mult, op1=ALU.add))
            step(V.tensor_tensor(sel[0], sel[0], sel[1], ALU.add))
            step(V.tensor_tensor(sc, sc, sel[0], ALU.mult))
            step(V.reduce_sum(m, sc, axis=AX.X))
            step(V.tensor_scalar(m, m, 1e-20, None, ALU.add))
            step(V.reciprocal(m, m))
            step(V.tensor_tensor(CMB[:, :, NSH:NE], sc, m.unsqueeze(2).to_broadcast([P, NT, NR]), ALU.mult))

        @block.sync
        def _(sp):
            def load(name, dst, src):
                sp.dma_start(dst, src).then_inc(sem("ld_" + name), 16)
            for j in range(2):
                load("x", X[:, 4 * j:4 * j + 4, :], x.rearrange("(t p) d -> p t d", p=P)[:, 4 * j:4 * j + 4, :])
            load("wq", WQR[:], wqkv.rearrange("(c p) n -> p c n", p=P))
            load("cst", CST[:], consts)
            load("wo0", WO0[:], wo0.rearrange("(c p) n -> p c n", p=P))
            load("wr", WRR[:], wr.rearrange("(c p) n -> p c n", p=P))
            load("gsus", GSUS[:], gsus)
            load("ds", DS[:], ds)
            load("rope", ROPE[:], rope)
            sp.wait_ge(sem("l0_slots"), 4)
            load("up", UP[:], up)
            load("down", DOWN[:], down)
            sp.wait_ge(sem("x1"), NT)
            load("prod", WQN[:], wqn)
            load("prod", WKN[:], wkn)
            load("prod", WV[:], wv)
            load("prod", WO1[:], wo1)
            load("wrn", WRN[:, :, 0:H1 * DR], wqr.rearrange("p k h d -> p k (h d)"))
            load("wrn", WKR[:], wkr.rearrange("p h d -> p (h d)"))
            load("wd", WDR[:], wd.rearrange("(c p) n -> p c n", p=P))
            sp.wait_ge(sem("proj"), 2 * NT)
            load("gu", GU[:], gu.rearrange("p f j c i -> p f (j c) i"))
            load("dnw", DNW[:], dnw)
            for tt in range(NT):
                sp.wait_ge(sem("y"), tt + 1)
                sp.dma_start(out[tile(tt), :], XN[:, tt, :]).then_inc(sem("stored"), 16)
            sp.wait_ge(sem("stored"), 16 * NT)

        @block.gpsimd
        def _(pool):
            nc.gpsimd.memset(HALF[:], -0.5).then_inc(sem("half"), 1)
            nc.gpsimd.memset(IDF[:], 0.0).then_inc(sem("cst0"), 1)
            nc.gpsimd.memset(IDB[:], 0.0).then_inc(sem("cst0"), 1)
            nc.gpsimd.memset(MASKB[:], 0.0).then_inc(sem("cst0"), 1)
            nc.gpsimd.memset(VA[:, :, :, D0:D0 + 1], 1.0).then_inc(sem("ones"), 1)
            nc.gpsimd.memset(f(ONE[:]), 1.0).then_inc(sem("one"), 1)
            nc.gpsimd.memset(CMB[:, :, 0:NSH], 1.0).then_inc(sem("ones"), 1)
            nc.gpsimd.memset(f(VRS[:, :, :, D0 + 1:32]), 0.0).then_inc(sem("ones"), 1)
            pool.wait_ge(sem("cst0"), 3)
            for m in (IDF, IDB):
                nc.gpsimd.affine_select(out=m[:], in_=m[:], pattern=[[-1, P]], compare_op=ALU.not_equal, fill=1.0,
                                        base=0, channel_multiplier=1).then_inc(sem("ident"), 1)
            nc.gpsimd.affine_select(out=MASKB[:], in_=MASKB[:], pattern=[[-1, P]], compare_op=ALU.is_ge, fill=NEG,
                                    base=0, channel_multiplier=1).then_inc(sem("ident"), 1)
            ln_pool(pool, 0, SHIFT)
            pool.wait_ge(sem("wq_hi"), 1)
            nc.gpsimd.tensor_tensor(WQL[:, :, 2 * D:], WQR[:, :, 2 * D:], f(WQH[:, :, 2 * D:]), ALU.subtract)\
                .then_inc(sem("wq_lo"), 1)
            pool.wait_ge(sem("wr_hi"), 1)
            nc.gpsimd.tensor_tensor(WRL[:], WRR[:], f(WRH[:]), ALU.subtract).then_inc(sem("wr_lo"), 1)
            for g in range(NT // 2 + 1):
                if g < NT // 2 - 1:
                    for qk in range(2):
                        pool.wait_ge(sem("l0_p1"), 2 * g + qk + 1)
                        z = Y[:, 2 * g:2 * g + 2, qk]
                        nc.gpsimd.tensor_tensor(z, z, SLT[:, qk, 2 * g:2 * g + 2, :, 0, :], ALU.subtract)\
                            .then_inc(sem("l0_r1"), 1)
                if g:
                    r = slice(2 * g - 2, 2 * g)
                    pool.wait_ge(sem("l0_p2"), 2 * g)
                    nc.gpsimd.tensor_tensor(SLT[:, 1, r, :, 6, :], Y[:, r, 1], SLT[:, 1, r, :, 3, :], ALU.subtract)\
                        .then_inc(sem("l0_p3k"), 1)
            pool.wait_ge(sem("l0_qkv"), NT)
            nc.gpsimd.memset(OT4[:], 0.0).then_inc(sem("ot4"), 1)
            loop_heads4(pool, lambda h, r, **kw: pool_head(pool, h))
            ln_pool(pool, 1)
            pool.wait_ge(sem("ld_up"), 16)
            pool.wait_ge(sem("ld_down"), 16)
            pool.wait_ge(sem("x1"), NT)
            moe_split(pool, 0, 0)
            moe_split(pool, 1, 1)
            with pool.Fori(1, NE // 2) as i:
                moe_split(pool, 2 * i, 0)
                moe_split(pool, 2 * i + 1, 1)
            pool.wait_ge(sem("m_dsplit"), NE)
            ln_pool(pool, 2)
            for q in range(H1 // 2):
                un_split(pool, q)
            for tt in range(NT):
                l1_sums(pool, tt)
            pool.wait_ge(sem("k_lo"), 2)

            def one(h, p, first=False, final=False):
                if not final:
                    a_lo(pool, h + 1, 1 - p)
                if not first:
                    a_normalise(pool, h - 1, 1 - p)
            loop_heads(pool, one)
            pool.wait_ge(sem("a_hi"), 2 * H1)
            pool.wait_ge(sem("a_lo"), 2 * H1)
            nc.gpsimd.tensor_copy(W2H[:], W2[:]).then_inc(sem("w2_hi"), 1)
            pool.wait_ge(sem("w2_hi"), 1)
            nc.gpsimd.tensor_tensor(W2L[:], W2[:], f(W2H[:]), ALU.subtract).then_inc(sem("w2_lo"), 1)
            a_normalise(pool, H1 - 1, 1)
            ln_pool(pool, 3)
            pool.wait_ge(sem("ld_gu"), 16)
            for k in range(NF):
                ff_split(pool, k)

        @block.scalar
        def _(act):
            act.wait_ge(sem("ld_wq"), 16)
            nc.scalar.copy(WQH[:, :, 2 * D:], WQR[:, :, 2 * D:]).then_inc(sem("wq_hi"), 1)
            for tt in range(NT):
                if tt % 2 == 0:
                    act.wait_ge(sem("ln_shift"), tt + 2)
                nc.scalar.activation(XN[:, tt, :], X[:, tt, :], ACT.Identity, bias=SHIFT[:, tt:tt + 1],
                                     scale=RSTD[:, tt:tt + 1]).then_inc(sem("ln_xn"), 1)
            ln_act(act, 0, LN_BANKS, (0, 1))
            act.wait_ge(sem("wc"), 3)
            nc.scalar.copy(WQH[:, :, 0:2 * D], WC[:]).then_inc(sem("wq_hi"), 1)
            act.wait_ge(sem("betac"), 3)
            nc.scalar.copy(BH[:], BETAC[:].unsqueeze(1).to_broadcast([1, H0, 2, D0])).then_inc(sem("beta_hi"), 1)
            ln_act(act, 0, LN_BANKS, (2, 3))
            act.wait_ge(sem("ld_wr"), 16)
            nc.scalar.copy(WRH[:], WRR[:]).then_inc(sem("wr_hi"), 1)
            for j in range(NT // 2 + 2):
                if j < NT // 2:
                    for tt in (2 * j, 2 * j + 1):
                        act.wait_ge(sem("l0_qkv"), tt + 1)
                        if tt >= 2:
                            act.wait_ge(sem("l0_vs"), tt - 1)
                        nc.scalar.activation(SQ[:, tt % 2], qk_bank(tt).rearrange("p (n d) -> p n d", d=D0), ACT.Square)\
                            .then_inc(sem("l0_csq"), 1)
                        nc.scalar.copy(VA[:, tt, :, 0:D0], PS[:, tt % 2, 0:D].rearrange("p (h d) -> p h d", h=H0))\
                            .then_inc(sem("l0_v"), 1)
                if 1 <= j <= NT // 2:
                    r = slice(2 * j - 2, 2 * j)
                    act.wait_ge(sem("l0_z"), 2 * j)
                    for qk in range(2):
                        nc.scalar.copy(SLT[:, qk, r, :, 0, :], Y[:, r, qk]).then_inc(sem("l0_p1"), 1)
                if j < NT // 2:
                    r = slice(2 * j, 2 * j + 2)
                    act.wait_ge(sem("l0_vs"), 2 * j + 2)
                    nc.scalar.activation(SD[:, r, 0, :], VS[:, r, 0, :], ACT.Sqrt, scale=1.0).then_inc(sem("l0_sd"), 1)
                    nc.scalar.activation(SD[:, r, 1, :], VS[:, r, 1, :], ACT.Sqrt, scale=1.0 / D0)\
                        .then_inc(sem("l0_sd"), 1)
                if j >= 2:
                    r = slice(2 * j - 4, 2 * j - 2)
                    for qk, s in ((0, 1), (1, 3)):
                        if j - 2 < NT // 2 - 1:
                            act.wait_ge(sem("l0_r1"), 2 * j - 4 + qk + 1)
                        else:
                            act.wait_ge(sem("l0_r1d"), qk + 1)
                        nc.scalar.copy(SLT[:, qk, r, :, s, :], Y[:, r, qk]).then_inc(sem("l0_p2"), 1)
            loop_heads4(act, lambda h, r, first=False, **kw: act_head(act, h, r % 2, first))
            for j in range(4):
                act.wait_ge(sem("l0_ot"), j + 1)
                bank = PS[:, 6 + j % 2, :].rearrange("p (c t) -> p c t", c=NC)
                nc.scalar.copy(OT0[:, :, 256 * j:256 * j + 256], bank).then_inc(sem("l0_oT"), 1)
            ln_act(act, 1, LN_BANKS)
            act.wait_ge(sem("logits"), 1)
            nc.scalar.activation(RT[0:NR].rearrange("p a b -> p (a b)"), PS[0:NR, 4:6, :].rearrange("p b n -> p (b n)"),
                                 ACT.Exp, scale=-1.0).then_inc(sem("rt_exp"), 1)
            moe_act(act, 0, 0)
            moe_act(act, 1, 1)
            with act.Fori(1, NE // 2) as i:
                moe_act(act, 2 * i, 0)
                moe_act(act, 2 * i + 1, 1)
            act.wait_ge(sem("ld_wd"), 16)
            nc.scalar.copy(WDH[:], WDR[:]).then_inc(sem("wd_hi"), 1)
            l1_products_out(act)
            ln_act(act, 2, LN2_BANKS)
            act.wait_ge(sem("ld_wrn"), 32)
            l1_latents_act(act)
            l1_unrotated_out(act, 0)
            l1_rotary_hi(act)
            for q in range(2, H1 // 2, 2):
                l1_unrotated_out(act, q)
            for tt in range(NT - 1):
                l1_transposed(act, tt)
            act.wait_ge(sem("q_tr"), 2 * NT - 2)
            nc.scalar.copy(KH[KVROWS, 0, :], f(LTH[KVROWS, 1, :])).then_inc(sem("k_hi"), 1)
            act.wait_ge(sem("qk_t"), 4 * (NT - 1))
            act.wait_ge(sem("proj"), 2 * NT)
            nc.scalar.copy(QH[:, 0, SOFAR], QT[:, 0, SOFAR]).then_inc(sem("a_hi0"), 1)
            nc.scalar.copy(KH[0:DR, 0, SOFAR], KT[0:DR, 0, SOFAR]).then_inc(sem("a_hi0"), 1)
            l1_transposed(act, NT - 1)
            act.wait_ge(sem("qk_t"), 4 * NT)
            nc.scalar.copy(QH[:, 0, tile(NT - 1)], QT[:, 0, tile(NT - 1)]).then_inc(sem("a_hi"), 1)
            nc.scalar.copy(KH[0:DR, 0, tile(NT - 1)], KT[0:DR, 0, tile(NT - 1)]).then_inc(sem("a_hi"), 1)
            nc.scalar.copy(KH[0:KVR, 1, :], f(LTH[KVROWS, 1, :])).then_inc(sem("k_hi"), 1)
            act.wait_ge(sem("k_hi"), 2)

            def one(h, p, first=False, final=False):
                for i in range(NT):
                    act_unit(act, h, p, i, final)
            loop_heads(act, one)
            a_group_out(act, H1 - 1, NT - 2, 1)
            for tt in range(NT):
                o1_hi(act, tt)
            ln_act(act, 3, LN3_BANKS)
            act.wait_ge(sem("ld_dnw"), 16)
            nc.scalar.copy(DNWH[:], DNW[:]).then_inc(sem("dnw_hi"), 1)
            act.wait_ge(sem("ld_gsus"), 16)
            for i, step in enumerate(FF_STEPS):
                ff_act(act, *step)
                if i:
                    ff_hi(act, *FF_STEPS[i - 1])
            ff_hi(act, *FF_STEPS[-1])

        @block.vector
        def _(dve):
            def x_loaded(tt):
                if tt % 4 == 0:
                    dve.wait_ge(sem("ld_x"), 32)
            wc = WC[:].rearrange("p c (n d) -> p c n d", d=D0)
            ws = WS[:, 0:NC * 2 * H0].rearrange("p (c n) -> p c n", c=NC)
            for j in range(NT // 2):
                ln_dve_stats(dve, 0, x_loaded, j)
            dve.wait_ge(sem("ld_wq"), 16)
            dve.wait_ge(sem("ld_cst"), 16)
            nc.vector.tensor_tensor(wc, WQR[:, :, 0:2 * D].rearrange("p c (n d) -> p c n d", d=D0),
                                    GAMMA.unsqueeze(1).unsqueeze(1).to_broadcast([P, NC, 2 * H0, D0]), ALU.mult)\
                .then_inc(sem("wc"), 1)
            dve.wait_ge(sem("wc"), 1)
            nc.vector.reduce_sum(ws, wc, axis=AX.X).then_inc(sem("wc"), 1)
            nc.vector.reduce_sum(WS[0:1, NC * 2 * H0:NC * 2 * H0 + 1], BETA[0:1, :], axis=AX.X).then_inc(sem("betac"), 1)
            dve.wait_ge(sem("wc"), 2)
            nc.vector.scalar_tensor_tensor(out=wc, in0=ws.unsqueeze(3).to_broadcast([P, NC, 2 * H0, D0]),
                                           scalar=-1.0 / D0, in1=wc, op0=ALU.mult, op1=ALU.add).then_inc(sem("wc"), 1)
            dve.wait_ge(sem("betac"), 1)
            for q in range(2):
                nc.vector.scalar_tensor_tensor(
                    out=BETAC[:, q, :], in0=WS[0:1, NC * 2 * H0:NC * 2 * H0 + 1].to_broadcast([1, D0]),
                    scalar=-1.0 / D0, in1=BETA[0:1, :], op0=ALU.mult, op1=ALU.add).then_inc(sem("betac"), 1)
            ln_dve_lo(dve, 0, LN_BANKS, 0)
            ln_dve_lo(dve, 0, LN_BANKS, 1)
            dve.wait_ge(sem("wq_hi"), 2)
            nc.vector.tensor_tensor(WQL[:, :, 0:2 * D], WC[:], f(WQH[:, :, 0:2 * D]), ALU.subtract).then_inc(sem("wq_lo"), 1)
            dve.wait_ge(sem("beta_hi"), 1)
            nc.vector.tensor_tensor(BL[:].rearrange("p (h q d) -> p h q d", q=2, d=D0),
                                    BETAC[:].unsqueeze(1).to_broadcast([1, H0, 2, D0]),
                                    f(BH[:]).rearrange("p (h q d) -> p h q d", q=2, d=D0), ALU.subtract)\
                .then_inc(sem("beta_lo"), 1)
            ln_dve_lo(dve, 0, LN_BANKS, 2)
            ln_dve_lo(dve, 0, LN_BANKS, 3)
            for j in range(NT // 2 + 2):
                if j < NT // 2:
                    for tt in (2 * j, 2 * j + 1):
                        dve.wait_ge(sem("l0_csq"), tt + 1)
                        nc.vector.reduce_sum(VS[:, tt], SQ[:, tt % 2], axis=AX.X).then_inc(sem("l0_vr0"), 1)
                        dve.wait_ge(sem("l0_vr0"), tt + 1)
                        nc.vector.tensor_tensor(VS[:, tt], VS[:, tt], CST[:, 80:112].rearrange("p (q h) -> p q h", q=2),
                                                ALU.add).then_inc(sem("l0_vs"), 1)
                    r = slice(2 * j, 2 * j + 2)
                    dve.wait_ge(sem("l0_sd"), 2 * j + 2)
                    nc.vector.reciprocal(SD[:, r], SD[:, r]).then_inc(sem("l0_rs"), 1)
                    dve.wait_ge(sem("l0_rs"), j + 1)
                    for tt in (2 * j, 2 * j + 1):
                        nc.vector.tensor_tensor(Y[:, tt].rearrange("p q h d -> p (q h) d"),
                                                qk_bank(tt).rearrange("p (n d) -> p n d", d=D0),
                                                SD[:, tt].rearrange("p q h -> p (q h)").unsqueeze(2)
                                                .to_broadcast([P, 2 * H0, D0]), ALU.mult).then_inc(sem("l0_z"), 1)
                if j == NT // 2:
                    for qk in range(2):
                        dve.wait_ge(sem("l0_p1"), 2 * j - 2 + qk + 1)
                        z = Y[:, 2 * j - 2:2 * j, qk]
                        nc.vector.tensor_tensor(z, z, SLT[:, qk, 2 * j - 2:2 * j, :, 0, :], ALU.subtract)\
                            .then_inc(sem("l0_r1d"), 1)
                if j >= 2:
                    l0_slots(dve, j - 2)
            dve.wait_ge(sem("l0_v"), NT)
            dve.wait_ge(sem("ones"), 3)
            dve_values(dve, 0, 0)
            dve_stack_out(dve, 0, 0, 0)
            dve_stack_out(dve, 0, 0, 1)
            dve.wait_ge(sem("ot4"), 1)
            loop_heads4(dve, lambda h, r, **kw: dve_head(dve, h, r, **kw))
            dve_lo(dve, H0 - 1, 3, 3)
            for g in (2, 3):
                dve_out(dve, H0 - 1, 3, g)
                dve_out_add(dve, H0 - 1, 3, g)
            for b in range(2):
                dve.wait_ge(sem("l0_tok"), 4 * b + 4)
                o = PS[:, 0:4, :].rearrange("p b (h e) -> p b h e", h=H0)
                z = RT[:, 4 * b:4 * b + 4, 0:H0]
                nc.vector.tensor_scalar(z, o[:, :, :, D0], EPS, None, ALU.add).then_inc(sem("l0_z1"), 1)
                dve.wait_ge(sem("l0_z1"), b + 1)
                nc.vector.reciprocal(z, z).then_inc(sem("l0_z2"), 1)
                dve.wait_ge(sem("l0_z2"), b + 1)
                for i in range(4):
                    nc.vector.tensor_tensor(XN[:, 4 * b + i].rearrange("p (h d) -> p h d", h=H0), o[:, i, :, 0:D0],
                                            z[:, i].unsqueeze(2).to_broadcast([P, H0, D0]), ALU.mult)\
                        .then_inc(sem("l0_on"), 1)

            def x1(tt):
                dve.wait_ge(sem("l0_wo"), tt + 1)
                nc.vector.tensor_tensor(X[:, tt], PS[:, 4 + tt % 2, 0:D], X[:, tt], ALU.add).then_inc(sem("x1"), 1)
                dve.wait_ge(sem("x1"), tt + 1)
            ln_dve(dve, 1, LN_BANKS, x1)
            between = {1: lambda: moe_lo(dve, 0, 0), 5: lambda: moe_lo(dve, 1, 1), 13: lambda: moe_lo(dve, 2, 0),
                       21: lambda: moe_lo(dve, 3, 1)}
            for e in range(NSH - 1):
                for b in range(4):
                    between[8 * e + 8 + b] = lambda e=e, b=b: moe_acc_bank(dve, e, b)
            router(dve, between)
            dve.wait_ge(sem("ones"), 2)

            def experts(i):
                moe_lo(dve, 2 * i, 0)
                moe_acc(dve, 2 * i - 1)
                moe_lo(dve, 2 * i + 1, 1)
                moe_acc(dve, 2 * i)
            experts(NSH // 2)
            with dve.Fori(NSH // 2 + 1, NE // 2) as i:
                experts(i)
            dve.wait_ge(sem("wd_hi"), 1)
            nc.vector.tensor_tensor(WDL[:], WDR[:], f(WDH[:]), ALU.subtract).then_inc(sem("wd_lo"), 1)

            def x2(tt):
                if tt % 2 == 0:
                    moe_acc_bank(dve, NE - 1, tt // 2)
                dve.wait_ge(sem("m_acc"), 8 * NE - NT + tt + 1)
            for j in range(NT // 2):
                ln_dve_stats(dve, 2, x2, j)
            for j in range(NT // 2):
                ln_dve_norm(dve, 2, j)
            for j in range(NT // 2):
                ln_dve_lo(dve, 2, LN2_BANKS, j)
            dve.wait_ge(sem("ld_wrn"), 32)
            l1_latents_dve(dve)
            l1_unrotated_out(dve, 1)
            l1_rotary_lo(dve)
            for q in range(3, H1 // 2, 2):
                l1_unrotated_out(dve, q)
            dve.wait_ge(sem("ld_rope"), 16)
            for tt in range(NT):
                l1_rotate(dve, tt)
            dve.wait_ge(sem("k_rot"), 3 * NT)
            dve.wait_ge(sem("k_tr"), 2 * NT - 4)
            nc.vector.tensor_tensor(KTOK[:, (NT - 1) % 2, :], TK[:, 0, :], TK[:, 1, :], ALU.add).then_inc(sem("k_sum"), 1)
            dve.wait_ge(sem("k_tr"), 2 * NT - 2)
            nc.vector.tensor_copy(KL[KVROWS, 0, :], f(LTL[KVROWS, 1, :])).then_inc(sem("k_lo"), 1)
            for cols, hi, lo in ((SOFAR, "a_hi0", "a_lo0"), (tile(NT - 1), "a_hi", "a_lo")):
                dve.wait_ge(sem(hi), 2)
                nc.vector.tensor_tensor(QL[:, 0, cols], QT[:, 0, cols], f(QH[:, 0, cols]), ALU.subtract)\
                    .then_inc(sem(lo), 1)
                nc.vector.tensor_tensor(KL[0:DR, 0, cols], KT[0:DR, 0, cols], f(KH[0:DR, 0, cols]), ALU.subtract)\
                    .then_inc(sem(lo), 1)
            dve.wait_ge(sem("k_tr"), 2 * NT)
            nc.vector.tensor_copy(KL[0:KVR, 1, :], f(LTL[KVROWS, 1, :])).then_inc(sem("k_lo"), 1)

            def one(h, p, first=False, final=False):
                for i in range(NT):
                    dve_unit(dve, h, p, i)
                    if i == 2 and not first:
                        a_weights_sum(dve, h - 1)
            loop_heads(dve, one)
            for i in range(NT - 3, NT):
                a_group_out(dve, H1 - 1, i, 0)
                a_out(dve, H1 - 1, i - 1, 1)
            a_out(dve, H1 - 1, NT - 1, 1)
            a_weights_sum(dve, H1 - 1)
            o1_lo(dve, 0)

            def x3(tt):
                if tt + 1 < NT:
                    o1_lo(dve, tt + 1)
                dve.wait_ge(sem("o1"), tt + 1)
                nc.vector.tensor_tensor(X[:, tt], PS[:, 2 + tt % 2, 0:D], X[:, tt], ALU.add).then_inc(sem("x3"), 1)
                dve.wait_ge(sem("x3"), tt + 1)
            ln_dve(dve, 3, LN3_BANKS, x3)
            dve.wait_ge(sem("dnw_hi"), 1)
            nc.vector.tensor_tensor(DNWL[:], DNW[:], f(DNWH[:]), ALU.subtract).then_inc(sem("dnw_lo"), 1)
            dve.wait_ge(sem("ld_ds"), 16)
            for i, step in enumerate(FF_STEPS):
                ff_gate(dve, *step)
                if i:
                    ff_lo(dve, *FF_STEPS[i - 1])
            ff_lo(dve, *FF_STEPS[-1])
            for tt in range(NT):
                dve.wait_ge(sem("ff_y"), tt + 1)
                nc.vector.tensor_tensor(XN[:, tt], PS[:, tt, 0:D], DS[:], ALU.mult).then_inc(sem("y_ds"), 1)
                dve.wait_ge(sem("y_ds"), tt + 1)
                nc.vector.tensor_tensor(XN[:, tt], XN[:, tt], X[:, tt], ALU.add).then_inc(sem("y"), 1)

        @block.tensor
        def _(pe):
            pe.wait_ge(sem("ident"), 3)
            for j in range(4):
                ln_pe(pe, 0, LN_BANKS, j)
            pe.wait_ge(sem("wq_lo"), 2)
            pe.wait_ge(sem("beta_lo"), 1)
            pe.wait_ge(sem("one"), 1)
            for tt in range(NT):
                ln_wait(pe, 0, "lo", tt // 2 + 1 if tt < 2 else 4)
                if tt >= 6:
                    pe.wait_ge(sem("l0_z"), tt - 5)
                if tt >= 2:
                    pe.wait_ge(sem("l0_v"), tt - 1)
                for c in range(NC):
                    mm3(qk_bank(tt), xt(c, tile(tt)), (WQH[:, c, 0:2 * D], WQL[:, c, 0:2 * D]), start=(c == 0),
                        stop=False)
                nc.tensor.matmul(qk_bank(tt), ONE[:, :], BH[:, :], start=False, stop=False)
                nc.tensor.matmul(qk_bank(tt), ONE[:, :], BL[:, :], start=False, stop=True)
                ln_wait(pe, 0, "lo", 4)
                for c in range(NC):
                    last = mm3(PS[:, tt % 2, 0:D], xt(c, tile(tt)), (WQH[:, c, 2 * D:], WQL[:, c, 2 * D:]),
                               start=(c == 0), stop=(c == NC - 1))
                last.then_inc(sem("l0_qkv"), 1)
            pe.wait_ge(sem("l0_qslots"), 4)
            pe.wait_ge(sem("ones"), 3)
            pe.wait_ge(sem("l0_v"), NT)
            l0_stack(pe, 0, 0)
            pe.wait_ge(sem("l0_slots"), 4)
            l0_stack(pe, 0, 1)
            loop_heads4(pe, lambda h, r, **kw: pe_head(pe, h, r % 2, **kw))
            l0_av(pe, H0 - 1, 1, 2)
            l0_av(pe, H0 - 1, 1, 3)
            pe.wait_ge(sem("l0_oev"), 4 * H0)
            for tt in range(NT):
                if tt >= 4:
                    pe.wait_ge(sem("l0_on"), tt - 3)
                for q in range(H0 // 4):
                    last = nc.tensor.transpose(PS[:, tt % 4, q * P:(q + 1) * P], OT4[:, q, tile(tt)], IDF[:, :])
                last.then_inc(sem("l0_tok"), 1)
            for j in range(4):
                pe.wait_ge(sem("l0_on"), 2 * j + 2)
                if j >= 2:
                    pe.wait_ge(sem("l0_oT"), j - 1)
                bank = PS[:, 6 + j % 2, :].rearrange("p (c t) -> p c t", c=NC)
                for i in range(2):
                    for c in range(NC):
                        last = nc.tensor.transpose(bank[:, c, i * P:(i + 1) * P],
                                                   XN[:, 2 * j + i, c * P:(c + 1) * P], IDF[:, :])
                last.then_inc(sem("l0_ot"), 1)
            pe.wait_ge(sem("ld_wo0"), 16)
            for tt in range(NT):
                pe.wait_ge(sem("l0_oT"), tt // 2 + 1)
                if tt >= 2:
                    pe.wait_ge(sem("x1"), tt - 1)
                for c in range(NC):
                    last = nc.tensor.matmul(PS[:, 4 + tt % 2, 0:D], OT0[:, c, tile(tt)], WO0[:, c, :],
                                            start=(c == 0), stop=(c == NC - 1))
                last.then_inc(sem("l0_wo"), 1)
                if tt in (5, 7):
                    ln_pe(pe, 1, LN_BANKS, (tt - 5) // 2)
            ln_pe(pe, 1, LN_BANKS, 2)
            ln_pe(pe, 1, LN_BANKS, 3)
            pe.wait_ge(sem("wr_lo"), 1)
            pe.wait_ge(sem("x1"), NT)
            for n in range(2):
                ln_wait(pe, 1, "lo", 2 * n + 2)
                for c in range(NC):
                    last = mm3(PS[0:NR, 4 + n, :], (WRH[:, c, :], WRL[:, c, :]), xt(c, slice(512 * n, 512 * n + 512)),
                               start=(c == 0), stop=(c == NC - 1))
            last.then_inc(sem("logits"), 1)
            moe_up(pe, 0, 0)
            pe.wait_ge(sem("rt_exp"), 1)
            for tt in range(NT):
                last = nc.tensor.transpose(PS[:, 6, tt * NR:(tt + 1) * NR], RT[0:NR, tt, :], IDF[0:NR, 0:NR])
            last.then_inc(sem("rt_tok"), 1)
            moe_up(pe, 1, 1)
            pe.wait_ge(sem("rt"), 1)
            moe_down(pe, 0, 0)

            def experts(i):
                moe_up(pe, 2 * i, 0)
                moe_down(pe, 2 * i - 1, 1)
                moe_up(pe, 2 * i + 1, 1)
                moe_down(pe, 2 * i, 0)
            experts(1)
            experts(NSH // 2)
            with pe.Fori(NSH // 2 + 1, NE // 2) as i:
                experts(i)
            moe_down(pe, NE - 1, 1)
            l1_products(pe)
            l1_latents(pe)
            pe.wait_ge(sem("ltl"), 4)
            l1_unrotated(pe, 0)
            l1_unrotated(pe, 1)
            l1_kv(pe)
            for q in range(2, H1 // 2):
                l1_unrotated(pe, q)
            pe.wait_ge(sem("rw_lo"), 2)
            pe.wait_ge(sem("kv"), 1)
            for tt in range(NT):
                l1_project(pe, tt)
                if tt == 0:
                    pe.wait_ge(sem("un_oa"), H1 // 2)
                    pe.wait_ge(sem("un_od"), H1 // 2)
                else:
                    l1_transpose(pe, tt - 1)
            l1_transpose(pe, NT - 1)
            pe.wait_ge(sem("k_lo"), 1)
            pe.wait_ge(sem("k_hi"), 1)
            pe.wait_ge(sem("qk_t"), 4 * NT)

            def one(h, p, first=False, final=False):
                for i in range(NT):
                    pe_unit(pe, h, p, i)
                if first:
                    pe.wait_ge(sem("k_lo"), 2)
                    pe.wait_ge(sem("k_hi"), 2)
            loop_heads(pe, one)
            for i in range(NT - 3, NT):
                a_transpose(pe, H1 - 1, i)
                a_values(pe, H1 - 1, i - 1)
            a_values(pe, H1 - 1, NT - 1)
            pe.wait_ge(sem("a_on"), H1)
            pe.wait_ge(sem("w2_lo"), 1)
            o1_transpose(pe, 0)
            for tt in range(NT):
                if tt + 1 < NT:
                    o1_transpose(pe, tt + 1)
                o1_project(pe, tt)
                if tt in (5, 7):
                    ln_pe(pe, 3, LN3_BANKS, (tt - 5) // 2)
            ln_pe(pe, 3, LN3_BANKS, 2)
            ln_pe(pe, 3, LN3_BANKS, 3)
            for k in range(NF):
                ff_up(pe, k)
            pe.wait_ge(sem("dnw_lo"), 1)
            pe.wait_ge(sem("ff_h"), 2 * (NF - 1))
            for tt in range(NT):
                for k in range(NF):
                    if tt % 4 == 0:
                        pe.wait_ge(sem("ff_hl"), 2 * k + 1 if tt == 0 else 2 * NF)
                    r = slice(0, LAST if k == NF - 1 else P)
                    last = mm3(PS[:, tt, 0:D], (HTH[r, k, tile(tt)], HTL[r, k, tile(tt)]), (DNWH[r, k, :], DNWL[r, k, :]),
                               start=(k == 0), stop=(k == NF - 1))
                last.then_inc(sem("ff_y"), 1)


def rope_tables():
    inv = 1.0 / (np.float32(10000.0) ** (np.arange(0, DR, 2, dtype=np.float32) / np.float32(DR)))
    fr = np.outer(np.arange(T, dtype=np.float32), inv.astype(np.float32)).astype(np.float32)
    c, s = np.cos(fr), np.sin(fr)
    tab = np.stack([np.concatenate([c, c], 1), np.concatenate([-s, s], 1)]).astype(np.float32)
    return np.ascontiguousarray(tab.reshape(2, NT, P, DR).transpose(2, 0, 1, 3))


def layout(i):
    z = np.zeros
    a = {}
    a["x"] = i["L0_attn_hidden_states"][0]
    cst = z((P, 208), np.float32)
    cst[:, 0:16], cst[:, 16:32] = i["L0_attn_gamma"], i["L0_attn_beta"]
    cst[:, 32:48] = i["L0_ffn_e_bias"]
    cst[:, 48:64] = 16 - np.arange(16)
    cst[:, 80:96], cst[:, 96:112] = EPS * D0, EPS * D0
    cst[:, 64:80] = np.tril(np.ones((4, 4), np.float32), -1).reshape(16)
    a["consts"] = cst
    a["wqkv"] = np.concatenate([i["L0_attn_Wq"].T, i["L0_attn_Wk"].T, i["L0_attn_Wv"].T], 1)
    a["wo0"] = i["L0_attn_Wo"].T
    a["wr"] = i["L0_ffn_router_weight"].T
    up = np.concatenate([i["L0_ffn_shared_up"].reshape(D, NSH, MI).transpose(1, 0, 2), i["L0_ffn_w_up"]], 0)
    a["up"] = up.reshape(NE, NC, P, MI).transpose(2, 0, 1, 3)
    down = np.concatenate([i["L0_ffn_shared_down"].reshape(NSH, MI, D), i["L0_ffn_w_down"]], 0)
    a["down"] = down.transpose(1, 0, 2)
    a["wd"] = np.concatenate([i["L1_attn_wq_down"], i["L1_attn_wkv_down"]], 1)
    order = np.concatenate([np.arange(0, DR, 2), np.arange(1, DR, 2)])
    a["wqn"] = i["L1_attn_wq_nope"].reshape(QR, H1, DN).transpose(2, 1, 0)
    a["wkn"] = i["L1_attn_wk_nope"].reshape(KVR, H1, DN).transpose(2, 1, 0)
    wqr = z((2, P, H1, DR), np.float32)
    q = i["L1_attn_wq_rope"].reshape(QR, H1, DR)[:, :, order]
    wqr[0], wqr[1, :QR - P] = q[:P], q[P:]
    a["wqr"] = wqr.transpose(1, 0, 2, 3)
    wkr = z((P, H1, DR), np.float32)
    wkr[P - KVR:] = i["L1_attn_wk_rope"].reshape(KVR, H1, DR)[:, :, order]
    a["wkr"] = wkr
    wv = z((96, H1, 2, P), np.float32)
    v = i["L1_attn_wv_up"].reshape(KVR, H1, 2, 96).transpose(3, 1, 2, 0)
    wv[:, 0::2, :, 0:64], wv[:, 1::2, :, 64:128] = v[:, 0::2], v[:, 1::2]
    a["wv"] = wv
    a["wo1"] = i["L1_attn_wo"].reshape(H1, 2, 96, D).transpose(2, 0, 1, 3)
    a["rope"] = rope_tables()
    pad = NF * P
    gu = z((2, pad, D), np.float32)
    gu[0, :FI], gu[1, :FI] = i["L1_ffn_gate_w"], i["L1_ffn_up_w"]
    gu = gu.reshape(2, NF, P, NC, P).transpose(4, 1, 0, 3, 2).copy()
    gu[:, -1, 0, :, LAST:] = gu[:, -1, 1, :, :LAST]
    a["gu"] = gu
    gsus = z((2, pad), np.float32)
    gsus[0, :FI], gsus[1, :FI] = i["L1_ffn_gate_s"], i["L1_ffn_up_s"]
    a["gsus"] = gsus.reshape(2, NF, P).transpose(2, 0, 1)
    dn = z((pad, D), np.float32)
    dn[:FI] = i["L1_ffn_down_w"].T
    a["dnw"] = dn.reshape(NF, P, D).transpose(1, 0, 2)
    a["ds"] = np.broadcast_to(i["L1_ffn_down_s"], (P, D))
    return {k: np.ascontiguousarray(v) for k, v in a.items()}


def program(nc, arrays, **kw):
    args = {n: nc.dram_tensor("in_" + n, list(a.shape), mybir.dt.from_np(a.dtype), kind="ExternalInput").ap()
            for n, a in arrays.items()}
    out = nc.dram_tensor("out", [T, D], F32, kind="ExternalOutput").ap()
    build(nc, out=out, **args, **kw)


def kernel(**inputs):
    import concourse.bacc as bacc
    from concourse.bass_utils import run_bass_kernel_spmd

    arrays = layout({k: np.asarray(v) for k, v in inputs.items()})
    nc = bacc.Bacc("TRN2", target_bir_lowering=False, num_devices=1)
    program(nc, arrays)
    r = run_bass_kernel_spmd(nc, [{"in_" + k: v for k, v in arrays.items()}], core_ids=[0])
    return r.results[0]["out"].reshape(1, T, D)
```
